# Optimizing a Trainium2 kernel written in Bass

```python
import numpy as np
import jax
import jax.numpy as jnp

def _softmax(x, axis=-1):
    return jax.nn.softmax(x, axis=axis)

def _gelu(x):
    return jax.nn.gelu(x, approximate=True)

def _silu(x):
    return jax.nn.silu(x)

def _sigmoid(x):
    return jax.nn.sigmoid(x)

def _layernorm(x, axis=-1, eps=1e-05):
    m = jnp.mean(x, axis=axis, keepdims=True)
    v = jnp.var(x, axis=axis, keepdims=True)
    return (x - m) / jnp.sqrt(v + eps)

def _scatter_add(tgt, idx, src, axis=0):
    return tgt.at[idx].add(src)

def _segment_sum(src, seg, n):
    return jax.ops.segment_sum(src, seg, n)
kernel_name = 'mk_perceiver_d4_seqx_r4_d6ad29'

def setup_inputs(seed: int=0):
    np.random.seed(seed)
    _w = jnp.asarray

    def _rec_inputs():
        import jax
        import jax.numpy as jnp
        _rk = jax.random.key(seed)
        x = -0.0005207 + 1.001 * jax.random.normal(jax.random.fold_in(_rk, 1), (1, 128, 512), jnp.float32)
        _lenS = 128 - jax.random.randint(jax.random.fold_in(_rk, 7), (1,), 0, max(1, 128 // 4) + 1, jnp.int32)
        _lenS2 = 12544 - jax.random.randint(jax.random.fold_in(_rk, 8), (1,), 0, max(1, 12544 // 4) + 1, jnp.int32)
        _ctx_2048P = jax.random.normal(jax.random.fold_in(_rk, 12), (1, 16, 512), jnp.float32)
        _ctx_2048c = jax.random.dirichlet(jax.random.fold_in(_rk, 512), 0.3 * jnp.ones((16,), jnp.float32), (1, 12544))
        _ctx_2048t = jnp.einsum('bsk,bkd->bsd', _ctx_2048c, _ctx_2048P)
        _ctx_2048t = _ctx_2048t * jax.lax.rsqrt(jnp.mean(jnp.square(_ctx_2048t)) + 1e-12) * 0.953939
        ctx_2048 = -5.72187e-05 + 0.999849 * (_ctx_2048t + 0.3 * jax.random.normal(jax.random.fold_in(_rk, 612), (1, 12544, 512), jnp.float32))
        _validS = jnp.arange(128)[None, :] < _lenS[:, None]
        _validS2 = jnp.arange(12544)[None, :] < _lenS2[:, None]
        _causal = jnp.tril(jnp.ones((128, 128), dtype=bool))
        mask_BxSx4224_bf0 = jnp.logical_not(jnp.ones((1, 128, 1056), dtype=bool))
        mask_BxS2_bk0 = jnp.logical_not(jnp.broadcast_to(_validS2[:, :], (1, 12544)))
        mask_1xSxS2_ff0 = jnp.where(jnp.ones((1, 128, 12544), dtype=bool), 0.0, -1000000000.0).astype(jnp.float32)
        return (x, ctx_2048, mask_BxSx4224_bf0, mask_BxS2_bk0, mask_1xSxS2_ff0)
    x, ctx_2048, mask_BxSx4224_bf0, mask_BxS2_bk0, mask_1xSxS2_ff0 = _rec_inputs()

    def _L0_xattn_setup():
        import jax, jax.numpy as jnp
        import numpy as np
        import math
        DIM = 512
        B, Q_LEN, KV_LEN = (8, 128, 1024)
        key = jax.random.key(seed)
        ks = jax.random.split(key, 8)
        x = jax.random.normal(ks[0], (B, Q_LEN, DIM), dtype=jnp.float32)
        mask = jnp.zeros((B, Q_LEN, KV_LEN + Q_LEN), dtype=bool)
        k_cache = jax.random.normal(ks[1], (B, KV_LEN, DIM), dtype=jnp.float32)
        v_cache = jax.random.normal(ks[2], (B, KV_LEN, DIM), dtype=jnp.float32)
        scale = 1.0 / math.sqrt(DIM)
        wq = jax.random.normal(ks[3], (DIM, DIM), dtype=jnp.float32) * scale
        wk = jax.random.normal(ks[4], (DIM, DIM), dtype=jnp.float32) * scale
        wv = jax.random.normal(ks[5], (DIM, DIM), dtype=jnp.float32) * scale
        wo = jax.random.normal(ks[6], (DIM, DIM), dtype=jnp.float32) * scale
        return {'x': x, 'mask': mask, 'k_cache': k_cache, 'v_cache': v_cache, 'wq': wq, 'wk': wk, 'wv': wv, 'wo': wo}
    _L0_xattn_all = _L0_xattn_setup()
    _L0_xattn_in = {k: v for k, v in _L0_xattn_all.items() if k in ('wq', 'wk', 'wv', 'wo')}
    del _L0_xattn_all

    def _L0_attn_setup():
        import jax, jax.numpy as jnp
        import numpy as np
        TOPK = 64
        NEG = -1e+30

        def hadamard(x):
            d = x.shape[-1]
            shape = x.shape
            x = x.reshape(-1, d)
            h = 1
            while h < d:
                x = x.reshape(-1, d // (2 * h), 2, h)
                a, b = (x[:, :, 0, :], x[:, :, 1, :])
                x = jnp.stack([a + b, a - b], axis=2).reshape(-1, d)
                h *= 2
            return (x * d ** (-0.5)).reshape(shape)
        key = jax.random.key(seed)
        ks = jax.random.split(key, 8)
        D, S, B = (512, 512, 1)
        Hi, Di, H, hd = (16, 128, 16, 128)
        w = 0.02
        return {'x': jax.random.normal(ks[0], (B, S, D), jnp.float32), 'wq_idx': jax.random.normal(ks[1], (D, Hi * Di), jnp.float32) * w, 'wk_idx': jax.random.normal(ks[2], (D, Di), jnp.float32) * w, 'w_iw': jax.random.normal(ks[3], (D, Hi), jnp.float32) * w, 'wq': jax.random.normal(ks[4], (D, H * hd), jnp.float32) * w, 'wk': jax.random.normal(ks[5], (D, hd), jnp.float32) * w, 'wv': jax.random.normal(ks[6], (D, hd), jnp.float32) * w, 'wo': jax.random.normal(ks[7], (H * hd, D), jnp.float32) * w}
    _L0_attn_all = _L0_attn_setup()
    _L0_attn_in = {k: v for k, v in _L0_attn_all.items() if k in ('wq_idx', 'wk_idx', 'w_iw', 'wq', 'wk', 'wv', 'wo')}
    del _L0_attn_all

    def _L0_ffn_setup():
        import jax, jax.numpy as jnp
        import numpy as np
        N_BLOCKS = 16
        BLOCK_SIZE = 128
        TOP_K = N_BLOCKS // 4
        key = jax.random.key(seed)
        k1, k2, k3, k4, k5 = jax.random.split(key, 5)
        in_f, out_f = (512, 2048)
        x = jax.random.normal(k1, (2, 1024, in_f), dtype=jnp.float32)
        Wr = jax.random.normal(k2, (N_BLOCKS, in_f), dtype=jnp.float32) * in_f ** (-0.5)
        br = jnp.zeros((N_BLOCKS,), dtype=jnp.float32)
        W1 = jax.random.normal(k3, (out_f, in_f), dtype=jnp.float32) * in_f ** (-0.5)
        W2 = jax.random.normal(k4, (in_f, out_f), dtype=jnp.float32) * out_f ** (-0.5)
        return {'x': x, 'Wr': Wr, 'br': br, 'W1': W1, 'W2': W2}
    _L0_ffn_all = _L0_ffn_setup()
    _L0_ffn_in = {k: v for k, v in _L0_ffn_all.items() if k in ('Wr', 'br', 'W1', 'W2')}
    del _L0_ffn_all

    def _L1_xattn_setup():
        import jax, jax.numpy as jnp
        import numpy as np
        key = jax.random.key(seed)
        k1, k2, k3 = jax.random.split(key, 3)
        B, S, D, M = (8, 512, 512, 128)
        hidden_states = jax.random.normal(k1, (B, S, D), dtype=jnp.float32)
        memory_tokens = jax.random.normal(k2, (B, M, D), dtype=jnp.float32)
        memory_mask = jax.random.randint(k3, (B, M), 0, 2).astype(jnp.bool_)
        return {'hidden_states': hidden_states, 'memory_tokens': memory_tokens, 'memory_mask': memory_mask}
    _L1_xattn_all = _L1_xattn_setup()
    _L1_xattn_in = {k: v for k, v in _L1_xattn_all.items() if k in ()}
    del _L1_xattn_all

    def _L1_attn_setup():
        import jax, jax.numpy as jnp
        import numpy as np
        B, S, D = (4, 1024, 512)
        IDENTITY_WEIGHT = 0.5
        ROT_DIM = D // 2

        def _layernorm(x, gamma, beta, eps=1e-05):
            mu = jnp.mean(x, axis=-1, keepdims=True)
            var = jnp.var(x, axis=-1, keepdims=True)
            return (x - mu) * jax.lax.rsqrt(var + eps) * gamma + beta

        def _rotary(t, rot_dim, theta=10000.0):
            seq = t.shape[-2]
            inv_freq = 1.0 / theta ** (jnp.arange(0, rot_dim, 2, dtype=jnp.float32) / rot_dim)
            freqs = jnp.arange(seq, dtype=jnp.float32)[:, None] * inv_freq[None, :]
            freqs = jnp.repeat(freqs, 2, axis=-1)
            cos, sin = (jnp.cos(freqs), jnp.sin(freqs))
            t_rot, t_pass = (t[..., :rot_dim], t[..., rot_dim:])
            x1, x2 = (t_rot[..., 0::2], t_rot[..., 1::2])
            rot_half = jnp.stack([-x2, x1], axis=-1).reshape(t_rot.shape)
            return jnp.concatenate([t_rot * cos + rot_half * sin, t_pass], axis=-1)

        def _cos_sim(x):
            return x / jnp.linalg.norm(x, axis=-1, keepdims=True)
        key = jax.random.key(seed)
        ks = jax.random.split(key, 3)
        scale = 0.02
        return {'X': jax.random.normal(ks[0], (B, S, D), jnp.float32), 'W_in': jax.random.normal(ks[1], (D, 3 * D), jnp.float32) * scale, 'b_in': jnp.zeros((3 * D,), jnp.float32), 'W_out': jax.random.normal(ks[2], (D, D), jnp.float32) * scale, 'b_out': jnp.zeros((D,), jnp.float32), 'gamma': jnp.ones((D,), jnp.float32), 'beta': jnp.zeros((D,), jnp.float32)}
    _L1_attn_all = _L1_attn_setup()
    _L1_attn_in = {k: v for k, v in _L1_attn_all.items() if k in ('W_in', 'b_in', 'W_out', 'b_out', 'gamma', 'beta')}
    del _L1_attn_all

    def _L1_ffn_setup():
        import jax, jax.numpy as jnp
        import numpy as np
        R = 64
        RP = 2
        K = 8
        SCALING = 16.0 / K
        key = jax.random.key(seed)
        ks = jax.random.split(key, 5)
        B, S, Din, Dout = (8, 1024, 512, 512)
        x = jax.random.normal(ks[0], (B, S, Din), dtype=jnp.float32)
        base_W = jax.random.normal(ks[1], (Dout, Din), dtype=jnp.float32) * Din ** (-0.5)
        router_W = jax.random.normal(ks[2], (R // RP, Din), dtype=jnp.float32) * Din ** (-0.5)
        A = jax.random.normal(ks[3], (R, Din), dtype=jnp.float32) * Din ** (-0.5)
        Bw = jax.random.normal(ks[4], (Dout, R), dtype=jnp.float32) * R ** (-0.5)
        biases = jnp.zeros((R,), dtype=jnp.float32)
        return {'x': x, 'base_W': base_W, 'router_W': router_W, 'A': A, 'B': Bw, 'biases': biases}
    _L1_ffn_all = _L1_ffn_setup()
    _L1_ffn_in = {k: v for k, v in _L1_ffn_all.items() if k in ('base_W', 'router_W', 'A', 'B', 'biases')}
    del _L1_ffn_all

    def _L2_xattn_setup():
        import jax, jax.numpy as jnp
        import numpy as np
        H = 512
        NH = 16
        NKV = 4
        HD = 128
        GROUPS = NH // NKV
        EPS = 1e-06
        B, S, SE = (1, 512, 1024)

        def _rmsnorm(x, w, eps=EPS):
            xf = x.astype(jnp.float32)
            var = jnp.mean(xf * xf, axis=-1, keepdims=True)
            return (xf * jax.lax.rsqrt(var + eps)).astype(x.dtype) * w
        key = jax.random.key(seed)
        ks = jax.random.split(key, 12)
        sc = 0.02
        return {'hidden_states': jax.random.normal(ks[0], (B, S, H), jnp.float32), 'encoder_hidden_states': jax.random.normal(ks[1], (B, SE, H), jnp.float32), 'attention_mask': jnp.zeros((B, S, SE), jnp.float32), 'Wq': jax.random.normal(ks[2], (H, NH * HD), jnp.float32) * sc, 'bq': jax.random.normal(ks[3], (NH * HD,), jnp.float32) * sc, 'Wk': jax.random.normal(ks[4], (H, NKV * HD), jnp.float32) * sc, 'bk': jax.random.normal(ks[5], (NKV * HD,), jnp.float32) * sc, 'Wv': jax.random.normal(ks[6], (H, NKV * HD), jnp.float32) * sc, 'bv': jax.random.normal(ks[7], (NKV * HD,), jnp.float32) * sc, 'Wo': jax.random.normal(ks[8], (NH * HD, H), jnp.float32) * sc, 'qn_w': jnp.ones((HD,), jnp.float32), 'kn_w': jnp.ones((HD,), jnp.float32)}
    _L2_xattn_all = _L2_xattn_setup()
    _L2_xattn_in = {k: v for k, v in _L2_xattn_all.items() if k in ('Wq', 'bq', 'Wk', 'bk', 'Wv', 'bv', 'Wo', 'qn_w', 'kn_w')}
    del _L2_xattn_all

    def _L2_attn_setup():
        import jax, jax.numpy as jnp
        import numpy as np
        import math
        D_MODEL = 512
        N_HEADS = 16
        HEAD_DIM = D_MODEL // N_HEADS
        B, T = (2, 512)
        key = jax.random.key(seed)
        ks = jax.random.split(key, 9)
        s = 1.0 / math.sqrt(D_MODEL)
        inp = {'x': jax.random.normal(ks[0], (B, T, D_MODEL), dtype=jnp.float32)}
        for i, name in enumerate(['q', 'k', 'v', 'o']):
            inp[f'w{name}'] = jax.random.uniform(ks[1 + 2 * i], (D_MODEL, D_MODEL), jnp.float32, -s, s)
            inp[f'b{name}'] = jax.random.uniform(ks[2 + 2 * i], (D_MODEL,), jnp.float32, -s, s)
        return inp
    _L2_attn_all = _L2_attn_setup()
    _L2_attn_in = {k: v for k, v in _L2_attn_all.items() if k in ('wq', 'bq', 'wk', 'bk', 'wv', 'bv', 'wo', 'bo')}
    del _L2_attn_all

    def _L2_ffn_setup():
        import jax, jax.numpy as jnp
        import numpy as np
        B, S, D, H = (4, 512, 512, 2048)

        def fwht(x):
            orig_shape = x.shape
            n = orig_shape[-1]
            x = x.reshape(-1, n)
            h = 1
            while h < n:
                xb = x.reshape(-1, n // (2 * h), 2, h)
                a = xb[:, :, 0, :]
                b = xb[:, :, 1, :]
                x = jnp.stack([a + b, a - b], axis=2).reshape(-1, n)
                h *= 2
            scale = jnp.asarray(1.0 / np.sqrt(n), dtype=x.dtype)
            return (x * scale).reshape(orig_shape)
        key = jax.random.key(seed)
        kx, k1, k2, k3 = jax.random.split(key, 4)
        x = jax.random.normal(kx, (B, S, D), dtype=jnp.float32)
        W1 = jax.random.normal(k1, (H, D), dtype=jnp.float32) * (1.0 / np.sqrt(D))
        W2 = jax.random.normal(k2, (D, H), dtype=jnp.float32) * (1.0 / np.sqrt(H))
        W3 = jax.random.normal(k3, (H, D), dtype=jnp.float32) * (1.0 / np.sqrt(D))
        return {'x': x, 'W1': W1, 'W2': W2, 'W3': W3}
    _L2_ffn_all = _L2_ffn_setup()
    _L2_ffn_in = {k: v for k, v in _L2_ffn_all.items() if k in ('W1', 'W2', 'W3')}
    del _L2_ffn_all

    def _L3_xattn_setup():
        import jax, jax.numpy as jnp
        import numpy as np
        DIM = 512
        NHEADS = 32
        HEAD_DIM = DIM // NHEADS
        EPS = 1e-06

        def _rmsnorm(t):
            return t * jax.lax.rsqrt(jnp.mean(t * t, axis=-1, keepdims=True) + EPS)
        key = jax.random.key(seed)
        kx, kc, kq, kk, kv = jax.random.split(key, 5)
        x = jax.random.normal(kx, (2, 1024, DIM), dtype=jnp.float32)
        context = jax.random.normal(kc, (2, 128, DIM), dtype=jnp.float32)
        std = 0.02
        Wq = jax.random.normal(kq, (DIM, DIM), dtype=jnp.float32) * std
        Wk = jax.random.normal(kk, (DIM, DIM), dtype=jnp.float32) * std
        Wv = jax.random.normal(kv, (DIM, DIM), dtype=jnp.float32) * std
        return {'x': x, 'context': context, 'Wq': Wq, 'Wk': Wk, 'Wv': Wv}
    _L3_xattn_all = _L3_xattn_setup()
    _L3_xattn_in = {k: v for k, v in _L3_xattn_all.items() if k in ('Wq', 'Wk', 'Wv')}
    del _L3_xattn_all

    def _L3_attn_setup():
        import jax, jax.numpy as jnp
        import numpy as np
        B, S, D = (2, 1024, 512)
        H, DK, DV = (16, 128, 128)
        SEG = 128
        UPDATE = 'delta'
        CAUSAL = True
        key = jax.random.key(seed)
        ks = jax.random.split(key, 6)
        s = 0.02
        return {'x': jax.random.normal(ks[0], (B, S, D), jnp.float32), 'Wq': jax.random.normal(ks[1], (D, H * DK), jnp.float32) * s, 'Wk': jax.random.normal(ks[2], (D, H * DK), jnp.float32) * s, 'Wv': jax.random.normal(ks[3], (D, H * DV), jnp.float32) * s, 'Wo': jax.random.normal(ks[4], (H * DV, D), jnp.float32) * s, 'betas': jax.random.normal(ks[5], (1, H, 1, DV), jnp.float32)}
    _L3_attn_all = _L3_attn_setup()
    _L3_attn_in = {k: v for k, v in _L3_attn_all.items() if k in ('Wq', 'Wk', 'Wv', 'Wo', 'betas')}
    del _L3_attn_all

    def _L3_ffn_setup():
        import jax, jax.numpy as jnp
        import numpy as np
        CAPACITY = 0.125
        HEAD_DIM = 128
        N_HEADS = 16
        N_KV_HEADS = 8
        ROPE_THETA = 10000.0
        EPS = 1e-06

        def _rms_norm(x, w):
            return x * jax.lax.rsqrt(jnp.mean(x * x, axis=-1, keepdims=True) + EPS) * w

        def _rotate_half(t):
            h = t.shape[-1] // 2
            return jnp.concatenate([-t[..., h:], t[..., :h]], axis=-1)
        key = jax.random.key(seed)
        ks = jax.random.split(key, 12)
        B, T, D = (4, 1024, 512)
        I = 2048
        s = 0.02
        return {'hidden_states': jax.random.normal(ks[0], (B, T, D), jnp.float32), 'w_router': jax.random.normal(ks[1], (D,), jnp.float32) * s, 'wq': jax.random.normal(ks[2], (D, N_HEADS * HEAD_DIM), jnp.float32) * s, 'bq': jnp.zeros((N_HEADS * HEAD_DIM,), jnp.float32), 'wk': jax.random.normal(ks[3], (D, N_KV_HEADS * HEAD_DIM), jnp.float32) * s, 'bk': jnp.zeros((N_KV_HEADS * HEAD_DIM,), jnp.float32), 'wv': jax.random.normal(ks[4], (D, N_KV_HEADS * HEAD_DIM), jnp.float32) * s, 'bv': jnp.zeros((N_KV_HEADS * HEAD_DIM,), jnp.float32), 'wo': jax.random.normal(ks[5], (N_HEADS * HEAD_DIM, D), jnp.float32) * s, 'w_gate': jax.random.normal(ks[6], (D, I), jnp.float32) * s, 'w_up': jax.random.normal(ks[7], (D, I), jnp.float32) * s, 'w_down': jax.random.normal(ks[8], (I, D), jnp.float32) * s, 'ln1_w': jnp.ones((D,), jnp.float32), 'ln2_w': jnp.ones((D,), jnp.float32)}
    _L3_ffn_all = _L3_ffn_setup()
    _L3_ffn_in = {k: v for k, v in _L3_ffn_all.items() if k in ('w_router', 'wq', 'bq', 'wk', 'bk', 'wv', 'bv', 'wo', 'w_gate', 'w_up', 'w_down', 'ln1_w', 'ln2_w')}
    del _L3_ffn_all
    return {'x': x, 'ctx_2048': ctx_2048, 'mask_BxSx4224_bf0': mask_BxSx4224_bf0, 'mask_BxS2_bk0': mask_BxS2_bk0, 'mask_1xSxS2_ff0': mask_1xSxS2_ff0, 'L0_xattn_wq': _L0_xattn_in['wq'], 'L0_xattn_wk': _L0_xattn_in['wk'], 'L0_xattn_wv': _L0_xattn_in['wv'], 'L0_xattn_wo': _L0_xattn_in['wo'], 'L0_attn_wq_idx': _L0_attn_in['wq_idx'], 'L0_attn_wk_idx': _L0_attn_in['wk_idx'], 'L0_attn_w_iw': _L0_attn_in['w_iw'], 'L0_attn_wq': _L0_attn_in['wq'], 'L0_attn_wk': _L0_attn_in['wk'], 'L0_attn_wv': _L0_attn_in['wv'], 'L0_attn_wo': _L0_attn_in['wo'], 'L0_ffn_Wr': _L0_ffn_in['Wr'], 'L0_ffn_br': _L0_ffn_in['br'], 'L0_ffn_W1': _L0_ffn_in['W1'], 'L0_ffn_W2': _L0_ffn_in['W2'], 'L1_attn_W_in': _L1_attn_in['W_in'], 'L1_attn_b_in': _L1_attn_in['b_in'], 'L1_attn_W_out': _L1_attn_in['W_out'], 'L1_attn_b_out': _L1_attn_in['b_out'], 'L1_attn_gamma': _L1_attn_in['gamma'], 'L1_attn_beta': _L1_attn_in['beta'], 'L1_ffn_base_W': _L1_ffn_in['base_W'], 'L1_ffn_router_W': _L1_ffn_in['router_W'], 'L1_ffn_A': _L1_ffn_in['A'], 'L1_ffn_B': _L1_ffn_in['B'], 'L1_ffn_biases': _L1_ffn_in['biases'], 'L2_xattn_Wq': _L2_xattn_in['Wq'], 'L2_xattn_bq': _L2_xattn_in['bq'], 'L2_xattn_Wk': _L2_xattn_in['Wk'], 'L2_xattn_bk': _L2_xattn_in['bk'], 'L2_xattn_Wv': _L2_xattn_in['Wv'], 'L2_xattn_bv': _L2_xattn_in['bv'], 'L2_xattn_Wo': _L2_xattn_in['Wo'], 'L2_xattn_qn_w': _L2_xattn_in['qn_w'], 'L2_xattn_kn_w': _L2_xattn_in['kn_w'], 'L2_attn_wq': _L2_attn_in['wq'], 'L2_attn_bq': _L2_attn_in['bq'], 'L2_attn_wk': _L2_attn_in['wk'], 'L2_attn_bk': _L2_attn_in['bk'], 'L2_attn_wv': _L2_attn_in['wv'], 'L2_attn_bv': _L2_attn_in['bv'], 'L2_attn_wo': _L2_attn_in['wo'], 'L2_attn_bo': _L2_attn_in['bo'], 'L2_ffn_W1': _L2_ffn_in['W1'], 'L2_ffn_W2': _L2_ffn_in['W2'], 'L2_ffn_W3': _L2_ffn_in['W3'], 'L3_xattn_Wq': _L3_xattn_in['Wq'], 'L3_xattn_Wk': _L3_xattn_in['Wk'], 'L3_xattn_Wv': _L3_xattn_in['Wv'], 'L3_attn_Wq': _L3_attn_in['Wq'], 'L3_attn_Wk': _L3_attn_in['Wk'], 'L3_attn_Wv': _L3_attn_in['Wv'], 'L3_attn_Wo': _L3_attn_in['Wo'], 'L3_attn_betas': _L3_attn_in['betas'], 'L3_ffn_w_router': _L3_ffn_in['w_router'], 'L3_ffn_wq': _L3_ffn_in['wq'], 'L3_ffn_bq': _L3_ffn_in['bq'], 'L3_ffn_wk': _L3_ffn_in['wk'], 'L3_ffn_bk': _L3_ffn_in['bk'], 'L3_ffn_wv': _L3_ffn_in['wv'], 'L3_ffn_bv': _L3_ffn_in['bv'], 'L3_ffn_wo': _L3_ffn_in['wo'], 'L3_ffn_w_gate': _L3_ffn_in['w_gate'], 'L3_ffn_w_up': _L3_ffn_in['w_up'], 'L3_ffn_w_down': _L3_ffn_in['w_down'], 'L3_ffn_ln1_w': _L3_ffn_in['ln1_w'], 'L3_ffn_ln2_w': _L3_ffn_in['ln2_w']}

def reference(x, ctx_2048, mask_BxSx4224_bf0, mask_BxS2_bk0, mask_1xSxS2_ff0, L0_xattn_wq, L0_xattn_wk, L0_xattn_wv, L0_xattn_wo, L0_attn_wq_idx, L0_attn_wk_idx, L0_attn_w_iw, L0_attn_wq, L0_attn_wk, L0_attn_wv, L0_attn_wo, L0_ffn_Wr, L0_ffn_br, L0_ffn_W1, L0_ffn_W2, L1_attn_W_in, L1_attn_b_in, L1_attn_W_out, L1_attn_b_out, L1_attn_gamma, L1_attn_beta, L1_ffn_base_W, L1_ffn_router_W, L1_ffn_A, L1_ffn_B, L1_ffn_biases, L2_xattn_Wq, L2_xattn_bq, L2_xattn_Wk, L2_xattn_bk, L2_xattn_Wv, L2_xattn_bv, L2_xattn_Wo, L2_xattn_qn_w, L2_xattn_kn_w, L2_attn_wq, L2_attn_bq, L2_attn_wk, L2_attn_bk, L2_attn_wv, L2_attn_bv, L2_attn_wo, L2_attn_bo, L2_ffn_W1, L2_ffn_W2, L2_ffn_W3, L3_xattn_Wq, L3_xattn_Wk, L3_xattn_Wv, L3_attn_Wq, L3_attn_Wk, L3_attn_Wv, L3_attn_Wo, L3_attn_betas, L3_ffn_w_router, L3_ffn_wq, L3_ffn_bq, L3_ffn_wk, L3_ffn_bk, L3_ffn_wv, L3_ffn_bv, L3_ffn_wo, L3_ffn_w_gate, L3_ffn_w_up, L3_ffn_w_down, L3_ffn_ln1_w, L3_ffn_ln2_w):
    import jax
    import jax.numpy as jnp

    def _L0_xattn_ref(x, mask, k_cache, v_cache, wq, wk, wv, wo):
        import jax, jax.numpy as jnp
        import numpy as np
        import math
        DIM = 512
        B, Q_LEN, KV_LEN = (8, 128, 1024)
        q = jnp.einsum('bsd,ed->bse', x, wq)
        k_new = jnp.einsum('bsd,ed->bse', x, wk)
        v_new = jnp.einsum('bsd,ed->bse', x, wv)
        k = jnp.concatenate([k_cache, k_new], axis=1)
        v = jnp.concatenate([v_cache, v_new], axis=1)
        scale = 1.0 / math.sqrt(q.shape[-1])
        scores = jnp.einsum('bqd,bkd->bqk', q, k) * scale
        attn = jax.nn.softmax(scores, axis=-1)
        out = jnp.einsum('bqk,bkd->bqd', attn, v)
        return jnp.einsum('bqd,ed->bqe', out, wo)

    def _L0_attn_ref(x, wq_idx, wk_idx, w_iw, wq, wk, wv, wo):
        import jax, jax.numpy as jnp
        import numpy as np
        TOPK = 64
        NEG = -1e+30

        def hadamard(x):
            d = x.shape[-1]
            shape = x.shape
            x = x.reshape(-1, d)
            h = 1
            while h < d:
                x = x.reshape(-1, d // (2 * h), 2, h)
                a, b = (x[:, :, 0, :], x[:, :, 1, :])
                x = jnp.stack([a + b, a - b], axis=2).reshape(-1, d)
                h *= 2
            return (x * d ** (-0.5)).reshape(shape)
        B, S, D = x.shape
        Di = wk_idx.shape[-1]
        Hi = w_iw.shape[-1]
        hd = wk.shape[-1]
        H = wq.shape[-1] // hd
        qi = hadamard((x @ wq_idx).reshape(B, S, Hi, Di))
        ki = hadamard(x @ wk_idx)
        iw = x @ w_iw
        logits = jax.nn.relu(jnp.einsum('bthd,bsd->bhts', qi, ki))
        I = jnp.einsum('bth,bhts->bts', iw, logits)
        t = jnp.arange(S)
        causal = t[None, :, None] >= t[None, None, :]
        I = jnp.where(causal, I, NEG)
        vals, idx = jax.lax.top_k(I, TOPK)
        valid = vals > NEG / 2
        q = (x @ wq).reshape(B, S, H, hd)
        k = x @ wk
        v = x @ wv
        gather = jax.vmap(lambda kk, ii: kk[ii])
        k_sel, v_sel = (gather(k, idx), gather(v, idx))
        scores = jnp.einsum('bthd,btkd->bhtk', q, k_sel) * hd ** (-0.5)
        scores = jnp.where(valid[:, None], scores, NEG)
        p = jax.nn.softmax(scores, axis=-1)
        o = jnp.einsum('bhtk,btkd->bthd', p, v_sel)
        return o.reshape(B, S, H * hd) @ wo

    def _L0_ffn_ref(x, Wr, br, W1, W2):
        import jax, jax.numpy as jnp
        import numpy as np
        N_BLOCKS = 16
        BLOCK_SIZE = 128
        TOP_K = N_BLOCKS // 4
        x_shape = x.shape
        in_f = x_shape[-1]
        xf = x.reshape(-1, in_f)
        n = xf.shape[0]
        prob = jax.nn.softmax(xf @ Wr.T + br, axis=-1)
        _, idx = jax.lax.top_k(prob, TOP_K)
        mask = jnp.zeros((n, N_BLOCKS), dtype=xf.dtype)
        mask = mask.at[jnp.arange(n)[:, None], idx].set(1.0)
        W1b = W1.reshape(N_BLOCKS, BLOCK_SIZE, in_f)
        h = jnp.einsum('nf,ibf->nib', xf, W1b)
        h = jax.nn.gelu(h, approximate=False) * mask[:, :, None]
        W2b = W2.reshape(in_f, N_BLOCKS, BLOCK_SIZE)
        y = jnp.einsum('nib,fib->nf', h, W2b)
        return y.reshape(x_shape)

    def _L1_xattn_ref(hidden_states, memory_tokens, memory_mask):
        import jax, jax.numpy as jnp
        import numpy as np
        B, S, D = hidden_states.shape
        scale = 1.0 / jnp.sqrt(jnp.asarray(D, hidden_states.dtype))
        scores = jnp.einsum('bsd,bmd->bsm', hidden_states, memory_tokens) * scale
        neg_inf = jnp.asarray(-1e+30, scores.dtype)
        scores = jnp.where(memory_mask[:, None, :], scores, neg_inf)
        attn = jax.nn.softmax(scores, axis=-1)
        readout = jnp.einsum('bsm,bmd->bsd', attn, memory_tokens)
        valid_b = jnp.any(memory_mask, axis=-1)
        out = jnp.where(valid_b[:, None, None], readout, jnp.zeros_like(readout))
        return out

    def _L1_attn_ref(X, W_in, b_in, W_out, b_out, gamma, beta):
        import jax, jax.numpy as jnp
        import numpy as np
        B, S, D = (4, 1024, 512)
        IDENTITY_WEIGHT = 0.5
        ROT_DIM = D // 2

        def _layernorm(x, gamma, beta, eps=1e-05):
            mu = jnp.mean(x, axis=-1, keepdims=True)
            var = jnp.var(x, axis=-1, keepdims=True)
            return (x - mu) * jax.lax.rsqrt(var + eps) * gamma + beta

        def _rotary(t, rot_dim, theta=10000.0):
            seq = t.shape[-2]
            inv_freq = 1.0 / theta ** (jnp.arange(0, rot_dim, 2, dtype=jnp.float32) / rot_dim)
            freqs = jnp.arange(seq, dtype=jnp.float32)[:, None] * inv_freq[None, :]
            freqs = jnp.repeat(freqs, 2, axis=-1)
            cos, sin = (jnp.cos(freqs), jnp.sin(freqs))
            t_rot, t_pass = (t[..., :rot_dim], t[..., rot_dim:])
            x1, x2 = (t_rot[..., 0::2], t_rot[..., 1::2])
            rot_half = jnp.stack([-x2, x1], axis=-1).reshape(t_rot.shape)
            return jnp.concatenate([t_rot * cos + rot_half * sin, t_pass], axis=-1)

        def _cos_sim(x):
            return x / jnp.linalg.norm(x, axis=-1, keepdims=True)
        Xn = _layernorm(X, gamma, beta)
        QKV = Xn @ W_in + b_in
        Q, K, V = jnp.split(QKV, 3, axis=-1)
        K = _rotary(K, ROT_DIM)
        V = _rotary(V, ROT_DIM)
        A = jnp.sum(_cos_sim(K) * _cos_sim(V), axis=-2)
        A = (1.0 - IDENTITY_WEIGHT) * A + IDENTITY_WEIGHT
        Y = A[:, None, :] * Q
        Y = Y @ W_out + b_out
        return Y + X

    def _L1_ffn_ref(x, base_W, router_W, A, B, biases):
        import jax, jax.numpy as jnp
        import numpy as np
        R = 64
        RP = 2
        K = 8
        SCALING = 16.0 / K
        Bsz, S, Din = x.shape
        N = Bsz * S
        xf = x.reshape(N, Din)
        logits = jax.nn.sigmoid(xf @ router_W.T)
        logits = jnp.repeat(logits, RP, axis=-1) + biases
        top_v, top_i = jax.lax.top_k(logits, K)
        rows = jnp.arange(N)[:, None]
        sparse = jnp.zeros((N, R), dtype=x.dtype).at[rows, top_i].set(top_v)
        gating = sparse / jnp.sum(sparse, axis=-1, keepdims=True) * K
        mid = xf @ A.T
        lora_out = mid * gating @ B.T
        base = xf @ base_W.T
        out = base + SCALING * lora_out
        return out.reshape(Bsz, S, -1)

    def _L2_xattn_ref(hidden_states, encoder_hidden_states, attention_mask, Wq, bq, Wk, bk, Wv, bv, Wo, qn_w, kn_w):
        import jax, jax.numpy as jnp
        import numpy as np
        H = 512
        NH = 16
        NKV = 4
        HD = 128
        GROUPS = NH // NKV
        EPS = 1e-06
        B, S, SE = (1, 512, 1024)

        def _rmsnorm(x, w, eps=EPS):
            xf = x.astype(jnp.float32)
            var = jnp.mean(xf * xf, axis=-1, keepdims=True)
            return (xf * jax.lax.rsqrt(var + eps)).astype(x.dtype) * w
        b, s, _ = hidden_states.shape
        se = encoder_hidden_states.shape[1]
        q = (hidden_states @ Wq + bq).reshape(b, s, NH, HD).transpose(0, 2, 1, 3)
        k = (encoder_hidden_states @ Wk + bk).reshape(b, se, NKV, HD).transpose(0, 2, 1, 3)
        v = (encoder_hidden_states @ Wv + bv).reshape(b, se, NKV, HD).transpose(0, 2, 1, 3)
        k = jnp.repeat(k, GROUPS, axis=1)
        v = jnp.repeat(v, GROUPS, axis=1)
        q = _rmsnorm(q, qn_w)
        k = _rmsnorm(k, kn_w)
        scale = 1.0 / np.sqrt(HD).astype(np.float32)
        scores = jnp.einsum('bhsd,bhed->bhse', q, k) * scale
        scores = scores + attention_mask[:, None, :, :]
        probs = jax.nn.softmax(scores.astype(jnp.float32), axis=-1).astype(q.dtype)
        out = jnp.einsum('bhse,bhed->bhsd', probs, v)
        out = out.transpose(0, 2, 1, 3).reshape(b, s, NH * HD)
        return out @ Wo

    def _L2_attn_ref(x, wq, bq, wk, bk, wv, bv, wo, bo):
        import jax, jax.numpy as jnp
        import numpy as np
        import math
        D_MODEL = 512
        N_HEADS = 16
        HEAD_DIM = D_MODEL // N_HEADS
        B, T = (2, 512)
        Bsz, S, _ = x.shape

        def proj(w, b):
            y = jnp.einsum('btd,ed->bte', x, w) + b
            return y.reshape(Bsz, S, N_HEADS, HEAD_DIM).transpose(0, 2, 1, 3)
        q = proj(wq, bq)
        k = proj(wk, bk)
        v = proj(wv, bv)
        scores = jnp.einsum('bhqd,bhkd->bhqk', q, k) / math.sqrt(HEAD_DIM)
        causal = jnp.tril(jnp.ones((S, S), dtype=bool))
        scores = jnp.where(causal[None, None], scores, -jnp.inf)
        attn = jax.nn.softmax(scores, axis=-1)
        out = jnp.einsum('bhqk,bhkd->bhqd', attn, v)
        out = out.transpose(0, 2, 1, 3).reshape(Bsz, S, D_MODEL)
        return jnp.einsum('btd,ed->bte', out, wo) + bo

    def _L2_ffn_ref(x, W1, W2, W3):
        import jax, jax.numpy as jnp
        import numpy as np
        B, S, D, H = (4, 512, 512, 2048)

        def fwht(x):
            orig_shape = x.shape
            n = orig_shape[-1]
            x = x.reshape(-1, n)
            h = 1
            while h < n:
                xb = x.reshape(-1, n // (2 * h), 2, h)
                a = xb[:, :, 0, :]
                b = xb[:, :, 1, :]
                x = jnp.stack([a + b, a - b], axis=2).reshape(-1, n)
                h *= 2
            scale = jnp.asarray(1.0 / np.sqrt(n), dtype=x.dtype)
            return (x * scale).reshape(orig_shape)
        up_gate = jnp.einsum('bsd,hd->bsh', x, W1)
        up_lin = jnp.einsum('bsd,hd->bsh', x, W3)
        hidden = jax.nn.silu(up_gate) * up_lin
        hidden = fwht(hidden)
        out = jnp.einsum('bsh,dh->bsd', hidden, W2)
        return out

    def _L3_xattn_ref(x, context, Wq, Wk, Wv):
        import jax, jax.numpy as jnp
        import numpy as np
        DIM = 512
        NHEADS = 32
        HEAD_DIM = DIM // NHEADS
        EPS = 1e-06

        def _rmsnorm(t):
            return t * jax.lax.rsqrt(jnp.mean(t * t, axis=-1, keepdims=True) + EPS)
        b, n, _ = x.shape
        m = context.shape[1]
        q = x @ Wq.T
        k_raw = context @ Wk.T
        v_raw = context @ Wv.T
        q = q.reshape(b, n, NHEADS, HEAD_DIM).transpose(0, 2, 1, 3)
        kv = jnp.concatenate([k_raw, v_raw], axis=-1)
        kv = kv.reshape(b, m, NHEADS, HEAD_DIM, 2)
        k = kv[..., 0].transpose(0, 2, 1, 3)
        v = kv[..., 1].transpose(0, 2, 1, 3)
        q = _rmsnorm(q)
        k = _rmsnorm(k)
        scale = HEAD_DIM ** (-0.5)
        scores = jnp.einsum('bhnd,bhmd->bhnm', q, k) * scale
        attn = jax.nn.softmax(scores, axis=-1)
        out = jnp.einsum('bhnm,bhmd->bhnd', attn, v)
        return out.transpose(0, 2, 1, 3).reshape(b, n, NHEADS * HEAD_DIM)

    def _L3_attn_ref(x, Wq, Wk, Wv, Wo, betas):
        import jax, jax.numpy as jnp
        import numpy as np
        B, S, D = (2, 1024, 512)
        H, DK, DV = (16, 128, 128)
        SEG = 128
        UPDATE = 'delta'
        CAUSAL = True
        Bsz, seq, _ = x.shape
        nseg = seq // SEG
        q = (x @ Wq).reshape(Bsz, seq, H, DK).transpose(0, 2, 1, 3)
        k = (x @ Wk).reshape(Bsz, seq, H, DK).transpose(0, 2, 1, 3)
        v = (x @ Wv).reshape(Bsz, seq, H, DV).transpose(0, 2, 1, 3)
        qs = q.reshape(Bsz, H, nseg, SEG, DK).transpose(2, 0, 1, 3, 4)
        ks_ = k.reshape(Bsz, H, nseg, SEG, DK).transpose(2, 0, 1, 3, 4)
        vs = v.reshape(Bsz, H, nseg, SEG, DV).transpose(2, 0, 1, 3, 4)
        causal_mask = jnp.tril(jnp.ones((SEG, SEG), bool))
        scale = DK ** 0.5
        beta = jax.nn.sigmoid(betas)

        def step(carry, seg):
            mem, z = carry
            qq, kk, vv = seg
            sigma_q = jax.nn.elu(qq) + 1.0
            scores = jnp.einsum('bhsk,bhtk->bhst', qq, kk) / scale
            if CAUSAL:
                scores = jnp.where(causal_mask, scores, -jnp.inf)
            att_dot = jax.nn.softmax(scores, axis=-1) @ vv
            att_mem = sigma_q @ mem / (sigma_q @ z)
            sigma_k = jax.nn.elu(kk) + 1.0
            if UPDATE == 'linear':
                mem_new = mem + jnp.einsum('bhsk,bhsv->bhkv', sigma_k, vv)
            else:
                delta = vv - sigma_k @ mem / (sigma_k @ z)
                mem_new = mem + jnp.einsum('bhsk,bhsv->bhkv', sigma_k, delta)
            z_new = z + sigma_k.sum(axis=-2, keepdims=True).transpose(0, 1, 3, 2)
            att = beta * att_mem + (1.0 - beta) * att_dot
            out = att.reshape(Bsz, SEG, H * DV) @ Wo
            return ((mem_new, z_new), out)
        mem0 = jnp.zeros((Bsz, H, DK, DV), x.dtype)
        z0 = jnp.ones((Bsz, H, DK, 1), x.dtype) / DK
        _, outs = jax.lax.scan(step, (mem0, z0), (qs, ks_, vs))
        return outs.transpose(1, 0, 2, 3).reshape(Bsz, seq, D)

    def _L3_ffn_ref(hidden_states, w_router, wq, bq, wk, bk, wv, bv, wo, w_gate, w_up, w_down, ln1_w, ln2_w):
        import jax, jax.numpy as jnp
        import numpy as np
        CAPACITY = 0.125
        HEAD_DIM = 128
        N_HEADS = 16
        N_KV_HEADS = 8
        ROPE_THETA = 10000.0
        EPS = 1e-06

        def _rms_norm(x, w):
            return x * jax.lax.rsqrt(jnp.mean(x * x, axis=-1, keepdims=True) + EPS) * w

        def _rotate_half(t):
            h = t.shape[-1] // 2
            return jnp.concatenate([-t[..., h:], t[..., :h]], axis=-1)
        B, T, D = hidden_states.shape
        k = max(1, int(T * CAPACITY))
        scores = jnp.einsum('btd,d->bt', hidden_states, w_router)
        _, idx = jax.lax.top_k(scores, k)
        idx = jnp.sort(idx, axis=-1)
        b = jnp.arange(B)[:, None]
        sel = hidden_states[b, idx]
        sel_scores = scores[b, idx]
        S = B * k
        x = sel.reshape(S, D)
        pos = idx.reshape(S)
        inv_freq = 1.0 / ROPE_THETA ** (jnp.arange(0, HEAD_DIM, 2, dtype=jnp.float32) / HEAD_DIM)
        ang = pos.astype(jnp.float32)[:, None] * inv_freq
        cos = jnp.concatenate([jnp.cos(ang), jnp.cos(ang)], axis=-1)[:, None, :]
        sin = jnp.concatenate([jnp.sin(ang), jnp.sin(ang)], axis=-1)[:, None, :]
        h = _rms_norm(x, ln1_w)
        q = (h @ wq + bq).reshape(S, N_HEADS, HEAD_DIM)
        kk = (h @ wk + bk).reshape(S, N_KV_HEADS, HEAD_DIM)
        v = (h @ wv + bv).reshape(S, N_KV_HEADS, HEAD_DIM)
        q = q * cos + _rotate_half(q) * sin
        kk = kk * cos + _rotate_half(kk) * sin
        rep = N_HEADS // N_KV_HEADS
        kk = jnp.repeat(kk, rep, axis=1)
        v = jnp.repeat(v, rep, axis=1)
        att = jnp.einsum('shd,thd->hst', q, kk) / np.sqrt(HEAD_DIM)
        causal = jnp.tril(jnp.ones((S, S), bool))
        att = jnp.where(causal[None], att, jnp.finfo(att.dtype).min)
        att = jax.nn.softmax(att, axis=-1)
        attn_out = jnp.einsum('hst,thd->shd', att, v).reshape(S, N_HEADS * HEAD_DIM) @ wo
        x1 = x + attn_out
        h2 = _rms_norm(x1, ln2_w)
        mlp = jax.nn.silu(h2 @ w_gate) * (h2 @ w_up) @ w_down
        processed = x1 + mlp
        gate = jax.nn.sigmoid(sel_scores).reshape(S, 1)
        gated = gate * processed + (1.0 - gate) * x
        output = hidden_states.at[b, idx].set(gated.reshape(B, k, D))
        return output
    x = x + _L0_xattn_ref(_layernorm(x, axis=-1), mask_BxSx4224_bf0, ctx_2048, ctx_2048, L0_xattn_wq, L0_xattn_wk, L0_xattn_wv, L0_xattn_wo)
    x = x + _L0_attn_ref(_layernorm(x, axis=-1), L0_attn_wq_idx, L0_attn_wk_idx, L0_attn_w_iw, L0_attn_wq, L0_attn_wk, L0_attn_wv, L0_attn_wo)
    x = x + _L0_ffn_ref(_layernorm(x, axis=-1), L0_ffn_Wr, L0_ffn_br, L0_ffn_W1, L0_ffn_W2)
    x = x + _L1_xattn_ref(_layernorm(x, axis=-1), ctx_2048, mask_BxS2_bk0)
    x = x + _L1_attn_ref(_layernorm(x, axis=-1), L1_attn_W_in, L1_attn_b_in, L1_attn_W_out, L1_attn_b_out, L1_attn_gamma, L1_attn_beta)
    x = x + _L1_ffn_ref(_layernorm(x, axis=-1), L1_ffn_base_W, L1_ffn_router_W, L1_ffn_A, L1_ffn_B, L1_ffn_biases)
    x = x + _L2_xattn_ref(_layernorm(x, axis=-1), ctx_2048, mask_1xSxS2_ff0, L2_xattn_Wq, L2_xattn_bq, L2_xattn_Wk, L2_xattn_bk, L2_xattn_Wv, L2_xattn_bv, L2_xattn_Wo, L2_xattn_qn_w, L2_xattn_kn_w)
    x = x + _L2_attn_ref(_layernorm(x, axis=-1), L2_attn_wq, L2_attn_bq, L2_attn_wk, L2_attn_bk, L2_attn_wv, L2_attn_bv, L2_attn_wo, L2_attn_bo)
    x = x + _L2_ffn_ref(_layernorm(x, axis=-1), L2_ffn_W1, L2_ffn_W2, L2_ffn_W3)
    x = x + _L3_xattn_ref(_layernorm(x, axis=-1), ctx_2048, L3_xattn_Wq, L3_xattn_Wk, L3_xattn_Wv)
    x = x + _L3_attn_ref(_layernorm(x, axis=-1), L3_attn_Wq, L3_attn_Wk, L3_attn_Wv, L3_attn_Wo, L3_attn_betas)
    x = x + _L3_ffn_ref(_layernorm(x, axis=-1), L3_ffn_w_router, L3_ffn_wq, L3_ffn_bq, L3_ffn_wk, L3_ffn_bk, L3_ffn_wv, L3_ffn_bv, L3_ffn_wo, L3_ffn_w_gate, L3_ffn_w_up, L3_ffn_w_down, L3_ffn_ln1_w, L3_ffn_ln2_w)
    return x

_drawn_inputs = setup_inputs


def setup_inputs(seed=0):
    import zlib

    import numpy as np

    out = dict(_drawn_inputs(seed))
    spreads = {'L0_ffn_br': (0.0, 0.1),
     'L1_attn_b_in': (0.0, 0.274),
     'L1_attn_b_out': (0.0, 0.1),
     'L1_attn_gamma': (1.0, 0.2),
     'L1_attn_beta': (0.0, 0.8),
     'L1_ffn_biases': (0.0, 0.1),
     'L2_xattn_qn_w': (1.0, 0.6),
     'L2_xattn_kn_w': (1.0, 0.6),
     'L3_ffn_bq': (0.0, 0.8),
     'L3_ffn_bk': (0.0, 0.8),
     'L3_ffn_bv': (0.0, 0.8),
     'L3_ffn_ln1_w': (1.0, 0.6),
     'L3_ffn_ln2_w': (1.0, 0.6)}
    factors = {'L0_xattn_wk': 3.811,
     'L0_xattn_wv': 3.715,
     'L2_xattn_bq': 8.0,
     'L2_xattn_bk': 23.595,
     'L2_xattn_bv': 8.0,
     'L2_attn_wq': 8.0,
     'L2_attn_bq': 8.0,
     'L2_attn_wk': 8.0,
     'L2_attn_bk': 64.0,
     'L2_attn_bv': 8.0,
     'L2_attn_bo': 6.19,
     'L3_attn_Wq': 8.0,
     'L3_attn_Wk': 8.0,
     'L3_attn_betas': 3.321,
     'L3_ffn_w_router': 2.797,
     'L3_ffn_wq': 8.0,
     'L3_ffn_wk': 8.0,
     'L3_ffn_wv': 2.753,
     'L3_ffn_wo': 2.817,
     'L3_ffn_w_gate': 8.0,
     'L3_ffn_w_up': 7.732,
     'L3_ffn_w_down': 7.995}
    for name, (base, spread) in spreads.items():
        noise = np.random.default_rng([zlib.crc32(name.encode()), seed]).standard_normal(out[name].shape)
        drawn = base * np.exp(spread * noise) if base else spread * noise
        out[name] = jnp.asarray(drawn.astype(out[name].dtype))
    for name, factor in factors.items():
        out[name] = (out[name] * factor).astype(out[name].dtype)
    return out
```

```python
from contextlib import ExitStack, contextmanager

import concourse.bass as bass
import numpy as np
from concourse import mybir

F32 = mybir.dt.float32
F32R = mybir.dt.float32r
U8 = mybir.dt.uint8
ALU = mybir.AluOpType
ACT = mybir.ActivationFunctionType
X = mybir.AxisListType.X

P = 128
D = 512
DC = D // P
KV = 12544
CHUNK = P
PER = 7
GROUP = PER * CHUNK
GROUPS = KV // GROUP
TILE = GROUP // 2
HEADS = 16
NEG = -1e30
RING = 6
TAKEN = -3e38

UNITS = (
    [("L0_xattn_wq", 1), ("L0_xattn_wk", 1), ("L0_xattn_wv", 1), ("L0_xattn_wo", 1)]
    + [("L0_attn_wq_idx", 4), ("L0_attn_wq", 4), ("L0_attn_wo", 4)]
    + [("L0_ffn_W1", 4), ("L0_ffn_W2", 4)]
    + [("L1_attn_W_in", 3), ("L1_attn_W_out", 1)]
    + [("L1_ffn_base_W", 1)]
    + [("L2_xattn_Wq", 4), ("L2_xattn_Wk", 1), ("L2_xattn_Wv", 1), ("L2_xattn_Wo", 4)]
    + [("L2_attn_wq", 1), ("L2_attn_wk", 1), ("L2_attn_wv", 1), ("L2_attn_wo", 1)]
    + [("L2_ffn_W1", 4), ("L2_ffn_W3", 4), ("L2_ffn_W2", 4)]
    + [("L3_xattn_Wq", 1), ("L3_xattn_Wkeys", 1), ("L3_xattn_Wvalues", 1)]
    + [("L3_attn_Wq", 4), ("L3_attn_Wk", 4), ("L3_attn_Wv", 4), ("L3_attn_Wo", 4)]
    + [("L3_ffn_wq", 4), ("L3_ffn_wk", 2), ("L3_ffn_wv", 2), ("L3_ffn_wo", 4)]
    + [("L3_ffn_w_gate", 4), ("L3_ffn_w_up", 4), ("L3_ffn_w_down", 4)]
)


class Chain:

    def __init__(self, engine, sem):
        self.engine, self.sem, self.count = engine, sem, 0

    def __call__(self, instruction):
        self.count += 1
        instruction.then_inc(self.sem, 1)
        self.engine.wait_ge(self.sem, self.count)


def wait_count(engine, sem, count):
    if not (isinstance(count, int) and count == 0):
        engine.wait_ge(sem, count)


def short(ap):
    return ap.bitcast(F32R)


def matmul_parts(nc, out, stationary, moving, start, stop):
    (sh, sl), (mh, ml) = stationary, moving
    nc.tensor.matmul(out, short(sh), short(mh), start=start, stop=False)
    nc.tensor.matmul(out, short(sh), short(ml), start=False, stop=False)
    return nc.tensor.matmul(out, short(sl), short(mh), start=False, stop=stop)


class Unit:

    def __init__(self, ring, number):
        self.ring, self.number, self.slot = ring, number, number % RING
        self.data = ring.slots[:, self.slot]

    def wait_landed(self, pe):
        pe.wait_ge(self.ring.landed[self.slot], 16 * (self.number // RING + 1))

    def done(self, last_matmul):
        last_matmul.then_inc(self.ring.done, 1)

    def wait_done(self, engine):
        engine.wait_ge(self.ring.done, self.number + 1)

    def refill(self, sp):
        if self.number + RING < self.ring.total:
            self.wait_done(sp)
            self.ring.load(sp, self.number + RING)


class WeightRing:

    def __init__(self, core, dram, start=0):
        self.names = [name for name, n in UNITS for _ in range(n)][start:]
        self.total = len(self.names)
        self.dram = [dram[start + u].rearrange("p (c n) -> p c n", c=DC) for u in range(self.total)]
        self.slots = core.sbuf("weight_ring", [P, RING, DC, D], F32)
        self.landed = [core.nc.alloc_semaphore(f"weights_landed_{i}") for i in range(RING)]
        self.done = core.nc.alloc_semaphore("weight_units_done")
        self.next = 0

    def load(self, sp, n):
        sp.dma_start(self.slots[:, n % RING], self.dram[n]).then_inc(self.landed[n % RING], 16)

    def take(self, name):
        count = dict(UNITS)[name]
        assert self.names[self.next] == name and self.names[self.next + count - 1] == name
        units = [Unit(self, self.next + i) for i in range(count)]
        self.next += count
        return units


class Core:
    def __init__(self, nc, ctx, dram):
        self.nc, self.ctx, self.dram = nc, ctx, dram
        self.sems, self.serial = {}, 0

    def sbuf(self, name, shape, dt=F32):
        return self.ctx.enter_context(self.nc.sbuf_tensor(name, shape, dt))

    def sem(self, name):
        if name not in self.sems:
            self.sems[name] = self.nc.alloc_semaphore(name)
        return self.sems[name]

    @contextmanager
    def stage(self):
        with self.nc.Block() as block:
            yield block
        if self.sems:
            numbers = sorted(s.num for s in self.sems.values())
            assert numbers[-1] - numbers[0] + 1 == len(numbers)
            self.nc.gpsimd.sem_clear(range(numbers[0], numbers[-1] + 1))
            self.nc.all_engine_barrier()

    @contextmanager
    def scratch(self, **shapes):
        with ExitStack() as stack:
            self.serial += 1
            yield [stack.enter_context(self.nc.sbuf_tensor(f"{k}_{self.serial}", v, F32)) for k, v in shapes.items()]




def norm_stage(core, src, dst, dstT, eps, rms=False, gain=None, shift=None, loads=(), scale=1.0):
    nc, ps, c = core.nc, core.psum, core
    with core.scratch(stats=[P, 6], moments=[P, 2], spread=[P, 1], rstd=[P, 1], square=[P, D]) as (
        stats, moments, spread, rstd, square,
    ), core.stage() as block:

        @block.sync
        def _(sp):
            for to, frm in loads:
                sp.dma_start(to, frm).then_inc(c.sem("operands_landed"), 16)
            if loads:
                sp.wait_ge(c.sem("operands_landed"), 16 * len(loads))

        @block.vector
        def _(dve):
            link = Chain(dve, c.sem("dve_chain"))
            if rms:
                link(nc.vector.tensor_tensor(square[:, :], src, src, ALU.mult))
                link(nc.vector.tensor_reduce(moments[:, 1:2], square[:, :], X, ALU.add))
                nc.vector.tensor_scalar(spread[:, :], moments[:, 1:2], 1.0 / D, eps, ALU.mult, ALU.add).then_inc(
                    c.sem("variance_ready"), 1)
            else:
                link(nc.vector.bn_stats(stats[:, :], src))
                link(nc.vector.bn_aggr(moments[:, :], stats[:, :]))
                nc.vector.tensor_scalar(spread[:, :], moments[:, 1:2], eps, None, ALU.add).then_inc(
                    c.sem("variance_ready"), 1)
            dve.wait_ge(c.sem("rstd_ready"), 1)
            if rms:
                steps = [lambda: nc.vector.tensor_scalar(dst, src, rstd[:, 0:1], None, ALU.mult)]
            else:
                steps = [lambda: nc.vector.tensor_scalar(dst, src, moments[:, 0:1], rstd[:, 0:1],
                                                         ALU.subtract, ALU.mult)]
            if loads:
                dve.wait_ge(c.sem("operands_landed"), 16 * len(loads))
            if gain is not None:
                steps.append(lambda: nc.vector.tensor_tensor(dst, dst, gain, ALU.mult))
            if shift is not None:
                steps.append(lambda: nc.vector.tensor_tensor(dst, dst, shift, ALU.add))
            for step in steps[:-1]:
                link(step())
            steps[-1]().then_inc(c.sem("normed"), 1)

        @block.gpsimd
        def _(pool):
            pool.wait_ge(c.sem("variance_ready"), 1)
            nc.gpsimd.tensor_tensor(rstd[:, :], spread[:, :], core.minus_half[:, 0:1], ALU.pow).then_inc(
                c.sem("rstd_ready"), 1)

        @block.tensor
        def _(pe):
            pe.wait_ge(c.sem("normed"), 1)
            for i in range(DC):
                last = nc.tensor.transpose(ps[0][:, i * P:(i + 1) * P], dst[:, i * P:(i + 1) * P], core.ident)
            last.then_inc(c.sem("transposed"), 1)

        @block.scalar
        def _(act):
            act.wait_ge(c.sem("transposed"), 1)
            nc.scalar.activation(dstT.rearrange("p c t -> p (c t)"), ps[0][:, :], ACT.Copy, scale=scale)


def transpose_stage(core, rows, cols, n, scale=1.0):
    nc, ps, c = core.nc, core.psum, core
    banks = (n + 3) // 4
    with core.stage() as block:

        @block.tensor
        def _(pe):
            for b in range(banks):
                if b >= 4:
                    pe.wait_ge(c.sem("copied"), b - 3)
                for i in range(4 * b, min(4 * b + 4, n)):
                    last = nc.tensor.transpose(ps[b % 4][:, (i % 4) * P:(i % 4 + 1) * P],
                                               rows[:, i * P:(i + 1) * P], core.ident)
                last.then_inc(c.sem("transposed"), 1)

        @block.scalar
        def _(act):
            for b in range(banks):
                k = min(4, n - 4 * b)
                act.wait_ge(c.sem("transposed"), b + 1)
                nc.scalar.activation(cols[:, 4 * b:4 * b + k, :].rearrange("p c t -> p (c t)"),
                                     ps[b % 4][:, 0:k * P], ACT.Copy, scale=scale).then_inc(c.sem("copied"), 1)


def rows_stage(core, aT, units, evacuate, on_scalar=False, after=None):
    nc, ps, c = core.nc, core.psum, core
    with core.stage() as block:

        @block.sync
        def _(sp):
            for u in units:
                u.refill(sp)

        @block.tensor
        def _(pe):
            for j, u in enumerate(units):
                u.wait_landed(pe)
                if j >= 4:
                    pe.wait_ge(c.sem("bank_evacuated"), j - 3)
                for i in range(DC):
                    last = nc.tensor.matmul(ps[j % 4][:, :], aT[:, i, :], u.data[:, i, :],
                                            start=(i == 0), stop=(i == DC - 1))
                u.done(last)

        def evacuate_all(engine, link):
            for j, u in enumerate(units):
                u.wait_done(engine)
                evacuate(j, ps[j % 4][:, :], link).then_inc(c.sem("bank_evacuated"), 1)

        if on_scalar:

            @block.scalar
            def _(act):
                evacuate_all(act, None)

        @block.vector
        def _(dve):
            link = Chain(dve, c.sem("dve_chain"))
            if not on_scalar:
                evacuate_all(dve, link)
            if after is not None:
                dve.wait_ge(c.sem("bank_evacuated"), len(units))
                after(link)


def cols_stage(core, aT, units, outT, scale=1.0):
    nc, ps, c = core.nc, core.psum, core
    with core.stage() as block:

        @block.sync
        def _(sp):
            for u in units:
                u.refill(sp)

        @block.tensor
        def _(pe):
            for j, u in enumerate(units):
                u.wait_landed(pe)
                if j >= 4:
                    pe.wait_ge(c.sem("bank_evacuated"), j - 3)
                for o in range(DC):
                    for i in range(DC):
                        last = nc.tensor.matmul(ps[j % 4][:, o * P:(o + 1) * P], u.data[:, i, o * P:(o + 1) * P],
                                                aT[:, i, :], start=(i == 0), stop=(i == DC - 1))
                u.done(last)

        @block.scalar
        def _(act):
            for j, u in enumerate(units):
                u.wait_done(act)
                nc.scalar.activation(outT[:, 4 * j:4 * j + 4, :].rearrange("p c t -> p (c t)"), ps[j % 4][:, :],
                                     ACT.Copy, scale=scale).then_inc(c.sem("bank_evacuated"), 1)


def down_stage(core, hT, units, evacuate, freed=()):
    nc, ps, c = core.nc, core.psum, core
    with core.stage() as block:

        @block.sync
        def _(sp):
            for u in [*freed, *units]:
                u.refill(sp)

        @block.tensor
        def _(pe):
            n = len(units) * DC
            for j, u in enumerate(units):
                u.wait_landed(pe)
                for i in range(DC):
                    k = j * DC + i
                    last = nc.tensor.matmul(ps[0][:, :], hT[:, k, :], u.data[:, i, :], start=(k == 0), stop=(k == n - 1))
                u.done(last)

        @block.vector
        def _(dve):
            units[-1].wait_done(dve)
            evacuate(ps[0][:, :], Chain(dve, c.sem("dve_chain")))


def heads_stage(core, q, k, v, mask, scale, out, value_rows=P):
    nc, ps, c = core.nc, core.psum, core
    G = HEADS // 4
    with core.scratch(scores0=[P, 4, P], scores1=[P, 4, P], probsT0=[P, 4, P], probsT1=[P, 4, P],
                      neg_max=[P, HEADS], total=[P, HEADS], inverse=[P, HEADS]) as (
        scores0, scores1, probsT0, probsT1, neg_max, total, inverse,
    ), core.stage() as block:
        scores, probsT = [scores0, scores1], [probsT0, probsT1]

        @block.tensor
        def _(pe):
            def score(g):
                if g >= 2:
                    pe.wait_ge(c.sem("scores_masked"), g - 1)
                for j in range(4):
                    last = nc.tensor.matmul(ps[g % 2][:, j * P:(j + 1) * P], q(4 * g + j), k(4 * g + j),
                                            start=True, stop=True)
                last.then_inc(c.sem("scores_ready"), 1)

            score(0)
            for g in range(G):
                if g + 1 < G:
                    score(g + 1)
                pe.wait_ge(c.sem("probs_ready"), g + 1)
                if g >= 2:
                    pe.wait_ge(c.sem("probsT_ready"), g - 1)
                for j in range(4):
                    last = nc.tensor.transpose(ps[2 + g % 2][:, j * P:(j + 1) * P], scores[g % 2][:, j, :], core.ident)
                last.then_inc(c.sem("probs_transposed"), 1)
                pe.wait_ge(c.sem("probsT_ready"), g + 1)
                if g >= 2:
                    pe.wait_ge(c.sem("out_stored"), g - 1)
                for j in range(4):
                    if value_rows == P:
                        to = ps[4 + g % 2][:, j * P:(j + 1) * P]
                    else:
                        to = ps[4 + g % 2][j * value_rows:(j + 1) * value_rows, 0:P]
                    last = nc.tensor.matmul(to, v(4 * g + j), probsT[g % 2][:, j, :], start=True, stop=True)
                last.then_inc(c.sem("out_ready"), 1)

        @block.vector
        def _(dve):
            link = Chain(dve, c.sem("dve_chain"))

            def add_mask(g):
                dve.wait_ge(c.sem("scores_ready"), g + 1)
                if g >= 2:
                    dve.wait_ge(c.sem("probs_transposed"), g - 1)
                link(nc.vector.scalar_tensor_tensor(
                    out=scores[g % 2][:, :, :], in0=ps[g % 2][:, :].rearrange("p (j t) -> p j t", j=4), scalar=scale,
                    in1=mask.unsqueeze(1).to_broadcast([P, 4, P]), op0=ALU.mult, op1=ALU.add))
                nc.vector.tensor_reduce(neg_max[:, 4 * g:4 * g + 4], scores[g % 2][:, :, :], X, ALU.max,
                                        negate=True).then_inc(c.sem("scores_masked"), 1)

            add_mask(0)
            for g in range(G):
                if g + 1 < G:
                    add_mask(g + 1)
                dve.wait_ge(c.sem("exp_ready"), 4 * g + 4)
                link(nc.vector.reciprocal(inverse[:, 4 * g:4 * g + 4], total[:, 4 * g:4 * g + 4]))
                nc.vector.tensor_tensor(scores[g % 2][:, :, :], scores[g % 2][:, :, :],
                                        inverse[:, 4 * g:4 * g + 4].unsqueeze(2).to_broadcast([P, 4, P]),
                                        ALU.mult).then_inc(c.sem("probs_ready"), 1)

        @block.scalar
        def _(act):
            def exps(g):
                act.wait_ge(c.sem("scores_masked"), g + 1)
                for h in range(4 * g, 4 * g + 4):
                    nc.scalar.activation(scores[g % 2][:, h % 4, :], scores[g % 2][:, h % 4, :], ACT.Exp,
                                         bias=neg_max[:, h:h + 1], accum_out=total[:, h:h + 1]).then_inc(
                        c.sem("exp_ready"), 1)

            exps(0)
            for g in range(G):
                if g + 1 < G:
                    exps(g + 1)
                act.wait_ge(c.sem("probs_transposed"), g + 1)
                if g >= 2:
                    act.wait_ge(c.sem("out_ready"), g - 1)
                nc.scalar.copy(probsT[g % 2][:, :, :].rearrange("p j t -> p (j t)"), ps[2 + g % 2][:, :]).then_inc(
                    c.sem("probsT_ready"), 1)
                act.wait_ge(c.sem("out_ready"), g + 1)
                out(g, ps[4 + g % 2]).then_inc(c.sem("out_stored"), 1)




def wide_scores_stage(core, qT, scores, extra_kT=None, maskrow=None):
    nc, ps, c = core.nc, core.psum, core
    with core.scratch(ctx0=[P, DC, GROUP], ctx1=[P, DC, GROUP], bias0=[P, TILE], bias1=[P, TILE], raw0=[P, TILE],
                      raw1=[P, TILE]) as (ctx0, ctx1, bias0, bias1, raw0, raw1), core.stage() as block:
        ctxT, bias, raw = [ctx0, ctx1], [bias0, bias1], [raw0, raw1]

        @block.sync
        def _(sp):
            for half in range(2):
                sp.dma_start(ctxT[half][:, :, :], core.dram["ctxT"][half]).then_inc(c.sem(f"ctxT_landed_{half}"), 16)
            if GROUPS > 2:
                with sp.Fori(0, GROUPS // 2 - 1) as i:
                    for half in range(2):
                        sp.wait_ge(c.sem("scores_ready"), i * 4 + (2 * half + 2))
                        sp.dma_start(ctxT[half][:, :, :], core.dram["ctxT"][bass.ds(i * 2 + (2 + half), 1)].rearrange(
                            "a p c n -> (a p) c n")).then_inc(c.sem(f"ctxT_landed_{half}"), 16)

        @block.tensor
        def _(pe):
            pe.sem_inc(c.sem("bank_free"), 4)
            with pe.Fori(0, GROUPS // 2) as i:
                for half in range(2):
                    pe.wait_ge(c.sem(f"ctxT_landed_{half}"), i * 16 + 16)
                    for t in range(2):
                        b = 2 * half + t
                        pe.wait_ge(c.sem("bank_free"), i * 4 + (b + 1))
                        for k in range(DC):
                            last = nc.tensor.matmul(ps[b][:, 0:TILE], qT[:, k, :],
                                                    ctxT[half][:, k, t * TILE:(t + 1) * TILE],
                                                    start=(k == 0), stop=(k == DC - 1))
                        last.then_inc(c.sem("scores_ready"), 1)
            if extra_kT is not None:
                for k in range(DC):
                    last = nc.tensor.matmul(ps[4][:, 0:P], qT[:, k, :], extra_kT[:, k, :],
                                            start=(k == 0), stop=(k == DC - 1))
                last.then_inc(c.sem("extra_ready"), 1)

        @block.vector
        def _(dve):
            link = Chain(dve, c.sem("dve_chain"))
            if maskrow is None:
                with dve.Fori(0, GROUPS // 2) as i:
                    for b in range(4):
                        dve.wait_ge(c.sem("scores_ready"), i * 4 + (b + 1))
                        nc.vector.tensor_copy(scores[:, bass.ds(i * (4 * TILE) + b * TILE, TILE)],
                                              ps[b][:, 0:TILE]).then_inc(c.sem("bank_free"), 1)
            else:
                with dve.Fori(0, GROUPS // 2) as i:
                    for b in range(4):
                        at = bass.ds(i * (4 * TILE) + b * TILE, TILE)
                        nc.vector.tensor_scalar(bias[b % 2][:, :], maskrow[:, at], 1.0, 1e30, ALU.subtract,
                                                ALU.mult).then_inc(c.sem("bias_made"), 1)
                        dve.wait_ge(c.sem("scores_ready"), i * 4 + (b + 1))
                        nc.vector.tensor_tensor(raw[b % 2][:, :], ps[b][:, 0:TILE], maskrow[:, at],
                                                ALU.mult).then_inc(c.sem("bank_free"), 1)
                        dve.wait_ge(c.sem("bias_made"), i * 4 + (b + 1))
                        dve.wait_ge(c.sem("bank_free"), i * 4 + (b + 5))
                        nc.vector.tensor_tensor(scores[:, at], raw[b % 2][:, :], bias[b % 2][:, :],
                                                ALU.add).then_inc(c.sem("masked"), 1)
                        dve.wait_ge(c.sem("masked"), i * 4 + (b + 1))
            if extra_kT is not None:
                dve.wait_ge(c.sem("extra_ready"), 1)
                link(nc.vector.tensor_copy(scores[:, KV:KV + P], ps[4][:, 0:P]))


def wide_values_stage(core, scores, out, extra_v=None):
    nc, ps, c = core.nc, core.psum, core
    keys = KV + (P if extra_v is not None else 0)
    with core.scratch(rows0=[P, PER, D], rows1=[P, PER, D], probs0=[P, GROUP], probs1=[P, GROUP],
                      probsT0=[P, PER, P], probsT1=[P, PER, P], neg_max=[P, 1], part=[P, 2], extra_part=[P, 1],
                      total=[P, 1], inverse=[P, 1], extra_p=[P, P], extra_pT=[P, P]) as (
        rows0, rows1, probs0, probs1, probsT0, probsT1, neg_max, part, extra_part, total, inverse, extra_p, extra_pT,
    ), core.stage() as block:
        rows, probs, probsT = [rows0, rows1], [probs0, probs1], [probsT0, probsT1]
        O = ps[4]

        @block.sync
        def _(sp):
            for half in range(2):
                sp.dma_start(rows[half][:, :, :], core.dram["ctx_rows"][half]).then_inc(c.sem(f"rows_landed_{half}"), 16)
            with sp.Fori(0, GROUPS // 2 - 1) as i:
                for half in range(2):
                    sp.wait_ge(c.sem("group_done"), i * 2 + (half + 1))
                    sp.dma_start(rows[half][:, :, :], core.dram["ctx_rows"][bass.ds(i * 2 + (2 + half), 1)].rearrange(
                        "a p k d -> (a p) k d")).then_inc(c.sem(f"rows_landed_{half}"), 16)

        @block.scalar
        def _(act):
            act.wait_ge(c.sem("max_ready"), 1)
            act.sem_inc(c.sem("probs_free"), 2)
            act.sem_inc(c.sem("parts_added"), 2)
            with act.Fori(0, GROUPS // 2) as i:
                for half in range(2):
                    act.wait_ge(c.sem("probs_free"), i * 2 + (half + 1))
                    act.wait_ge(c.sem("parts_added"), i * 2 + (half + 1))
                    nc.scalar.activation(probs[half][:, :], scores[:, bass.ds(i * (2 * GROUP) + half * GROUP, GROUP)],
                                         ACT.Exp, bias=neg_max[:, 0:1],
                                         accum_out=part[:, half:half + 1]).then_inc(c.sem("probs_ready"), 1)
                for half in range(2):
                    act.wait_ge(c.sem("transposed"), i * 2 + (half + 1))
                    nc.scalar.copy(probsT[half][:, 4:PER, :].rearrange("p k t -> p (k t)"),
                                   ps[2 * half + 1][:, 0:(PER - 4) * P]).then_inc(c.sem("probsT_tail_ready"), 1)
            if extra_v is not None:
                nc.scalar.activation(extra_p[:, :], scores[:, KV:KV + P], ACT.Exp, bias=neg_max[:, 0:1],
                                     accum_out=extra_part[:, :]).then_inc(c.sem("extra_p_ready"), 1)
                act.wait_ge(c.sem("extra_transposed"), 1)
                nc.scalar.copy(extra_pT[:, :], ps[5][:, 0:P]).then_inc(c.sem("extra_pT_ready"), 1)

        @block.tensor
        def _(pe):
            nc.tensor.matmul(O[:, :], core.zeros[:, 0:P], core.zeros[:, 0:D], start=True, stop=False,
                             skip_group_check=True)
            with pe.Fori(0, GROUPS // 2) as i:
                for half in range(2):
                    pe.wait_ge(c.sem("probs_ready"), i * 2 + (half + 1))
                    for k in range(PER):
                        to = ps[2 * half + k // 4][:, (k % 4) * P:(k % 4 + 1) * P]
                        last = nc.tensor.transpose(to, probs[half][:, k * P:(k + 1) * P], core.ident)
                    last.then_inc(c.sem("transposed"), 1)
                for half in range(2):
                    pe.wait_ge(c.sem(f"rows_landed_{half}"), i * 16 + 16)
                    pe.wait_ge(c.sem("probsT_head_ready"), i * 2 + (half + 1))
                    pe.wait_ge(c.sem("probsT_tail_ready"), i * 2 + (half + 1))
                    for k in range(PER):
                        last = nc.tensor.matmul(O[:, :], probsT[half][:, k, :], rows[half][:, k, :], start=False,
                                                stop=False, skip_group_check=True)
                    last.then_inc(c.sem("group_done"), 1)
            if extra_v is not None:
                pe.wait_ge(c.sem("extra_p_ready"), 1)
                nc.tensor.transpose(ps[5][:, 0:P], extra_p[:, :], core.ident).then_inc(c.sem("extra_transposed"), 1)
                pe.wait_ge(c.sem("extra_pT_ready"), 1)
                nc.tensor.matmul(O[:, :], extra_pT[:, :], extra_v, start=False, stop=True,
                                 skip_group_check=True).then_inc(c.sem("group_done"), 1)

        @block.vector
        def _(dve):
            link = Chain(dve, c.sem("dve_chain"))
            nc.vector.tensor_reduce(neg_max[:, :], scores[:, 0:keys], X, ALU.max, negate=True).then_inc(
                c.sem("max_ready"), 1)
            link(nc.vector.memset(total[:, :], 0.0))
            with dve.Fori(0, GROUPS // 2) as i:
                for half in range(2):
                    dve.wait_ge(c.sem("transposed"), i * 2 + (half + 1))
                    nc.vector.tensor_copy(probsT[half][:, 0:4, :].rearrange("p k t -> p (k t)"),
                                          ps[2 * half][:, :]).then_inc(c.sem("probsT_head_ready"), 1)
                    dve.sem_inc(c.sem("probs_free"), 1)
                    nc.vector.tensor_tensor(total[:, :], total[:, :], part[:, half:half + 1], ALU.add).then_inc(
                        c.sem("parts_added"), 1)
                    dve.wait_ge(c.sem("parts_added"), i * 2 + (half + 3))
            n = GROUPS
            if extra_v is not None:
                dve.wait_ge(c.sem("extra_p_ready"), 1)
                link(nc.vector.tensor_tensor(total[:, :], total[:, :], extra_part[:, :], ALU.add))
                n += 1
            link(nc.vector.reciprocal(inverse[:, :], total[:, :]))
            dve.wait_ge(c.sem("group_done"), n)
            link(nc.vector.tensor_scalar(out, O[:, :], inverse[:, 0:1], None, ALU.mult))




def add_to_x(core):
    def evacuate(bank, link):
        link(core.nc.vector.tensor_tensor(core.x, core.x, bank, ALU.add))
    return evacuate


def l0_xattn(core):
    ring, nc = core.ring, core.nc
    with core.scratch(scores=[P, KV + P], xn=[P, D], xnT=[P, DC, P], qT=[P, DC, P], kT=[P, DC, P], v=[P, D],
                      o=[P, D]) as (scores, xn, xnT, qT, kT, v, o):
        norm_stage(core, core.x, xn[:, :], xnT[:, :, :], 1e-5)
        cols_stage(core, xnT, ring.take("L0_xattn_wq"), qT, scale=D ** -0.5)
        cols_stage(core, xnT, ring.take("L0_xattn_wk"), kT)
        rows_stage(core, xnT, ring.take("L0_xattn_wv"), lambda j, bank, link: nc.vector.tensor_copy(v[:, :], bank))
        wide_scores_stage(core, qT, scores, extra_kT=kT)
        wide_values_stage(core, scores, o[:, :], extra_v=v[:, :])
        transpose_stage(core, o, qT, DC)
        down_stage(core, qT, ring.take("L0_xattn_wo"), add_to_x(core))


def small_products_stage(core, aT, products, evacuate, refills=()):
    nc, c = core.nc, core
    with core.stage() as block:

        @block.tensor
        def _(pe):
            for out, kind, w in products:
                for i in range(DC):
                    lhsT, rhs = (aT[:, i, :], w[:, i, :]) if kind == "rows" else (w[:, i, :], aT[:, i, :])
                    last = nc.tensor.matmul(out, lhsT, rhs, start=(i == 0), stop=(i == DC - 1))
            last.then_inc(c.sem("products_ready"), 1)

        @block.vector
        def _(dve):
            dve.wait_ge(c.sem("products_ready"), 1)
            evacuate(Chain(dve, c.sem("dve_chain")))


def chain_stage(core, steps):
    c = core
    with core.stage() as block:

        def run(engine, name):
            for n, (who, step) in enumerate(steps):
                if who == name:
                    if n:
                        engine.wait_ge(c.sem("step_done"), n)
                    step().then_inc(c.sem("step_done"), 1)

        block.vector(lambda dve: run(dve, "vector"))
        block.scalar(lambda act: run(act, "scalar"))
        block.gpsimd(lambda pool: run(pool, "gpsimd"))


def l0_attn(core):
    ring, nc, ps, c = core.ring, core.nc, core.psum, core
    small = core.operands[:, 0:DC * 400].rearrange("p (c n) -> p c n", c=DC)
    wk_idx, wk, wv, w_iw = small[:, :, 0:P], small[:, :, P:2 * P], small[:, :, 2 * P:3 * P], small[:, :, 3 * P:]
    hadamard = core.table["hadamard"]
    K = 64
    with core.scratch(xn=[P, D], xnT=[P, DC, P], qT=[P, HEADS, P], oT=[P, HEADS, P], keysT=[P, P], kT=[P, P],
                      v=[P, P], head_weight=[P, HEADS], index=[P, P], work=[P, P], top8=[P, 8], mask=[P, P]) as (
        xn, xnT, qT, oT, keysT, kT, v, head_weight, index, work, top8, mask,
    ):
        norm_stage(core, core.x, xn[:, :], xnT[:, :, :], 1e-5,
                   loads=[(core.operands[:, 0:DC * 400], core.dram["L0_attn_small"])])
        cols_stage(core, xnT, ring.take("L0_attn_wq_idx"), oT)

        def evacuate(link):
            nc.vector.tensor_copy(keysT[:, :], ps[0][:, 0:P])
            nc.vector.tensor_copy(kT[:, :], ps[1][:, 0:P])
            nc.vector.tensor_copy(v[:, :], ps[2][:, 0:P])
            link(nc.vector.tensor_copy(head_weight[:, :], ps[3][:, 0:HEADS]))

        small_products_stage(core, xnT, [(ps[0][:, 0:P], "cols", wk_idx), (ps[1][:, 0:P], "cols", wk),
                                         (ps[2][:, 0:P], "rows", wv), (ps[3][:, 0:HEADS], "rows", w_iw)], evacuate)

        with core.stage() as block:

            @block.tensor
            def _(pe):
                for g in range(4):
                    nc.tensor.matmul(ps[g][:, :], hadamard, oT[:, 4 * g:4 * g + 4, :].rearrange("p h t -> p (h t)"),
                                     start=True, stop=True).then_inc(c.sem("transform_ready"), 1)
                nc.tensor.matmul(ps[4][:, 0:P], hadamard, keysT[:, :], start=True, stop=True).then_inc(
                    c.sem("transform_ready"), 1)

            @block.scalar
            def _(act):
                for g in range(4):
                    act.wait_ge(c.sem("transform_ready"), g + 1)
                    nc.scalar.activation(qT[:, 4 * g:4 * g + 4, :].rearrange("p h t -> p (h t)"), ps[g][:, :],
                                         ACT.Copy, scale=P ** -0.5)

            @block.vector
            def _(dve):
                dve.wait_ge(c.sem("transform_ready"), 5)
                nc.vector.tensor_scalar(keysT[:, :], ps[4][:, 0:P], P ** -0.5, None, ALU.mult)

        with core.stage() as block:

            @block.tensor
            def _(pe):
                for h in range(HEADS):
                    last = nc.tensor.matmul(ps[h // 4][:, (h % 4) * P:(h % 4 + 1) * P], qT[:, h, :], keysT[:, :],
                                            start=True, stop=True)
                    if h % 4 == 3:
                        last.then_inc(c.sem("logits_ready"), 1)

            @block.scalar
            def _(act):
                for g in range(4):
                    act.wait_ge(c.sem("logits_ready"), g + 1)
                    nc.scalar.activation(oT[:, 4 * g:4 * g + 4, :].rearrange("p h t -> p (h t)"), ps[g][:, :],
                                         ACT.Relu).then_inc(c.sem("relu_ready"), 1)

            @block.vector
            def _(dve):
                link = Chain(dve, c.sem("dve_chain"))
                link(nc.vector.memset(index[:, :], 0.0))
                for h in range(HEADS):
                    dve.wait_ge(c.sem("relu_ready"), h // 4 + 1)
                    link(nc.vector.scalar_tensor_tensor(out=index[:, :], in0=oT[:, h, :],
                                                        scalar=head_weight[:, h:h + 1], in1=index[:, :],
                                                        op0=ALU.mult, op1=ALU.add))
                link(nc.vector.tensor_tensor(index[:, :], index[:, :], core.table["causal"], ALU.add))
                link(nc.vector.tensor_copy(work[:, :], index[:, :]))
                for _ in range(K // 8):
                    link(nc.vector.max(top8[:, :], work[:, :]))
                    link(nc.vector.match_replace(work[:, :], top8[:, :], work[:, :], TAKEN))
                link(nc.vector.tensor_scalar(index[:, :], index[:, :], NEG / 2, None, ALU.is_gt))
                link(nc.vector.scalar_tensor_tensor(out=mask[:, :], in0=work[:, :], scalar=TAKEN / 2,
                                                    in1=index[:, :], op0=ALU.is_le, op1=ALU.mult))
                link(nc.vector.tensor_scalar(mask[:, :], mask[:, :], 1.0, -NEG, ALU.subtract, ALU.mult))

        cols_stage(core, xnT, ring.take("L0_attn_wq"), qT)
        heads_stage(core, lambda h: qT[:, h, :], lambda h: kT[:, :], lambda h: v[:, :], mask[:, :], P ** -0.5,
                    lambda g, bank: nc.scalar.copy(oT[:, 4 * g:4 * g + 4, :].rearrange("p h t -> p (h t)"), bank[:, :]))
        down_stage(core, oT, ring.take("L0_attn_wo"), add_to_x(core))


def l0_ffn(core):
    ring, nc, ps = core.ring, core.nc, core.psum
    router = core.operands[:, 0:DC * 16].rearrange("p (c n) -> p c n", c=DC)
    bias = core.operands[:, DC * 16:DC * 16 + 16]
    E, PAD = 16, 8
    with core.scratch(xn=[P, D], xnT=[P, DC, P], h=[P, HEADS, P], hT=[P, HEADS, P], prob=[P, E + PAD],
                      left=[P, E + PAD], top8=[P, 8], neg_max=[P, 1], chosen=[P, E]) as (
        xn, xnT, h, hT, prob, left, top8, neg_max, chosen,
    ):
        norm_stage(core, core.x, xn[:, :], xnT[:, :, :], 1e-5,
                   loads=[(core.operands[:, 0:DC * 16], core.dram["L0_ffn_small"]),
                          (bias, core.dram["L0_ffn_rows"].partition_broadcast(P))])

        def evacuate(link):
            link(nc.vector.tensor_tensor(prob[:, 0:E], ps[0][:, 0:E], bias, ALU.add))

        small_products_stage(core, xnT, [(ps[0][:, 0:E], "rows", router)], evacuate)
        chain_stage(core, [
            ("vector", lambda: nc.vector.tensor_reduce(neg_max[:, :], prob[:, 0:E], X, ALU.max, negate=True)),
            ("scalar", lambda: nc.scalar.activation(prob[:, 0:E], prob[:, 0:E], ACT.Exp, bias=neg_max[:, 0:1])),
            ("vector", lambda: nc.vector.memset(prob[:, E:E + PAD], -1.0)),
            ("vector", lambda: nc.vector.max(top8[:, :], prob[:, :])),
            ("vector", lambda: nc.vector.memset(top8[:, 4:8], -1.0)),
            ("vector", lambda: nc.vector.match_replace(left[:, :], top8[:, :], prob[:, :], TAKEN)),
            ("vector", lambda: nc.vector.tensor_scalar(chosen[:, :], left[:, 0:E], TAKEN / 2, None, ALU.is_le)),
        ])
        rows_stage(core, xnT, ring.take("L0_ffn_W1"),
                   lambda j, bank, link: nc.scalar.activation(h[:, 4 * j:4 * j + 4, :].rearrange("p e t -> p (e t)"),
                                                              bank, ACT.Gelu),
                   on_scalar=True,
                   after=lambda link: link(nc.vector.tensor_tensor(
                       h[:, :, :], h[:, :, :], chosen[:, :].unsqueeze(2).to_broadcast([P, E, P]), ALU.mult)))
        transpose_stage(core, h[:, :, :].rearrange("p e t -> p (e t)"), hT, HEADS)
        down_stage(core, hT, ring.take("L0_ffn_W2"), add_to_x(core))


def l1_xattn(core):
    nc = core.nc
    with core.scratch(scores=[P, KV], xn=[P, D], xnT=[P, DC, P], o=[P, D], any_seen=[P, 1]) as (
        scores, xn, xnT, o, any_seen,
    ), nc.sbuf_tensor("seen", [P, KV], U8) as seen:
        norm_stage(core, core.x, xn[:, :], xnT[:, :, :], 1e-5, scale=D ** -0.5,
                   loads=[(seen[:, :], core.dram["memory_mask"].partition_broadcast(P))])
        wide_scores_stage(core, xnT, scores, maskrow=seen)
        wide_values_stage(core, scores, o[:, :])
        chain_stage(core, [
            ("vector", lambda: nc.vector.tensor_reduce(any_seen[:, :], seen[:, :], X, ALU.max)),
            ("vector", lambda: nc.vector.scalar_tensor_tensor(out=core.x, in0=o[:, :], scalar=any_seen[:, 0:1],
                                                              in1=core.x, op0=ALU.mult, op1=ALU.add)),
        ])


def rotation_steps(core, first, second, cos, sin, t):
    nc = core.nc
    V = nc.vector.tensor_tensor
    return [
        ("vector", lambda: V(t[0], first, cos, ALU.mult)),
        ("vector", lambda: V(t[1], second, sin, ALU.mult)),
        ("vector", lambda: V(t[2], second, cos, ALU.mult)),
        ("vector", lambda: V(t[3], first, sin, ALU.mult)),
        ("vector", lambda: V(first, t[0], t[1], ALU.subtract)),
        ("vector", lambda: V(second, t[2], t[3], ALU.add)),
    ]


def head_norm_steps(core, rows, heads, width, eps, square, sums, mean=True):
    nc = core.nc
    r3 = rows.rearrange("p (h d) -> p h d", h=heads)
    s3 = square.rearrange("p (h d) -> p h d", h=heads)
    return [
        ("vector", lambda: nc.vector.tensor_tensor(square, rows, rows, ALU.mult)),
        ("vector", lambda: nc.vector.tensor_reduce(sums, s3, X, ALU.add)),
        ("vector", lambda: nc.vector.tensor_scalar(sums, sums, 1.0 / width if mean else 1.0, eps, ALU.mult, ALU.add)),
        ("gpsimd", lambda: nc.gpsimd.tensor_tensor(sums, sums, core.minus_half[:, 0:heads], ALU.pow)),
        ("vector", lambda: nc.vector.tensor_tensor(r3, r3, sums.unsqueeze(2).to_broadcast([P, heads, width]),
                                                   ALU.mult)),
    ]


def l1_attn(core):
    ring, nc, ps, c = core.ring, core.nc, core.psum, core
    ops = core.operands
    b_in, b_out, gamma, beta = ops[:, 0:3 * D], ops[:, 3 * D:4 * D], ops[:, 4 * D:5 * D], ops[:, 5 * D:6 * D]
    R = D // 2
    cos, sin = core.table["cos1"], core.table["sin1"]
    with core.scratch(xn=[P, D], xnT=[P, DC, P], xg=[P, D], xgT=[P, DC, P], qkv=[P, 3 * D], square=[P, D],
                      turn=[P, 4, R // 2], sums=[P, 1], y=[P, D]) as (xn, xnT, xg, xgT, qkv, square, turn, sums, y):
        norm_stage(core, core.x, xn[:, :], xnT[:, :, :], 1e-5,
                   loads=[(ops[:, 0:6 * D], core.dram["L1_attn_rows"].partition_broadcast(P))])
        norm_stage(core, xn[:, :], xg[:, :], xgT[:, :, :], 1e-5, gain=gamma, shift=beta)
        rows_stage(core, xgT, ring.take("L1_attn_W_in"),
                   lambda j, bank, link: nc.vector.tensor_tensor(qkv[:, j * D:(j + 1) * D], bank,
                                                                 b_in[:, j * D:(j + 1) * D], ALU.add))
        steps = []
        for part in (1, 2):
            rows = qkv[:, part * D:(part + 1) * D]
            pairs = rows[:, 0:R].rearrange("p (i two) -> p i two", two=2)
            steps += rotation_steps(core, pairs[:, :, 0], pairs[:, :, 1], cos, sin, [turn[:, i, :] for i in range(4)])
            steps += head_norm_steps(core, rows, 1, D, 0.0, square[:, :], sums[:, :], mean=False)
        steps.append(("vector", lambda: nc.vector.tensor_tensor(y[:, :], qkv[:, D:2 * D], qkv[:, 2 * D:3 * D], ALU.mult)))
        chain_stage(core, steps)
        with core.stage() as block:

            @block.tensor
            def _(pe):
                nc.tensor.matmul(ps[0][:, :], core.ones, y[:, :], start=True, stop=True).then_inc(
                    c.sem("token_sum_ready"), 1)

            @block.vector
            def _(dve):
                link = Chain(dve, c.sem("dve_chain"))
                dve.wait_ge(c.sem("token_sum_ready"), 1)
                link(nc.vector.tensor_scalar(square[:, :], ps[0][:, :], 0.5, 0.5, ALU.mult, ALU.add))
                link(nc.vector.tensor_tensor(y[:, :], square[:, :], qkv[:, 0:D], ALU.mult))
                link(nc.vector.tensor_tensor(core.x, core.x, xn[:, :], ALU.add))
                link(nc.vector.tensor_tensor(core.x, core.x, b_out, ALU.add))

        transpose_stage(core, y, xgT, DC)
        down_stage(core, xgT, ring.take("L1_attn_W_out"), add_to_x(core))


def l1_ffn(core):
    ring, nc, ps, c = core.ring, core.nc, core.psum, core
    R, K = 64, 8
    ops = core.operands
    small = ops[:, 0:DC * 96].rearrange("p (c n) -> p c n", c=DC)
    upT, biases = ops[0:R, 384:384 + D], ops[:, 896:896 + R]
    with core.scratch(xn=[P, D], xnT=[P, DC, P], sig=[P, R // 2], logits=[P, R], mid=[P, R], top8=[P, 8], left=[P, R],
                      total=[P, 1], midT=[R, P]) as (xn, xnT, sig, logits, mid, top8, left, total, midT):
        norm_stage(core, core.x, xn[:, :], xnT[:, :, :], 1e-5,
                   loads=[(ops[:, 0:384], core.dram["L1_ffn_small"]), (upT, core.dram["L1_ffn_BT"]),
                          (biases, core.dram["L1_ffn_rows"].partition_broadcast(P))])

        def evacuate(link):
            nc.vector.tensor_copy(sig[:, :], ps[0][:, 0:R // 2])
            link(nc.vector.tensor_copy(mid[:, :], ps[0][:, R // 2:R // 2 + R]))

        small_products_stage(core, xnT, [(ps[0][:, 0:96], "rows", small)], evacuate)
        l3, b3 = logits[:, :].rearrange("p (r two) -> p r two", two=2), biases.rearrange("p (r two) -> p r two", two=2)
        V = nc.vector
        chain_stage(core, [
            ("scalar", lambda: nc.scalar.activation(sig[:, :], sig[:, :], ACT.Sigmoid)),
            ("vector", lambda: V.tensor_tensor(l3, sig[:, :].unsqueeze(2).to_broadcast([P, R // 2, 2]), b3, ALU.add)),
            ("vector", lambda: V.max(top8[:, :], logits[:, :])),
            ("vector", lambda: V.match_replace(left[:, :], top8[:, :], logits[:, :], TAKEN)),
            ("vector", lambda: V.tensor_reduce(total[:, :], top8[:, :], X, ALU.add)),
            ("vector", lambda: V.reciprocal(total[:, :], total[:, :])),
            ("vector", lambda: V.scalar_tensor_tensor(out=logits[:, :], in0=left[:, :], scalar=TAKEN / 2,
                                                      in1=logits[:, :], op0=ALU.is_le, op1=ALU.mult)),
            ("vector", lambda: V.tensor_scalar(logits[:, :], logits[:, :], total[:, 0:1], K * 16.0 / K, ALU.mult,
                                               ALU.mult)),
            ("vector", lambda: V.tensor_tensor(mid[:, :], mid[:, :], logits[:, :], ALU.mult)),
        ])
        (base,) = ring.take("L1_ffn_base_W")
        with core.stage() as block:

            @block.sync
            def _(sp):
                base.refill(sp)

            @block.tensor
            def _(pe):
                nc.tensor.transpose(ps[1][0:R, 0:P], mid[:, :], core.ident).then_inc(c.sem("transposed"), 1)
                base.wait_landed(pe)
                for i in range(DC):
                    last = nc.tensor.matmul(ps[0][:, :], xnT[:, i, :], base.data[:, i, :], start=(i == 0), stop=False)
                base.done(last)
                pe.wait_ge(c.sem("midT_ready"), 1)
                nc.tensor.matmul(ps[0][:, :], midT[:, :], upT, start=False, stop=True).then_inc(
                    c.sem("output_ready"), 1)

            @block.scalar
            def _(act):
                act.wait_ge(c.sem("transposed"), 1)
                nc.scalar.copy(midT[:, :], ps[1][0:R, 0:P]).then_inc(c.sem("midT_ready"), 1)

            @block.vector
            def _(dve):
                dve.wait_ge(c.sem("output_ready"), 1)
                nc.vector.tensor_tensor(core.x, core.x, ps[0][:, :], ALU.add)


KVH = 4
USES = 3 * PER


class SideBank:

    def __init__(self):
        self.before = {h: ("values" if h % 2 else "keys", h // 2) for h in range(2 * PER)}
        self.after = {2 * j + 2: ("keysT", j) for j in range(PER)}
        order = []
        for h in range(HEADS):
            order += [self.before[h]] if h in self.before else []
            order += [self.after[h]] if h in self.after else []
        self.index = {use: n for n, use in enumerate(order)}
        assert len(order) == USES


def over_groups(engine, group, count=GROUPS):
    group(1, -1, 0, False, True)
    with engine.Fori(0, count // 2 - 1) as i:
        for b in range(2):
            group(b, i * 2 + b, i + b, True, True)
    group(0, count - 2, count // 2 - 1, True, True)
    group(1, count - 1, None, True, False)


def grouped_stage(core, qT, wk, wv, bk, acc, total):
    nc, c, ps = core.nc, core, core.psum
    side = SideBank()
    with core.scratch(ctx0=[P, DC, P], ctx1=[P, DC, P], parts0=[P, 2, DC, P], parts1=[P, 2, DC, P],
                      w=[P, 2, 2, DC, D], keysT0=[P, KVH, GROUP], keysT1=[P, KVH, GROUP],
                      values0=[P, PER, D], values1=[P, PER, D], mask0=[P, 2, TILE], mask1=[P, 2, TILE],
                      probs0=[P, 2, TILE], probs1=[P, 2, TILE], probsT0=[P, PER, P], probsT1=[P, PER, P],
                      keys0=[P, D], keys1=[P, D], square=[P, D], sumsq=[P, KVH], rnorm=[P, KVH],
                      top=[P, HEADS], neg0=[P, HEADS], neg1=[P, HEADS], decay0=[P, HEADS], decay1=[P, HEADS],
                      part0=[P, HEADS], part1=[P, HEADS]) as (
        ctx0, ctx1, parts0, parts1, w, keysT0, keysT1, values0, values1, mask0, mask1, probs0, probs1, probsT0,
        probsT1, keys0, keys1, square, sumsq, rnorm, top, neg0, neg1, decay0, decay1, part0, part1,
    ), core.stage() as block:
        ctxT, keysT, values, mask = [ctx0, ctx1], [keysT0, keysT1], [values0, values1], [mask0, mask1]
        probs, probsT, keys, neg = [probs0, probs1], [probsT0, probsT1], [keys0, keys1], [neg0, neg1]
        decay, part, parts = [decay0, decay1], [part0, part1], [parts0, parts1]
        dram, units = core.dram, (wk, wv)

        @block.sync
        def _(sp):
            def load_mask(b, g, masked):
                sp.wait_ge(c.sem("scores_masked"), masked * HEADS + 2)
                sp.dma_start(mask[b][:, :, :].rearrange("p a n -> p (a n)"),
                             dram["score_mask"][bass.ds(g, 1)].rearrange("a p n -> (a p) n")).then_inc(
                    c.sem(f"mask_landed_{b}"), 16)

            def two_groups(i, chunks):
                for m in range(chunks):
                    sp.wait_ge(c.sem("ctx_lo_ready"), i * (2 * PER) + (m + 1))
                    sp.dma_start(ctxT[m % 2][:, :, :], dram["ctxT_chunks"][bass.ds(
                        i * (2 * PER) + (2 + m), 1)].rearrange("a p c n -> (a p) c n")).then_inc(
                        c.sem(f"ctxT_landed_{m % 2}"), 16)
                    if m == PER - 1:
                        load_mask(1, i * 2 + 1, i * 2)
                    if m == 2 * PER - 1:
                        load_mask(0, i * 2 + 2, i * 2 + 1)

            for b in range(2):
                sp.dma_start(ctxT[b][:, :, :], dram["ctxT_chunks"][b]).then_inc(c.sem(f"ctxT_landed_{b}"), 16)
            load_mask(0, 0, 0)
            for u in units:
                u.refill(sp)
            with sp.Fori(0, GROUPS // 2 - 1) as i:
                two_groups(i, 2 * PER)
            two_groups(GROUPS // 2 - 1, 2 * PER - 2)

        @block.tensor
        def _(pe):
            pe.wait_ge(c.sem("weight_lo_ready"), 2)
            for u in units:
                u.done(nc.tensor.matmul(ps[7][:, 0:P], core.zeros[:, 0:P], core.zeros[:, 0:P], start=True, stop=True))

            def project(b, use, g):
                what, j = use
                wait_count(pe, c.sem("side_evacuated"), g * USES + side.index[use])
                if what == "keysT":
                    pe.wait_ge(c.sem("keys_normed"), g * PER + (j + 1))
                    for kh in range(KVH):
                        last = nc.tensor.transpose(ps[7][:, kh * P:(kh + 1) * P],
                                                   keys[j % 2][:, kh * P:(kh + 1) * P], core.ident)
                else:
                    pe.wait_ge(c.sem("ctx_lo_ready"), g * PER + (j + 1))
                    which, own = ("keys", "values").index(what), parts[(b + j) % 2]
                    for i in range(DC):
                        last = matmul_parts(nc, ps[7], [own[:, s, i, :] for s in range(2)],
                                            [w[:, which, s, i, :] for s in range(2)], i == 0, i == DC - 1)
                last.then_inc(c.sem("side_product"), 1)

            def score(b, h, g):
                pe.wait_ge(c.sem("scores_masked"), g * HEADS + (h + 1))
                for t in range(2):
                    last = nc.tensor.matmul(ps[2 * (h % 2) + t][:, 0:TILE], qT[:, h, :],
                                            keysT[b][:, h // 4, t * TILE:(t + 1) * TILE], start=True, stop=True)
                last.then_inc(c.sem("scores_ready"), 1)

            def transpose_probs(h, g):
                pe.wait_ge(c.sem("probs_ready"), g * HEADS + (h + 1))
                pe.wait_ge(c.sem("probsT_head_ready"), g * HEADS + (h + 1))
                pe.wait_ge(c.sem("probsT_tail_ready"), g * HEADS + (h + 1))
                flat = probs[h % 2][:, :, :].rearrange("p a n -> p (a n)")
                for k in range(PER):
                    last = nc.tensor.transpose(ps[4 + k // 4][:, (k % 4) * P:(k % 4 + 1) * P],
                                               flat[:, k * P:(k + 1) * P], core.ident)
                last.then_inc(c.sem("probs_transposed"), 1)

            def weigh(b, h, g):
                pe.wait_ge(c.sem("probsT_head_ready"), g * HEADS + (h + 2))
                pe.wait_ge(c.sem("probsT_tail_ready"), g * HEADS + (h + 2))
                pe.wait_ge(c.sem("out_added"), g * HEADS + (h + 1))
                kh = h // 4
                for k in range(PER):
                    last = nc.tensor.matmul(ps[6][:, 0:P], probsT[h % 2][:, k, :],
                                            values[b][:, k, kh * P:(kh + 1) * P], start=(k == 0),
                                            stop=(k == PER - 1))
                last.then_inc(c.sem("out_ready"), 1)

            def group(b, g, landed, attend, prepare):
                if attend:
                    pe.wait_ge(c.sem("side_evacuated"), g * USES + USES)
                    score(b, 0, g)
                for h in range(HEADS):
                    if attend and h + 1 < HEADS:
                        score(b, h + 1, g)
                    if prepare and h in side.before:
                        project(1 - b, side.before[h], g + 1)
                    if attend:
                        transpose_probs(h, g)
                        if h > 0:
                            weigh(b, h - 1, g)
                    if prepare and h in side.after:
                        project(1 - b, side.after[h], g + 1)
                if attend:
                    weigh(b, HEADS - 1, g)

            over_groups(pe, group)

        def splits(g, j):
            return not (isinstance(g, int) and g * PER + j + 1 >= GROUPS * PER)

        @block.vector
        def _(dve):
            def ctx_lo(b, g, j):
                dve.wait_ge(c.sem("ctx_hi_ready"), g * PER + (j + 1))
                nc.vector.tensor_tensor(short(parts[b][:, 1, :, :]), ctxT[b][:, :, :], parts[b][:, 0, :, :],
                                        ALU.subtract).then_inc(c.sem("ctx_lo_ready"), 1)

            def evacuate_keys(g, j):
                dve.wait_ge(c.sem("side_product"), g * USES + (side.index["keys", j] + 1))
                nc.vector.tensor_tensor(keys[j % 2][:, :], ps[7], bk, ALU.add).then_inc(c.sem("side_evacuated"), 1)

            def spread_of_keys(g, j):
                dve.wait_ge(c.sem("keys_squared"), g * PER + (j + 1))
                nc.vector.tensor_reduce(sumsq[:, :], square[:, :].rearrange("p (h d) -> p h d", h=KVH), X,
                                        ALU.add).then_inc(c.sem("sumsq_ready"), 1)
                dve.wait_ge(c.sem("sumsq_ready"), g * PER + (j + 1))
                nc.vector.tensor_scalar(sumsq[:, :], sumsq[:, :], 1.0 / P, 1e-6, ALU.mult, ALU.add).then_inc(
                    c.sem("spread_ready"), 1)

            def norm_keys(g, j):
                dve.wait_ge(c.sem("rnorm_ready"), g * PER + (j + 1))
                k3 = keys[j % 2][:, :].rearrange("p (h d) -> p h d", h=KVH)
                nc.vector.tensor_tensor(k3, k3, rnorm[:, :].unsqueeze(2).to_broadcast([P, KVH, P]),
                                        ALU.mult).then_inc(c.sem("keys_normed"), 1)

            def store_keysT(b, g, j):
                dve.wait_ge(c.sem("side_product"), g * USES + (side.index["keysT", j] + 1))
                nc.vector.tensor_copy(keysT[b][:, :, j * P:(j + 1) * P], ps[7].rearrange(
                    "p (h t) -> p h t", h=KVH)).then_inc(c.sem("side_evacuated"), 1)

            def mask_scores(b, h, g):
                dve.wait_ge(c.sem("scores_ready"), g * HEADS + (h + 1))
                dve.wait_ge(c.sem("probs_transposed"), g * HEADS + (h + 1))
                dve.sem_inc(c.sem("masking_started"), 1)
                nc.vector.tensor_tensor_reduce(
                    out=probs[h % 2][:, :, :], in0=core.banks[:, 2 * (h % 2):2 * (h % 2) + 2, 0:TILE],
                    in1=mask[b][:, :, :], scale=1.0, scalar=-3e38, op0=ALU.add, op1=ALU.max,
                    accum_out=top[:, h:h + 1]).then_inc(c.sem("scores_masked"), 1)
                dve.wait_ge(c.sem("scores_masked"), g * HEADS + (h + 3))
                nc.vector.scalar_tensor_tensor(out=neg[b][:, h:h + 1], in0=top[:, h:h + 1], scalar=-1.0,
                                               in1=neg[1 - b][:, h:h + 1], op0=ALU.mult, op1=ALU.min).then_inc(
                    c.sem("max_ready"), 1)

            def add_out(b, h, g):
                dve.wait_ge(c.sem("out_ready"), g * HEADS + (h + 1))
                nc.vector.scalar_tensor_tensor(out=acc[:, h, :], in0=acc[:, h, :], scalar=decay[b][:, h:h + 1],
                                               in1=ps[6][:, 0:P], op0=ALU.mult,
                                               op1=ALU.add).then_inc(c.sem("out_added"), 1)

            def group(b, g, landed, attend, prepare):
                n = g + 1
                if attend:
                    dve.wait_ge(c.sem(f"mask_landed_{b}"), (g - b) * 8 + 16)
                    mask_scores(b, 0, g)
                for h in range(HEADS):
                    if prepare and h % 2 == 1 and h - 1 in side.after:
                        store_keysT(1 - b, n, side.after[h - 1][1])
                    if attend and h > 1:
                        add_out(b, h - 2, g)
                    if attend and h + 1 < HEADS:
                        mask_scores(b, h + 1, g)
                    if prepare and h in side.before and h % 2 == 0:
                        evacuate_keys(n, h // 2)
                        if splits(n, h // 2):
                            ctx_lo((b + h // 2) % 2, n, h // 2 + 1)
                    if prepare and h % 2 == 0 and h > 0:
                        norm_keys(n, h // 2 - 1)
                    if attend:
                        dve.wait_ge(c.sem("probs_transposed"), g * HEADS + (h + 3))
                        nc.vector.tensor_copy(probsT[h % 2][:, 0:4, :].rearrange("p k t -> p (k t)"),
                                              ps[4]).then_inc(c.sem("probsT_head_ready"), 1)
                    if prepare and h in side.before and h % 2 == 1:
                        spread_of_keys(n, h // 2)
                if attend:
                    add_out(b, HEADS - 2, g)
                    add_out(b, HEADS - 1, g)
                    dve.wait_ge(c.sem("probs_ready"), g * HEADS + HEADS)
                    nc.vector.tensor_tensor(total, total, decay[b][:, :], ALU.mult).then_inc(c.sem("totalled"), 1)
                    dve.wait_ge(c.sem("totalled"), g * 2 + 1)
                    nc.vector.tensor_tensor(total, total, part[b][:, :], ALU.add).then_inc(c.sem("totalled"), 1)
                    dve.wait_ge(c.sem("totalled"), g * 2 + 2)

            dve.sem_inc(c.sem("scores_masked"), 2)
            dve.sem_inc(c.sem("probs_transposed"), 2)
            dve.sem_inc(c.sem("out_added"), 1)
            dve.sem_inc(c.sem("probsT_head_ready"), 1)
            dve.sem_inc(c.sem("probsT_tail_ready"), 1)
            nc.vector.memset(neg[1][:, :], 3e38)
            nc.vector.memset(total, 0.0)
            nc.vector.memset(acc.rearrange("p h d -> p (h d)"), 0.0).then_inc(c.sem("cleared"), 1)
            dve.wait_ge(c.sem("cleared"), 1)
            ctx_lo(0, 0, 0)
            for k, u in enumerate(units):
                dve.wait_ge(c.sem("weight_hi_ready"), k + 1)
                nc.vector.tensor_tensor(short(w[:, k, 1, :, :]), u.data, w[:, k, 0, :, :], ALU.subtract).then_inc(
                    c.sem("weight_lo_ready"), 1)
            over_groups(dve, group)

        @block.gpsimd
        def _(pool):
            with pool.Fori(0, GROUPS * PER) as n:
                pool.wait_ge(c.sem("spread_ready"), n + 1)
                nc.gpsimd.tensor_tensor(rnorm[:, :], sumsq[:, :], core.minus_half[:, 0:KVH], ALU.pow).then_inc(
                    c.sem("rnorm_ready"), 1)

        @block.scalar
        def _(act):
            def ctx_hi(b, g, j):
                act.wait_ge(c.sem(f"ctxT_landed_{b}"), g * (8 * PER) + ((j - b) * 8 + 16))
                nc.scalar.copy(short(parts[b][:, 0, :, :]), ctxT[b][:, :, :]).then_inc(c.sem("ctx_hi_ready"), 1)

            def square_keys(g, j):
                act.wait_ge(c.sem("side_evacuated"), g * USES + (side.index["keys", j] + 1))
                wait_count(act, c.sem("sumsq_ready"), g * PER + j)
                nc.scalar.activation(square[:, :], keys[j % 2][:, :], ACT.Square).then_inc(c.sem("keys_squared"), 1)

            def store_values(b, g, j):
                act.wait_ge(c.sem("side_product"), g * USES + (side.index["values", j] + 1))
                nc.scalar.copy(values[b][:, j, :], ps[7]).then_inc(c.sem("side_evacuated"), 1)

            def exp_scores(b, h, g):
                act.wait_ge(c.sem("max_ready"), g * HEADS + (h + 1))
                nc.scalar.activation(decay[b][:, h:h + 1], neg[1 - b][:, h:h + 1], ACT.Exp, scale=-1.0,
                                     bias=neg[b][:, h:h + 1])
                flat = probs[h % 2][:, :, :].rearrange("p a n -> p (a n)")
                nc.scalar.activation(flat, flat, ACT.Exp, bias=neg[b][:, h:h + 1],
                                     accum_out=part[b][:, h:h + 1]).then_inc(c.sem("probs_ready"), 1)

            def group(b, g, landed, attend, prepare):
                n = g + 1
                if attend:
                    exp_scores(b, 0, g)
                for h in range(HEADS):
                    if attend and h + 1 < HEADS:
                        exp_scores(b, h + 1, g)
                    if prepare and h in side.before and h % 2 == 0 and splits(n, h // 2):
                        act.wait_ge(c.sem("side_product"), n * USES + (side.index["keys", h // 2] + 1))
                        ctx_hi((b + h // 2) % 2, n, h // 2 + 1)
                    if prepare and h in side.before and h % 2 == 1:
                        store_values(1 - b, n, h // 2)
                    if attend:
                        act.wait_ge(c.sem("probs_transposed"), g * HEADS + (h + 3))
                        nc.scalar.copy(probsT[h % 2][:, 4:PER, :].rearrange("p k t -> p (k t)"),
                                       ps[5][:, 0:(PER - 4) * P]).then_inc(c.sem("probsT_tail_ready"), 1)
                    if prepare and h in side.before and h % 2 == 0:
                        square_keys(n, h // 2)

            ctx_hi(0, 0, 0)
            for k, u in enumerate(units):
                u.wait_landed(act)
                nc.scalar.copy(short(w[:, k, 0, :, :]), u.data).then_inc(c.sem("weight_hi_ready"), 1)
            over_groups(act, group)


def l2_xattn(core):
    ring, nc = core.ring, core.nc
    ops = core.operands
    bk, bv = ops[:, 0:D], ops[:, D:2 * D]
    qn, kn = ops[:, 2 * D:2 * D + P], ops[:, 2 * D + P:2 * D + 2 * P]
    rows = core.dram["L2_xattn_rows"]
    V = nc.vector
    with core.scratch(qT=[P, HEADS, P], acc=[P, HEADS, P], total=[P, HEADS]) as (qT, acc, total):
        with core.scratch(xn=[P, D], xnT=[P, DC, P], q=[P, HEADS * P], square=[P, HEADS * P], sums=[P, HEADS],
                          bias=[P, HEADS * P]) as (xn, xnT, q, square, sums, bias):
            norm_stage(core, core.x, xn[:, :], xnT[:, :, :], 1e-5,
                       loads=[(ops, rows[0:2 * D + 2 * P].partition_broadcast(P)),
                              (bias[:, :], rows[2 * D + 2 * P:2 * D + 2 * P + HEADS * P].partition_broadcast(P))])
            rows_stage(core, xnT, ring.take("L2_xattn_Wq"),
                       lambda j, bank, link: V.tensor_tensor(q[:, j * D:(j + 1) * D], bank,
                                                             bias[:, j * D:(j + 1) * D], ALU.add))
            q3 = q[:, :].rearrange("p (h d) -> p h d", h=HEADS)
            steps = head_norm_steps(core, q[:, :], HEADS, P, 1e-6, square[:, :], sums[:, :])
            for w in (qn, kn):
                steps.append(("vector", lambda w=w: V.tensor_tensor(q3, q3, w.unsqueeze(1).to_broadcast(
                    [P, HEADS, P]), ALU.mult)))
            chain_stage(core, steps)
            transpose_stage(core, q, qT, HEADS, scale=P ** -0.5)
        (wk,), (wv,) = ring.take("L2_xattn_Wk"), ring.take("L2_xattn_Wv")
        grouped_stage(core, qT, wk, wv, bk, acc[:, :, :], total[:, :])
        acc4 = acc[:, :, :].rearrange("p (k g) d -> p k g d", k=KVH)
        bv4 = bv.rearrange("p (k d) -> p k d", k=KVH).unsqueeze(2).to_broadcast([P, KVH, HEADS // KVH, P])
        chain_stage(core, [
            ("vector", lambda: V.reciprocal(total[:, :], total[:, :])),
            ("vector", lambda: V.tensor_tensor(acc[:, :, :], acc[:, :, :],
                                               total[:, :].unsqueeze(2).to_broadcast([P, HEADS, P]), ALU.mult)),
            ("vector", lambda: V.tensor_tensor(acc4, acc4, bv4, ALU.add)),
        ])
        transpose_stage(core, acc[:, :, :].rearrange("p h d -> p (h d)"), qT, HEADS)
        down_stage(core, qT, ring.take("L2_xattn_Wo"), add_to_x(core))


def l2_attn(core):
    ring, nc = core.ring, core.nc
    W = D // HEADS
    ops = core.operands
    V = nc.vector
    with core.scratch(xn=[P, D], xnT=[P, DC, P], q=[P, D], k=[P, D], v=[P, D], qT=[P, DC, P], kT=[P, DC, P],
                      own_qT=[P, HEADS, P], oT=[P, DC, P]) as (xn, xnT, q, k, v, qT, kT, own_qT, oT):
        norm_stage(core, core.x, xn[:, :], xnT[:, :, :], 1e-5,
                   loads=[(ops, core.dram["L2_attn_rows"].partition_broadcast(P))])
        rows_stage(core, xnT, ring.take("L2_attn_wq") + ring.take("L2_attn_wk") + ring.take("L2_attn_wv"),
                   lambda j, bank, link: V.tensor_tensor((q, k, v)[j][:, :], bank, ops[:, j * D:(j + 1) * D], ALU.add))
        transpose_stage(core, q, qT, DC)
        transpose_stage(core, k, kT, DC)
        own4 = own_qT[:, :, :].rearrange("p (c b) t -> p c b t", b=4)
        steps = [("vector", lambda: V.memset(own_qT[:, :, :].rearrange("p h t -> p (h t)"), 0.0))]
        for b in range(4):
            at = slice(W * b, W * (b + 1))
            steps.append(("vector", lambda at=at, b=b: V.tensor_copy(own4[at, :, b, :], qT[at, :, :])))
        steps.append(("vector", lambda: V.tensor_tensor(core.x, core.x, ops[:, 3 * D:4 * D], ALU.add)))
        chain_stage(core, steps)
        heads_stage(core, lambda h: own_qT[:, h, :], lambda h: kT[:, h // 4, :], lambda h: v[:, h * W:(h + 1) * W],
                    core.table["causal"], W ** -0.5, lambda g, bank: nc.scalar.copy(oT[:, g, :], bank[:, 0:P]),
                    value_rows=W)
        down_stage(core, oT, ring.take("L2_attn_wo"), add_to_x(core))


def l2_ffn(core):
    ring, nc, ps, c = core.ring, core.nc, core.psum, core
    F = 2048
    V = nc.vector
    with core.scratch(xn=[P, D], xnT=[P, DC, P], h=[P, F], other=[P, F], hT=[P, HEADS, P], outT=[P, HEADS, P]) as (
        xn, xnT, h, other, hT, outT,
    ):
        norm_stage(core, core.x, xn[:, :], xnT[:, :, :], 1e-5)
        rows_stage(core, xnT, ring.take("L2_ffn_W1"),
                   lambda j, bank, link: nc.scalar.activation(h[:, j * D:(j + 1) * D], bank, ACT.Silu), on_scalar=True)
        rows_stage(core, xnT, ring.take("L2_ffn_W3"),
                   lambda j, bank, link: V.tensor_tensor(h[:, j * D:(j + 1) * D], h[:, j * D:(j + 1) * D], bank,
                                                         ALU.mult))
        steps, a, b = [], h, other
        for width in (P, 2 * P, 4 * P, 8 * P):
            va, vb = (t[:, :].rearrange("p (n two w) -> p n two w", two=2, w=width) for t in (a, b))
            for half, op in enumerate((ALU.add, ALU.subtract)):
                steps.append(("vector", lambda va=va, vb=vb, half=half, op=op: V.tensor_tensor(
                    vb[:, :, half, :], va[:, :, 0, :], va[:, :, 1, :], op)))
            a, b = b, a
        chain_stage(core, steps)
        transpose_stage(core, a, hT, HEADS)
        with core.stage() as block:

            @block.tensor
            def _(pe):
                for g in range(4):
                    nc.tensor.matmul(ps[g], core.table["hadamard"], hT[:, 4 * g:4 * g + 4, :].rearrange(
                        "p h t -> p (h t)"), start=True, stop=True).then_inc(c.sem("transform_ready"), 1)

            @block.scalar
            def _(act):
                for g in range(4):
                    act.wait_ge(c.sem("transform_ready"), g + 1)
                    nc.scalar.activation(outT[:, 4 * g:4 * g + 4, :].rearrange("p h t -> p (h t)"), ps[g],
                                         ACT.Copy, scale=F ** -0.5)

        down_stage(core, outT, ring.take("L2_ffn_W2"), add_to_x(core))


NARROW = 32
W16 = D // NARROW


def narrow_stage(core, own_qT, wkeys, wvalues):
    nc, c, ps = core.nc, core, core.psum
    chunks = KV // P
    with core.scratch(ctx0=[P, DC, P], ctx1=[P, DC, P], parts0=[P, 2, DC, P], parts1=[P, 2, DC, P],
                      keysT0=[P, 8, P], keysT1=[P, 8, P], values0=[P, NARROW, 32], values1=[P, NARROW, 32],
                      probs0=[P, 4, D], probs1=[P, 4, D], keys=[P, D], key_parts=[P, HEADS, 2, 32], square=[P, D],
                      sumsq=[P, NARROW], rnorm=[P, NARROW], w=[P, 2, 2, DC, D]) as (
        ctx0, ctx1, parts0, parts1, keysT0, keysT1, values0, values1, probs0, probs1, keys, key_parts, square,
        sumsq, rnorm, w,
    ), core.stage() as block:
        ctxT, parts, keysT, values = [ctx0, ctx1], [parts0, parts1], [keysT0, keysT1], [values0, values1]
        probs = [probs0, probs1]
        units = (wkeys, wvalues)

        def splits(g):
            return not (isinstance(g, int) and g + 2 >= chunks)

        @block.sync
        def _(sp):
            chunk_of = core.dram["ctxT_chunks"]
            for b in range(2):
                sp.dma_start(ctxT[b][:, :, :], chunk_of[b]).then_inc(c.sem(f"ctxT_landed_{b}"), 16)
            for u in units:
                u.refill(sp)
            with sp.Fori(0, chunks // 2 - 1) as i:
                for b in range(2):
                    sp.wait_ge(c.sem("ctx_lo_ready"), i * 2 + (b + 1))
                    sp.dma_start(ctxT[b][:, :, :], chunk_of[bass.ds(i * 2 + (2 + b), 1)].rearrange(
                        "a p c n -> (a p) c n")).then_inc(c.sem(f"ctxT_landed_{b}"), 16)

        @block.tensor
        def _(pe):
            def project(b, n, which, bank, signal):
                for i in range(DC):
                    last = matmul_parts(nc, ps[bank], [parts[b][:, s, i, :] for s in range(2)],
                                        [w[:, which, s, i, :] for s in range(2)], i == 0, i == DC - 1)
                last.then_inc(c.sem(signal), 1)

            def project_keys(b, n):
                pe.wait_ge(c.sem("ctx_lo_ready"), n + 1)
                wait_count(pe, c.sem("keysT_head_stored"), n)
                project(b, n, 0, 6, "keys_product")

            def project_values(b, n):
                wait_count(pe, c.sem("keysT_tail_stored"), n)
                project(b, n, 1, 7, "values_product")

            def transpose_keys(n):
                pe.wait_ge(c.sem("key_hi_ready"), n + 1)
                pe.wait_ge(c.sem("key_lo_ready"), n + 1)
                flat = key_parts[:, :, :, :].rearrange("p g s f -> p (g s f)")
                for bank in (6, 7):
                    if bank == 7:
                        pe.wait_ge(c.sem("values_stored"), n + 1)
                    for i in range(DC):
                        at = ((bank - 6) * DC + i) * P
                        last = nc.tensor.transpose(ps[bank][:, i * P:(i + 1) * P], flat[:, at:at + P], core.ident)
                    last.then_inc(c.sem("keysT_product"), 1)

            def score(b, g, t):
                pe.wait_ge(c.sem("probs_ready"), g * 2 + (t + 1))
                for half in range(2):
                    for s in range(2):
                        for r in range(4):
                            at, k = slice(64 * (r % 2), 64 * (r % 2) + 64), 2 * (2 * t + half) + r // 2
                            last = nc.tensor.matmul(ps[r][:, half * 2 * P:(half + 1) * 2 * P],
                                                    short(keysT[b][at, k, :]),
                                                    short(own_qT[at, k, s, :, :].rearrange("p e t -> p (e t)")),
                                                    start=(s == 0), stop=(s == 1))
                last.then_inc(c.sem("scores_ready"), 1)

            def weigh(b, g, t):
                pe.wait_ge(c.sem("probs_ready"), g * 2 + (t + 2))
                for n in range(4 * t, 4 * t + 4):
                    half, e = n // 2 % 2, n % 2
                    for j in range(4):
                        last = nc.tensor.matmul(ps[4 + t][32 * j:32 * j + 32, (n % 4) * P:(n % 4 + 1) * P],
                                                values[b][:, 4 * n - 3 * e + 2 * j, :],
                                                probs[t][:, j, (2 * half + e) * P:(2 * half + e + 1) * P],
                                                start=False, stop=False, skip_group_check=True)
                last.then_inc(c.sem("round_done"), 1)

            def chunk(b, g, landed, attend, prepare):
                n = g + 1
                if prepare:
                    project_keys(1 - b, n)
                if attend:
                    pe.wait_ge(c.sem("keysT_head_stored"), g + 1)
                    pe.wait_ge(c.sem("keysT_tail_stored"), g + 1)
                    score(b, g, 0)
                if prepare:
                    project_values(1 - b, n)
                if attend:
                    score(b, g, 1)
                    weigh(b, g, 0)
                    weigh(b, g, 1)
                if prepare:
                    transpose_keys(n)

            for bank in (4, 5):
                nc.tensor.matmul(ps[bank], core.zeros[:, 0:P], core.zeros[:, :], start=True, stop=False,
                                 skip_group_check=True)
            pe.wait_ge(c.sem("weight_lo_ready"), 2)
            for u in units:
                u.done(nc.tensor.matmul(ps[0][:, 0:P], core.zeros[:, 0:P], core.zeros[:, 0:P], start=True,
                                        stop=True))
            over_groups(pe, chunk, chunks)

        @block.vector
        def _(dve):
            def ctx_lo(b, m):
                dve.wait_ge(c.sem("ctx_hi_ready"), m + 1)
                nc.vector.tensor_tensor(short(parts[b][:, 1, :, :]), ctxT[b][:, :, :], parts[b][:, 0, :, :],
                                        ALU.subtract).then_inc(c.sem("ctx_lo_ready"), 1)

            def chunk(b, g, landed, attend, prepare):
                if not prepare:
                    return
                n = g + 1
                dve.wait_ge(c.sem("keys_squared"), n + 1)
                nc.vector.tensor_reduce(sumsq[:, :], square[:, :].rearrange("p (h d) -> p h d", h=NARROW), X,
                                        ALU.add).then_inc(c.sem("sumsq_ready"), 1)
                dve.wait_ge(c.sem("sumsq_ready"), n + 1)
                nc.vector.tensor_scalar(sumsq[:, :], sumsq[:, :], 1.0 / W16, 1e-6, ALU.mult, ALU.add).then_inc(
                    c.sem("spread_ready"), 1)
                if splits(g):
                    ctx_lo(b, n + 1)
                dve.wait_ge(c.sem("rnorm_ready"), n + 1)
                nc.vector.tensor_tensor(keys[:, :].rearrange("p (h d) -> p h d", h=NARROW),
                                        ps[6].rearrange("p (h d) -> p h d", h=NARROW),
                                        rnorm[:, :].unsqueeze(2).to_broadcast([P, NARROW, W16]),
                                        ALU.mult).then_inc(c.sem("keys_normed"), 1)
                dve.wait_ge(c.sem("key_hi_ready"), n + 1)
                nc.vector.tensor_tensor(short(key_parts[:, :, 1, :]), keys[:, :].rearrange("p (g f) -> p g f", f=32),
                                        key_parts[:, :, 0, :], ALU.subtract).then_inc(c.sem("key_lo_ready"), 1)
                dve.wait_ge(c.sem("values_product"), n + 1)
                nc.vector.tensor_copy(values[1 - b][:, :, 0:W16], ps[7].rearrange(
                    "p (h d) -> p h d", h=NARROW)).then_inc(c.sem("values_stored"), 1)
                dve.wait_ge(c.sem("keysT_product"), n * 2 + 1)
                nc.vector.tensor_copy(short(keysT[1 - b][:, 0:DC, :].rearrange("p c t -> p (c t)")), ps[6]).then_inc(
                    c.sem("keysT_head_stored"), 1)

            for b in range(2):
                nc.vector.memset(values[b][:, :, :].rearrange("p h d -> p (h d)"), 0.0).then_inc(c.sem("cleared"), 1)
            dve.wait_ge(c.sem("cleared"), 2)
            for b in range(2):
                nc.vector.memset(values[b][:, :, W16:W16 + 1], 1.0).then_inc(c.sem("cleared"), 1)
            dve.wait_ge(c.sem("cleared"), 4)
            ctx_lo(0, 0)
            for k, u in enumerate(units):
                dve.wait_ge(c.sem("weight_hi_ready"), k + 1)
                nc.vector.tensor_tensor(short(w[:, k, 1, :, :]), u.data, w[:, k, 0, :, :], ALU.subtract).then_inc(
                    c.sem("weight_lo_ready"), 1)
            over_groups(dve, chunk, chunks)

        @block.gpsimd
        def _(pool):
            with pool.Fori(0, chunks) as n:
                pool.wait_ge(c.sem("spread_ready"), n + 1)
                nc.gpsimd.tensor_tensor(rnorm[:, :], sumsq[:, :], core.minus_half[:, 0:NARROW], ALU.pow).then_inc(
                    c.sem("rnorm_ready"), 1)

        @block.scalar
        def _(act):
            def ctx_hi(b, m, landed):
                act.wait_ge(c.sem(f"ctxT_landed_{b}"), landed)
                wait_count(act, c.sem("values_product"), m - 1 if not isinstance(m, int) else max(m - 1, 0))
                nc.scalar.copy(short(parts[b][:, 0, :, :]), ctxT[b][:, :, :]).then_inc(c.sem("ctx_hi_ready"), 1)

            def exps(b, g, t):
                act.wait_ge(c.sem("scores_ready"), g * 2 + (t + 1))
                act.wait_ge(c.sem("round_done"), g * 2 + (t + 1))
                nc.scalar.activation(probs[t][:, :, :], core.banks[:, 0:4, :], ACT.Exp).then_inc(
                    c.sem("probs_ready"), 1)

            def chunk(b, g, landed, attend, prepare):
                n = g + 1
                if prepare:
                    act.wait_ge(c.sem("keys_product"), n + 1)
                    wait_count(act, c.sem("sumsq_ready"), n)
                    nc.scalar.activation(square[:, :], ps[6], ACT.Square).then_inc(c.sem("keys_squared"), 1)
                if attend:
                    exps(b, g, 0)
                if prepare and splits(g):
                    ctx_hi(b, n + 1, (g - b) * 8 + 32)
                if attend:
                    exps(b, g, 1)
                if prepare:
                    act.wait_ge(c.sem("keys_normed"), n + 1)
                    nc.scalar.copy(short(key_parts[:, :, 0, :]), keys[:, :].rearrange(
                        "p (g f) -> p g f", f=32)).then_inc(c.sem("key_hi_ready"), 1)
                    act.wait_ge(c.sem("keysT_product"), n * 2 + 2)
                    nc.scalar.copy(short(keysT[1 - b][:, DC:8, :].rearrange("p c t -> p (c t)")), ps[7]).then_inc(
                        c.sem("keysT_tail_stored"), 1)

            act.sem_inc(c.sem("probs_ready"), 1)
            act.sem_inc(c.sem("round_done"), 2)
            ctx_hi(0, 0, 16)
            for k, u in enumerate(units):
                u.wait_landed(act)
                nc.scalar.copy(short(w[:, k, 0, :, :]), u.data).then_inc(c.sem("weight_hi_ready"), 1)
            over_groups(act, chunk, chunks)


def l3_xattn(core):
    ring, nc, ps, c = core.ring, core.nc, core.psum, core
    V = nc.vector
    with core.scratch(own_qT=[P, 8, 2, 2, P], outT=[P, 8, P], out=[P, D], inverse=[P, 8, 4]) as (
        own_qT, outT, out, inverse,
    ):
        with core.scratch(xn=[P, D], xnT=[P, DC, P], q=[P, D], square=[P, D], sums=[P, NARROW], twice=[P, 2 * D],
                          qT=[P, 8, P], own=[P, 2, 8, P]) as (xn, xnT, q, square, sums, twice, qT, own):
            norm_stage(core, core.x, xn[:, :], xnT[:, :, :], 1e-5)
            rows_stage(core, xnT, ring.take("L3_xattn_Wq"), lambda j, bank, link: V.tensor_copy(q[:, :], bank))
            chain_stage(core, head_norm_steps(core, q[:, :], NARROW, W16, 1e-6, square[:, :], sums[:, :]))
            pairs = twice[:, :].rearrange("p (g s f) -> p g s f", s=2, f=32)
            chain_stage(core, [("vector", lambda i=i: V.tensor_copy(pairs[:, :, i, :], q[:, :].rearrange(
                "p (g f) -> p g f", f=32))) for i in range(2)])
            transpose_stage(core, twice, qT, 8, scale=W16 ** -0.5)
            parity = core.table["head_parity"]
            steps = []
            for e in range(2):
                steps += [
                    ("vector", lambda e=e: V.tensor_scalar(own[:, e, :, :], qT[:, :, :], parity[:, e:e + 1], None,
                                                           ALU.mult)),
                    ("vector", lambda e=e: V.tensor_copy(short(own_qT[:, :, 0, e, :]), own[:, e, :, :])),
                    ("vector", lambda e=e: V.tensor_tensor(short(own_qT[:, :, 1, e, :]), own[:, e, :, :],
                                                           own_qT[:, :, 0, e, :], ALU.subtract)),
                ]
            chain_stage(core, steps)
        (wkeys,), (wvalues,) = ring.take("L3_xattn_Wkeys"), ring.take("L3_xattn_Wvalues")
        narrow_stage(core, own_qT, wkeys, wvalues)

        with core.stage() as block:

            @block.scalar
            def _(act):
                for i in range(2):
                    nc.scalar.copy(outT[:, 4 * i:4 * i + 4, :].rearrange("p n t -> p (n t)"), ps[4 + i]).then_inc(
                        c.sem("sums_copied"), 1)

            @block.tensor
            def _(pe):
                for n in range(8):
                    pe.wait_ge(c.sem("sums_copied"), n // 4 + 1)
                    nc.tensor.transpose(ps[n // 4][:, (n % 4) * P:(n % 4 + 1) * P], outT[:, n, :],
                                        core.ident).then_inc(c.sem("transposed"), 1)

            @block.vector
            def _(dve):
                link = Chain(dve, c.sem("dve_chain"))
                dve.wait_ge(c.sem("transposed"), 8)
                for t in range(4):
                    rows = ps[t // 2][:, (t % 2) * 2 * P:(t % 2 + 1) * 2 * P].rearrange(
                        "p (e j d) -> p e j d", e=2, j=4)
                    own = inverse[:, 2 * t:2 * t + 2, :]
                    link(V.reciprocal(own, rows[:, :, :, W16]))
                    link(V.tensor_tensor(
                        out[:, t * P:(t + 1) * P].rearrange("p (j e d) -> p e j d", j=4, e=2),
                        rows[:, :, :, 0:W16], own.unsqueeze(3).to_broadcast([P, 2, 4, W16]), ALU.mult))
                link(V.tensor_tensor(core.x, core.x, out[:, :], ALU.add))


def l3_attn(core):
    ring, nc, ps, c = core.ring, core.nc, core.psum, core
    V = nc.vector
    F = HEADS * P
    rest = core.operands[:, 0:HEADS]
    with core.scratch(xn=[P, D], xnT=[P, DC, P], qT=[P, HEADS, P], kT=[P, HEADS, P], v=[P, F],
                      oT=[P, HEADS, P]) as (xn, xnT, qT, kT, v, oT):
        norm_stage(core, core.x, xn[:, :], xnT[:, :, :], 1e-5, loads=[(rest, core.dram["L3_attn_betas"])])
        cols_stage(core, xnT, ring.take("L3_attn_Wq"), qT)
        cols_stage(core, xnT, ring.take("L3_attn_Wk"), kT)
        rows_stage(core, xnT, ring.take("L3_attn_Wv"), lambda j, bank, link: V.tensor_copy(
            v[:, j * D:(j + 1) * D], bank))
        chain_stage(core, [
            ("scalar", lambda: nc.scalar.activation(rest, rest, ACT.Sigmoid)),
            ("vector", lambda: V.tensor_scalar(rest, rest, -1.0, 1.0, ALU.mult, ALU.add)),
        ])

        def store(g, bank):
            for j in range(4):
                h = 4 * g + j
                last = nc.scalar.activation(oT[:, :, 8 * h:8 * h + 8], bank[:, j * P:(j + 1) * P].rearrange(
                    "p (m k) -> p k m", k=HEADS), ACT.Copy, scale=rest[:, h:h + 1])
            return last

        heads_stage(core, lambda h: qT[:, h, :], lambda h: kT[:, h, :], lambda h: v[:, h * P:(h + 1) * P],
                    core.table["causal"], P ** -0.5, store)
        down_stage(core, oT, ring.take("L3_attn_Wo"), add_to_x(core))


def l3_ffn(core):
    ring, nc, ps, c = core.ring, core.nc, core.psum, core
    V = nc.vector
    F, KV_HEADS, CHOSEN = HEADS * P, 8, P // 8
    ops = core.operands
    bq, bk, bv = ops[:, 0:F], ops[:, F:F + 1024], ops[:, F + 1024:F + 2048]
    ln1, ln2, router = (ops[:, F + 2048 + i * D:F + 2048 + (i + 1) * D] for i in range(3))
    cos, sin = core.table["cos3"], core.table["sin3"]
    with core.scratch(xn=[P, D], xnT=[P, DC, P], score=[P, 1], score_all=[P, P], row=[P, P], left=[P, P], top8=[P, 8],
                      chosen=[P, 1], gate=[P, 1], mask=[P, P], x1=[P, D], h2=[P, D], h2T=[P, DC, P]) as (
        xn, xnT, score, score_all, row, left, top8, chosen, gate, mask, x1, h2, h2T,
    ):
        norm_stage(core, core.x, xn[:, :], xnT[:, :, :], 1e-5,
                   loads=[(ops, core.dram["L3_ffn_rows"].partition_broadcast(P))])
        chain_stage(core, [
            ("vector", lambda: V.tensor_tensor(x1[:, :], xn[:, :], router, ALU.mult)),
            ("vector", lambda: V.tensor_reduce(score[:, :], x1[:, :], X, ALU.add)),
            ("scalar", lambda: nc.scalar.activation(gate[:, :], score[:, :], ACT.Sigmoid)),
            ("vector", lambda: V.tensor_copy(score_all[:, :], score[:, 0:1].to_broadcast([P, P]))),
        ])
        with core.stage() as block:

            @block.tensor
            def _(pe):
                nc.tensor.transpose(ps[0][:, 0:P], score_all[:, :], core.ident).then_inc(c.sem("row_ready"), 1)

            @block.vector
            def _(dve):
                link = Chain(dve, c.sem("dve_chain"))
                dve.wait_ge(c.sem("row_ready"), 1)
                link(V.tensor_copy(left[:, :], ps[0][:, 0:P]))
                for _ in range(CHOSEN // 8):
                    link(V.max(top8[:, :], left[:, :]))
                    link(V.match_replace(left[:, :], top8[:, :], left[:, :], TAKEN))
                link(V.tensor_scalar(row[:, :], left[:, :], TAKEN / 2, None, ALU.is_le))
                link(V.tensor_scalar(mask[:, :], row[:, :], 1.0, -NEG, ALU.subtract, ALU.mult))
                link(V.tensor_tensor(mask[:, :], mask[:, :], core.table["causal"], ALU.min))
                link(V.tensor_tensor(row[:, :], row[:, :], core.ident, ALU.mult))
                link(V.tensor_reduce(chosen[:, :], row[:, :], X, ALU.add))
                link(V.tensor_tensor(gate[:, :], gate[:, :], chosen[:, :], ALU.mult))

        with core.scratch(h=[P, D], hT=[P, DC, P], q=[P, F], k=[P, KV_HEADS * P], v=[P, KV_HEADS * P],
                          qT=[P, HEADS, P], kT=[P, KV_HEADS, P], turn=[P, 2 * F], oT=[P, HEADS, P]) as (
            h, hT, q, k, v, qT, kT, turn, oT,
        ):
            norm_stage(core, xn[:, :], h[:, :], hT[:, :, :], 1e-6, rms=True, gain=ln1)
            rows_stage(core, hT, ring.take("L3_ffn_wq"), lambda j, bank, link: V.tensor_tensor(
                q[:, j * D:(j + 1) * D], bank, bq[:, j * D:(j + 1) * D], ALU.add))
            rows_stage(core, hT, ring.take("L3_ffn_wk") + ring.take("L3_ffn_wv"), lambda j, bank, link: V.tensor_tensor(
                (k, k, v, v)[j][:, (j % 2) * D:(j % 2 + 1) * D], bank,
                (bk, bk, bv, bv)[j][:, (j % 2) * D:(j % 2 + 1) * D], ALU.add))
            steps = []
            for rows, heads in ((q, HEADS), (k, KV_HEADS)):
                half = rows[:, :].rearrange("p (h two i) -> p h two i", h=heads, two=2)
                n = heads * P // 2
                t = [turn[:, i * n:(i + 1) * n].rearrange("p (h i) -> p h i", h=heads) for i in range(4)]
                wide = [a.unsqueeze(1).to_broadcast([P, heads, P // 2]) for a in (cos, sin)]
                steps += rotation_steps(core, half[:, :, 0, :], half[:, :, 1, :], *wide, t)
            chain_stage(core, steps)
            transpose_stage(core, q, qT, HEADS)
            transpose_stage(core, k, kT, KV_HEADS)
            heads_stage(core, lambda i: qT[:, i, :], lambda i: kT[:, i // 2, :],
                        lambda i: v[:, (i // 2) * P:(i // 2 + 1) * P], mask[:, :], P ** -0.5,
                        lambda g, bank: nc.scalar.copy(oT[:, 4 * g:4 * g + 4, :].rearrange("p h t -> p (h t)"), bank))
            down_stage(core, oT, ring.take("L3_ffn_wo"),
                       lambda bank, link: link(V.tensor_tensor(x1[:, :], xn[:, :], bank, ALU.add)))
        norm_stage(core, x1[:, :], h2[:, :], h2T[:, :, :], 1e-6, rms=True, gain=ln2)
        with core.scratch(up=[P, F], upT=[P, HEADS, P]) as (up, upT):
            rows_stage(core, h2T, ring.take("L3_ffn_w_gate"), lambda j, bank, link: nc.scalar.activation(
                up[:, j * D:(j + 1) * D], bank, ACT.Silu), on_scalar=True)
            rows_stage(core, h2T, ring.take("L3_ffn_w_up"), lambda j, bank, link: V.tensor_tensor(
                up[:, j * D:(j + 1) * D], up[:, j * D:(j + 1) * D], bank, ALU.mult))
            transpose_stage(core, up, upT, HEADS)

            def finish(bank, link):
                link(V.tensor_tensor(x1[:, :], x1[:, :], bank, ALU.add))
                link(V.tensor_tensor(x1[:, :], x1[:, :], xn[:, :], ALU.subtract))
                link(V.scalar_tensor_tensor(out=x1[:, :], in0=x1[:, :], scalar=gate[:, 0:1], in1=xn[:, :],
                                            op0=ALU.mult, op1=ALU.add))
                link(V.tensor_tensor(core.x, core.x, x1[:, :], ALU.add))

            down_stage(core, upT, ring.take("L3_ffn_w_down"), finish)


BLOCKS = [(l0_xattn, 16), (l0_attn, DC * 400), (l0_ffn, DC * 16 + 16), (l1_xattn, 16), (l1_attn, 6 * D),
          (l1_ffn, 960), (l2_xattn, 2 * D + 2 * P), (l2_attn, 4 * D), (l2_ffn, 16), (l3_xattn, 16), (l3_attn, HEADS),
          (l3_ffn, 4096 + 3 * D)]


def build(nc, dram, first=0, last=12):
    with ExitStack() as ctx:
        core = Core(nc, ctx, dram)
        core.banks = ctx.enter_context(nc.psum_tensor("banks", [P, 8, D], F32))
        core.psum = [core.banks[:, i, :] for i in range(8)]
        starts = ["L0_xattn_wq", "L0_attn_wq_idx", "L0_ffn_W1", None, "L1_attn_W_in", "L1_ffn_base_W",
                  "L2_xattn_Wq", "L2_attn_wq", "L2_ffn_W1", "L3_xattn_Wq", "L3_attn_Wq", "L3_ffn_wq"]
        names = [name for name, n in UNITS for _ in range(n)]
        s = starts[first] or starts[first + 1]
        core.ring = WeightRing(core, dram["weights"], names.index(s))
        x = core.sbuf("x", [P, D])
        zeros = core.sbuf("zeros", [P, D])
        ones = core.sbuf("ones", [P, P])
        half = core.sbuf("minus_half", [P, 32])
        tables = core.sbuf("tables", [P, TABLES])
        core.x, core.zeros, core.ones, core.minus_half = x[:, :], zeros, ones[:, :], half
        core.table = {name: tables[:, a:b] for name, (a, b) in TABLE_AT.items()}
        core.ident = core.table["identity"]

        with core.stage() as block:

            @block.sync
            def _(sp):
                sp.dma_start(x[:, :], dram["x"]).then_inc(core.sem("x_landed"), 16)
                sp.dma_start(tables[:, :], dram["tables"]).then_inc(core.sem("x_landed"), 16)
                for n in range(min(RING, core.ring.total)):
                    core.ring.load(sp, n)
                sp.wait_ge(core.sem("x_landed"), 32)

            @block.vector
            def _(dve):
                nc.vector.memset(zeros[:, :], 0.0)
                nc.vector.memset(ones[:, :], 1.0)
                nc.vector.memset(half[:, :], -0.5)

        for block_of_layer, words in BLOCKS[first:last]:
            with core.scratch(operands=[P, words]) as (operands,):
                core.operands = operands[:, :]
                block_of_layer(core)

        with core.stage() as block:

            @block.sync
            def _(sp):
                sp.dma_start(dram["out"], x[:, :]).then_inc(core.sem("out_stored"), 16)
                sp.wait_ge(core.sem("out_stored"), 16)




def rotation_tables(width, half_first):
    inverse = (1.0 / 10000.0 ** (np.arange(0, width, 2, dtype=np.float32) / np.float32(width))).astype(np.float32)
    angle = (np.arange(P, dtype=np.float32)[:, None] * inverse[None, :]).astype(np.float32)
    return np.cos(angle), np.sin(angle)


def constant_tables():
    hadamard = np.array([[1.0]])
    while len(hadamard) < P:
        hadamard = np.block([[hadamard, hadamard], [hadamard, -hadamard]])
    p = np.arange(P)
    cos1, sin1 = rotation_tables(256, False)
    cos3, sin3 = rotation_tables(P, True)
    return {
        "identity": np.eye(P),
        "hadamard": hadamard,
        "causal": np.where(p[:, None] >= p[None, :], 0.0, NEG),
        "head_parity": np.stack([(p // 16) % 2 == 0, (p // 16) % 2 == 1], 1),
        "cos1": cos1, "sin1": sin1, "cos3": cos3, "sin3": sin3,
    }


TABLE_AT, TABLES = {}, 0
for _name, _t in constant_tables().items():
    TABLE_AT[_name] = (TABLES, TABLES + _t.shape[1])
    TABLES += _t.shape[1]


def unit_rows(w):
    n = w.shape[1] // D
    return w.reshape(DC, P, n, D).transpose(2, 1, 0, 3).reshape(n, P, DC * D)


def unit_down(w):
    n = w.shape[0] // D
    return w.reshape(n, DC, P, D).transpose(0, 2, 1, 3).reshape(n, P, DC * D)


def small_columns(*ws):
    w = np.concatenate(ws, 1)
    return w.reshape(DC, P, -1).transpose(1, 0, 2).reshape(P, -1)


def small_operands(a):
    return {
        "L0_attn_small": small_columns(a["L0_attn_wk_idx"], a["L0_attn_wk"], a["L0_attn_wv"], a["L0_attn_w_iw"]),
        "L0_ffn_small": small_columns(a["L0_ffn_Wr"].T),
        "L0_ffn_rows": a["L0_ffn_br"],
        "L1_attn_rows": np.concatenate([a["L1_attn_" + n] for n in ("b_in", "b_out", "gamma", "beta")]),
        "L1_ffn_small": small_columns(a["L1_ffn_router_W"].T, a["L1_ffn_A"].T),
        "L2_xattn_rows": np.concatenate([a["L2_xattn_" + n] for n in ("bk", "bv", "qn_w", "kn_w", "bq")]),
        "L2_attn_rows": np.concatenate([a["L2_attn_" + n] for n in ("bq", "bk", "bv", "bo")]),
        "L3_attn_betas": np.ascontiguousarray(a["L3_attn_betas"].reshape(HEADS, P).T),
        "L3_ffn_rows": np.concatenate([a["L3_ffn_" + n] for n in ("bq", "bk", "bv", "ln1_w", "ln2_w", "w_router")]),
        "L1_ffn_BT": np.ascontiguousarray(a["L1_ffn_B"].T),
        "L1_ffn_rows": a["L1_ffn_biases"],
    }


def layout(a):
    kv = np.concatenate([a["L3_xattn_Wk"], a["L3_xattn_Wv"]], 0)
    w = {n: a[n].T for n in ("L0_xattn_wq", "L0_xattn_wk", "L0_xattn_wv", "L0_xattn_wo", "L0_ffn_W1", "L0_ffn_W2",
                             "L1_ffn_base_W", "L2_attn_wq", "L2_attn_wk", "L2_attn_wv", "L2_attn_wo", "L2_ffn_W1",
                             "L2_ffn_W3", "L2_ffn_W2", "L3_xattn_Wq")}
    w["L3_xattn_Wkeys"], w["L3_xattn_Wvalues"] = kv[0::2].T, kv[1::2].T
    parts = []
    for name, n in UNITS:
        m = w[name] if name in w else a[name]
        parts.append(unit_rows(m) if m.shape[0] == D else unit_down(m))
        assert len(parts[-1]) == n
    ctx = a["ctx_2048"][0]
    return {
        "weights": np.ascontiguousarray(np.concatenate(parts, 0)),
        "x": a["x"][0],
        "ctxT": np.ascontiguousarray(ctx.reshape(GROUPS, GROUP, DC, P).transpose(0, 3, 2, 1)),
        "ctxT_chunks": np.ascontiguousarray(ctx.reshape(KV // P, P, DC, P).transpose(0, 3, 2, 1)),
        "ctx_rows": np.ascontiguousarray(ctx.reshape(GROUPS, PER, P, D).transpose(0, 2, 1, 3)),
        "tables": np.concatenate(list(constant_tables().values()), 1).astype(np.float32),
        **small_operands(a),
        "score_mask": np.ascontiguousarray(a["mask_1xSxS2_ff0"][0].reshape(P, GROUPS, GROUP).transpose(1, 0, 2)),
        "memory_mask": a["mask_BxS2_bk0"].reshape(KV),
    }


def kernel(**inputs):
    import concourse.bacc as bacc
    from concourse.bass_utils import run_bass_kernel_spmd

    a = {k: np.ascontiguousarray(v) for k, v in inputs.items()}
    arrays = layout(a)
    nc = bacc.Bacc("TRN2", target_bir_lowering=False, num_devices=1)
    dram = {n: nc.dram_tensor(f"in_{n}", v.shape, mybir.dt.from_np(v.dtype), kind="ExternalInput").ap()
            for n, v in arrays.items()}
    dram["out"] = nc.dram_tensor("out_x", (P, D), F32, kind="ExternalOutput").ap()
    build(nc, dram)
    got = run_bass_kernel_spmd(nc, [{f"in_{n}": v for n, v in arrays.items()}], core_ids=[0])
    return np.asarray(got.results[0]["out_x"]).reshape(1, P, D)
```

```python
from contextlib import ExitStack, contextmanager

import concourse.bass as bass
import numpy as np
from concourse import mybir

F32 = mybir.dt.float32
F32R = mybir.dt.float32r
U8 = mybir.dt.uint8
ALU = mybir.AluOpType
ACT = mybir.ActivationFunctionType
X = mybir.AxisListType.X

P = 128
D = 512
DC = D // P
KV = 12544
CHUNK = P
PER = 7
GROUP = PER * CHUNK
GROUPS = KV // GROUP
TILE = GROUP // 2
HEADS = 16
NEG = -1e30
RING = 6
TAKEN = -3e38

UNITS = (
    [("L0_xattn_wq", 1), ("L0_xattn_wk", 1), ("L0_xattn_wv", 1), ("L0_xattn_wo", 1)]
    + [("L0_attn_wq_idx", 4), ("L0_attn_wq", 4), ("L0_attn_wo", 4)]
    + [("L0_ffn_W1", 4), ("L0_ffn_W2", 4)]
    + [("L1_attn_W_in", 3), ("L1_attn_W_out", 1)]
    + [("L1_ffn_base_W", 1)]
    + [("L2_xattn_Wq", 4), ("L2_xattn_Wk", 1), ("L2_xattn_Wv", 1), ("L2_xattn_Wo", 4)]
    + [("L2_attn_wq", 1), ("L2_attn_wk", 1), ("L2_attn_wv", 1), ("L2_attn_wo", 1)]
    + [("L2_ffn_W1", 4), ("L2_ffn_W3", 4), ("L2_ffn_W2", 4)]
    + [("L3_xattn_Wq", 1), ("L3_xattn_Wkeys", 1), ("L3_xattn_Wvalues", 1)]
    + [("L3_attn_Wq", 4), ("L3_attn_Wk", 4), ("L3_attn_Wv", 4), ("L3_attn_Wo", 4)]
    + [("L3_ffn_wq", 4), ("L3_ffn_wk", 2), ("L3_ffn_wv", 2), ("L3_ffn_wo", 4)]
    + [("L3_ffn_w_gate", 4), ("L3_ffn_w_up", 4), ("L3_ffn_w_down", 4)]
)


class Chain:

    def __init__(self, engine, sem):
        self.engine, self.sem, self.count = engine, sem, 0

    def __call__(self, instruction):
        self.count += 1
        instruction.then_inc(self.sem, 1)
        self.engine.wait_ge(self.sem, self.count)


def wait_count(engine, sem, count):
    if not (isinstance(count, int) and count == 0):
        engine.wait_ge(sem, count)


def short(ap):
    return ap.bitcast(F32R)


def matmul_parts(nc, out, stationary, moving, start, stop):
    (sh, sl), (mh, ml) = stationary, moving
    nc.tensor.matmul(out, short(sh), short(mh), start=start, stop=False)
    nc.tensor.matmul(out, short(sh), short(ml), start=False, stop=False)
    return nc.tensor.matmul(out, short(sl), short(mh), start=False, stop=stop)


class Unit:

    def __init__(self, ring, number):
        self.ring, self.number, self.slot = ring, number, number % RING
        self.data = ring.slots[:, self.slot]

    def wait_landed(self, pe):
        pe.wait_ge(self.ring.landed[self.slot], 16 * (self.number // RING + 1))

    def done(self, last_matmul):
        last_matmul.then_inc(self.ring.done, 1)

    def wait_done(self, engine):
        engine.wait_ge(self.ring.done, self.number + 1)

    def refill(self, sp):
        if self.number + RING < self.ring.total:
            self.wait_done(sp)
            self.ring.load(sp, self.number + RING)


class WeightRing:

    def __init__(self, core, dram):
        self.names = [name for name, n in UNITS for _ in range(n)]
        self.total = len(self.names)
        self.dram = [dram[u].rearrange("p (c n) -> p c n", c=DC) for u in range(self.total)]
        self.slots = core.sbuf("weight_ring", [P, RING, DC, D], F32)
        self.landed = [core.nc.alloc_semaphore(f"weights_landed_{i}") for i in range(RING)]
        self.done = core.nc.alloc_semaphore("weight_units_done")
        self.next = 0

    def load(self, sp, n):
        sp.dma_start(self.slots[:, n % RING], self.dram[n]).then_inc(self.landed[n % RING], 16)

    def take(self, name):
        count = dict(UNITS)[name]
        assert self.names[self.next] == name and self.names[self.next + count - 1] == name
        units = [Unit(self, self.next + i) for i in range(count)]
        self.next += count
        return units


class Core:
    def __init__(self, nc, ctx, dram):
        self.nc, self.ctx, self.dram = nc, ctx, dram
        self.sems, self.serial = {}, 0

    def sbuf(self, name, shape, dt=F32):
        return self.ctx.enter_context(self.nc.sbuf_tensor(name, shape, dt))

    def sem(self, name):
        if name not in self.sems:
            self.sems[name] = self.nc.alloc_semaphore(name)
        return self.sems[name]

    @contextmanager
    def stage(self):
        with self.nc.Block() as block:
            yield block
        if self.sems:
            numbers = sorted(s.num for s in self.sems.values())
            assert numbers[-1] - numbers[0] + 1 == len(numbers)
            self.nc.gpsimd.sem_clear(range(numbers[0], numbers[-1] + 1))
            self.nc.all_engine_barrier()

    @contextmanager
    def scratch(self, **shapes):
        with ExitStack() as stack:
            self.serial += 1
            yield [stack.enter_context(self.nc.sbuf_tensor(f"{k}_{self.serial}", v, F32)) for k, v in shapes.items()]




def norm_stage(core, src, dst, dstT, eps, rms=False, gain=None, shift=None, loads=(), scale=1.0):
    nc, ps, c = core.nc, core.psum, core
    with core.scratch(stats=[P, 6], moments=[P, 2], spread=[P, 1], rstd=[P, 1], square=[P, D]) as (
        stats, moments, spread, rstd, square,
    ), core.stage() as block:

        @block.sync
        def _(sp):
            for to, frm in loads:
                sp.dma_start(to, frm).then_inc(c.sem("operands_landed"), 16)
            if loads:
                sp.wait_ge(c.sem("operands_landed"), 16 * len(loads))

        @block.vector
        def _(dve):
            link = Chain(dve, c.sem("dve_chain"))
            if rms:
                link(nc.vector.tensor_tensor(square[:, :], src, src, ALU.mult))
                link(nc.vector.tensor_reduce(moments[:, 1:2], square[:, :], X, ALU.add))
                nc.vector.tensor_scalar(spread[:, :], moments[:, 1:2], 1.0 / D, eps, ALU.mult, ALU.add).then_inc(
                    c.sem("variance_ready"), 1)
            else:
                link(nc.vector.bn_stats(stats[:, :], src))
                link(nc.vector.bn_aggr(moments[:, :], stats[:, :]))
                nc.vector.tensor_scalar(spread[:, :], moments[:, 1:2], eps, None, ALU.add).then_inc(
                    c.sem("variance_ready"), 1)
            dve.wait_ge(c.sem("rstd_ready"), 1)
            if rms:
                steps = [lambda: nc.vector.tensor_scalar(dst, src, rstd[:, 0:1], None, ALU.mult)]
            else:
                steps = [lambda: nc.vector.tensor_scalar(dst, src, moments[:, 0:1], rstd[:, 0:1],
                                                         ALU.subtract, ALU.mult)]
            if loads:
                dve.wait_ge(c.sem("operands_landed"), 16 * len(loads))
            if gain is not None:
                steps.append(lambda: nc.vector.tensor_tensor(dst, dst, gain, ALU.mult))
            if shift is not None:
                steps.append(lambda: nc.vector.tensor_tensor(dst, dst, shift, ALU.add))
            for step in steps[:-1]:
                link(step())
            steps[-1]().then_inc(c.sem("normed"), 1)

        @block.gpsimd
        def _(pool):
            pool.wait_ge(c.sem("variance_ready"), 1)
            nc.gpsimd.tensor_tensor(rstd[:, :], spread[:, :], core.minus_half[:, 0:1], ALU.pow).then_inc(
                c.sem("rstd_ready"), 1)

        @block.tensor
        def _(pe):
            pe.wait_ge(c.sem("normed"), 1)
            for i in range(DC):
                last = nc.tensor.transpose(ps[0][:, i * P:(i + 1) * P], dst[:, i * P:(i + 1) * P], core.ident)
            last.then_inc(c.sem("transposed"), 1)

        @block.scalar
        def _(act):
            act.wait_ge(c.sem("transposed"), 1)
            nc.scalar.activation(dstT.rearrange("p c t -> p (c t)"), ps[0][:, :], ACT.Copy, scale=scale)


def transpose_stage(core, rows, cols, n, scale=1.0):
    nc, ps, c = core.nc, core.psum, core
    banks = (n + 3) // 4
    with core.stage() as block:

        @block.tensor
        def _(pe):
            for b in range(banks):
                if b >= 4:
                    pe.wait_ge(c.sem("copied"), b - 3)
                for i in range(4 * b, min(4 * b + 4, n)):
                    last = nc.tensor.transpose(ps[b % 4][:, (i % 4) * P:(i % 4 + 1) * P],
                                               rows[:, i * P:(i + 1) * P], core.ident)
                last.then_inc(c.sem("transposed"), 1)

        @block.scalar
        def _(act):
            for b in range(banks):
                k = min(4, n - 4 * b)
                act.wait_ge(c.sem("transposed"), b + 1)
                nc.scalar.activation(cols[:, 4 * b:4 * b + k, :].rearrange("p c t -> p (c t)"),
                                     ps[b % 4][:, 0:k * P], ACT.Copy, scale=scale).then_inc(c.sem("copied"), 1)


def rows_stage(core, aT, units, evacuate, on_scalar=False, after=None):
    nc, ps, c = core.nc, core.psum, core
    with core.stage() as block:

        @block.sync
        def _(sp):
            for u in units:
                u.refill(sp)

        @block.tensor
        def _(pe):
            for j, u in enumerate(units):
                u.wait_landed(pe)
                if j >= 4:
                    pe.wait_ge(c.sem("bank_evacuated"), j - 3)
                for i in range(DC):
                    last = nc.tensor.matmul(ps[j % 4][:, :], aT[:, i, :], u.data[:, i, :],
                                            start=(i == 0), stop=(i == DC - 1))
                u.done(last)

        def evacuate_all(engine, link):
            for j, u in enumerate(units):
                u.wait_done(engine)
                evacuate(j, ps[j % 4][:, :], link).then_inc(c.sem("bank_evacuated"), 1)

        if on_scalar:

            @block.scalar
            def _(act):
                evacuate_all(act, None)

        @block.vector
        def _(dve):
            link = Chain(dve, c.sem("dve_chain"))
            if not on_scalar:
                evacuate_all(dve, link)
            if after is not None:
                dve.wait_ge(c.sem("bank_evacuated"), len(units))
                after(link)


def cols_stage(core, aT, units, outT, scale=1.0):
    nc, ps, c = core.nc, core.psum, core
    with core.stage() as block:

        @block.sync
        def _(sp):
            for u in units:
                u.refill(sp)

        @block.tensor
        def _(pe):
            for j, u in enumerate(units):
                u.wait_landed(pe)
                if j >= 4:
                    pe.wait_ge(c.sem("bank_evacuated"), j - 3)
                for o in range(DC):
                    for i in range(DC):
                        last = nc.tensor.matmul(ps[j % 4][:, o * P:(o + 1) * P], u.data[:, i, o * P:(o + 1) * P],
                                                aT[:, i, :], start=(i == 0), stop=(i == DC - 1))
                u.done(last)

        @block.scalar
        def _(act):
            for j, u in enumerate(units):
                u.wait_done(act)
                nc.scalar.activation(outT[:, 4 * j:4 * j + 4, :].rearrange("p c t -> p (c t)"), ps[j % 4][:, :],
                                     ACT.Copy, scale=scale).then_inc(c.sem("bank_evacuated"), 1)


def down_stage(core, hT, units, evacuate):
    nc, ps, c = core.nc, core.psum, core
    with core.stage() as block:

        @block.sync
        def _(sp):
            for u in units:
                u.refill(sp)

        @block.tensor
        def _(pe):
            n = len(units) * DC
            for j, u in enumerate(units):
                u.wait_landed(pe)
                for i in range(DC):
                    k = j * DC + i
                    last = nc.tensor.matmul(ps[0][:, :], hT[:, k, :], u.data[:, i, :], start=(k == 0),
                                            stop=(k == n - 1))
                u.done(last)

        @block.vector
        def _(dve):
            units[-1].wait_done(dve)
            evacuate(ps[0][:, :], Chain(dve, c.sem("dve_chain")))


def heads_stage(core, q, k, v, mask, scale, out, value_rows=P):
    nc, ps, c = core.nc, core.psum, core
    G = HEADS // 4
    with core.scratch(scores=[P, G, 4, P], probsT=[P, 2, 4, P], neg_max=[P, HEADS], total=[P, HEADS],
                      inverse=[P, HEADS]) as (scores, probsT, neg_max, total, inverse), core.stage() as block:

        @block.tensor
        def _(pe):
            def transpose(g):
                pe.wait_ge(c.sem("probs_ready"), g + 1)
                if g >= 2:
                    pe.wait_ge(c.sem("probsT_ready"), g - 1)
                for j in range(4):
                    last = nc.tensor.transpose(ps[4 + g % 2][:, j * P:(j + 1) * P], scores[:, g, j, :], core.ident)
                last.then_inc(c.sem("probs_transposed"), 1)

            def weigh(g):
                pe.wait_ge(c.sem("probsT_ready"), g + 1)
                if g >= 2:
                    pe.wait_ge(c.sem("out_stored"), g - 1)
                for j in range(4):
                    if value_rows == P:
                        to = ps[6 + g % 2][:, j * P:(j + 1) * P]
                    else:
                        to = ps[6 + g % 2][j * value_rows:(j + 1) * value_rows, 0:P]
                    last = nc.tensor.matmul(to, v(4 * g + j), probsT[:, g % 2, j, :], start=True, stop=True)
                last.then_inc(c.sem("out_ready"), 1)

            for g in range(G):
                for j in range(4):
                    last = nc.tensor.matmul(ps[g][:, j * P:(j + 1) * P], q(4 * g + j), k(4 * g + j),
                                            start=True, stop=True)
                last.then_inc(c.sem("scores_ready"), 1)
            transpose(0)
            for g in range(G):
                if g + 1 < G:
                    transpose(g + 1)
                weigh(g)

        @block.vector
        def _(dve):
            link = Chain(dve, c.sem("dve_chain"))

            def add_mask(g):
                dve.wait_ge(c.sem("scores_ready"), g + 1)
                link(nc.vector.scalar_tensor_tensor(
                    out=scores[:, g, :, :], in0=ps[g][:, :].rearrange("p (j t) -> p j t", j=4), scalar=scale,
                    in1=mask.unsqueeze(1).to_broadcast([P, 4, P]), op0=ALU.mult, op1=ALU.add))
                nc.vector.tensor_reduce(neg_max[:, 4 * g:4 * g + 4], scores[:, g, :, :], X, ALU.max,
                                        negate=True).then_inc(c.sem("scores_masked"), 1)

            def normalise(g):
                dve.wait_ge(c.sem("exp_ready"), 4 * g + 4)
                link(nc.vector.reciprocal(inverse[:, 4 * g:4 * g + 4], total[:, 4 * g:4 * g + 4]))
                nc.vector.tensor_tensor(scores[:, g, :, :], scores[:, g, :, :],
                                        inverse[:, 4 * g:4 * g + 4].unsqueeze(2).to_broadcast([P, 4, P]),
                                        ALU.mult).then_inc(c.sem("probs_ready"), 1)

            add_mask(0)
            add_mask(1)
            for g in range(G):
                normalise(g)
                if g + 2 < G:
                    add_mask(g + 2)

        @block.scalar
        def _(act):
            def exps(g):
                act.wait_ge(c.sem("scores_masked"), g + 1)
                for h in range(4 * g, 4 * g + 4):
                    nc.scalar.activation(scores[:, g, h % 4, :], scores[:, g, h % 4, :], ACT.Exp,
                                         bias=neg_max[:, h:h + 1], accum_out=total[:, h:h + 1]).then_inc(
                        c.sem("exp_ready"), 1)

            def copy_probsT(g):
                act.wait_ge(c.sem("probs_transposed"), g + 1)
                if g >= 2:
                    act.wait_ge(c.sem("out_ready"), g - 1)
                nc.scalar.copy(probsT[:, g % 2, :, :].rearrange("p j t -> p (j t)"), ps[4 + g % 2][:, :]).then_inc(
                    c.sem("probsT_ready"), 1)

            def store(g):
                act.wait_ge(c.sem("out_ready"), g + 1)
                out(g, ps[6 + g % 2]).then_inc(c.sem("out_stored"), 1)

            exps(0)
            exps(1)
            for g in range(G):
                copy_probsT(g)
                if g + 2 < G:
                    exps(g + 2)
                if g > 0:
                    store(g - 1)
            store(G - 1)




def over_steps(engine, step):
    step(1, -1, False, True, False)
    step(0, 0, True, True, False)
    with engine.Fori(0, GROUPS // 2 - 1) as i:
        for n in range(2):
            step(1 - n, i * 2 + (n + 1), True, True, True)
    step(1, GROUPS - 1, True, False, True)


GPSIMD_ROWS = 3


def wide_stage(core, qT, out, own_kT=None, own_v=None, seen=None):
    nc, ps, c = core.nc, core.psum, core
    pieces = ((0, 3), (3, 5), (5, PER))
    with core.scratch(rows0=[P, PER, D], rows1=[P, PER, D], row_parts=[P, 2, PER, D], col_parts=[P, 2, DC, GROUP],
                      q_parts=[P, 2, DC, P], probs=[P, 2, TILE], probT_parts=[P, 2, PER * P], seen_scores=[P, 2, TILE],
                      unseen=[P, 2, TILE], acc=[P, D], own_p=[P, P], own_pT=[P, P], top=[P, 1], neg0=[P, 1],
                      neg1=[P, 1], decay0=[P, 1], decay1=[P, 1], part0=[P, 1], part1=[P, 1], total=[P, 1]) as (
        rows0, rows1, row_parts, col_parts, q_parts, probs, probT_parts, seen_scores, unseen, acc, own_p, own_pT,
        top, neg0, neg1, decay0, decay1, part0, part1, total,
    ), core.stage() as block:
        rows, neg, decay, part = [rows0, rows1], [neg0, neg1], [decay0, decay1], [part0, part1]
        scores = core.banks[:, 0:2, 0:TILE]
        probsT = core.banks[:, 5:7, :].rearrange("p b n -> p (b n)")[:, 0:GROUP]

        def columns_bank(b, k):
            return ps[2 + (b + k) % 2]

        def seen_of(g):
            return seen[:, bass.ds(g * GROUP, GROUP)].rearrange("p (a n) -> p a n", a=2)

        def row_lo(engine, ops, signal, b, g, k):
            engine.wait_ge(c.sem("row_hi_ready"), g * PER + (k + 1))
            ops.tensor_tensor(short(row_parts[:, 1, k, :]), rows[b][:, k, :], row_parts[:, 0, k, :],
                              ALU.subtract).then_inc(c.sem(signal), 1)

        def wait_row_lo(engine, g, k):
            if k < GPSIMD_ROWS:
                engine.wait_ge(c.sem("gpsimd_rows_ready"), g * GPSIMD_ROWS + (k + 1))
            else:
                engine.wait_ge(c.sem("vector_rows_ready"), g * (PER - GPSIMD_ROWS) + (k - GPSIMD_ROWS + 1))

        @block.sync
        def _(sp):
            for b in range(2):
                for p, (k0, k1) in enumerate(pieces):
                    sp.dma_start(rows[b][:, k0:k1, :], core.dram["ctx_rows"][b, :, k0:k1, :]).then_inc(
                        c.sem(f"rows_landed_{b}_{p}"), 16)
            with sp.Fori(0, GROUPS // 2 - 1) as i:
                for b in range(2):
                    for p, (k0, k1) in enumerate(pieces):
                        wait_row_lo(sp, i * 2 + b, k1 - 1)
                        sp.dma_start(rows[b][:, k0:k1, :], core.dram["ctx_rows"][
                            bass.ds(i * 2 + (2 + b), 1), :, k0:k1, :].rearrange("a p k d -> (a p) k d")).then_inc(
                            c.sem(f"rows_landed_{b}_{p}"), 16)

        @block.tensor
        def _(pe):
            def columns(b, n, k):
                for p, (k0, k1) in enumerate(pieces):
                    if k == k0:
                        pe.wait_ge(c.sem(f"rows_landed_{b}_{p}"), (n - b) * 8 + 16)
                if not (isinstance(n, int) and n * PER + k < 2):
                    pe.wait_ge(c.sem("col_lo_ready"), n * PER + (k - 1))
                for i in range(DC):
                    last = nc.tensor.transpose(columns_bank(b, k)[:, i * P:(i + 1) * P],
                                               rows[b][:, k, i * P:(i + 1) * P], core.ident)
                last.then_inc(c.sem("columns_ready"), 1)

            def weigh_chunk(m, k):
                if k == 0:
                    pe.wait_ge(c.sem("probT_lo_ready"), m + 1)
                    pe.wait_ge(c.sem("out_added"), m + 1)
                wait_row_lo(pe, m, k)
                matmul_parts(nc, ps[4], [probT_parts[:, s, k * P:(k + 1) * P] for s in range(2)],
                             [row_parts[:, s, k, :] for s in range(2)], k == 0, k == PER - 1).then_inc(
                    c.sem("chunk_weighed"), 1)

            def step(b, g, attend, prepare, weigh):
                if attend:
                    pe.wait_ge(c.sem("col_lo_ready"), g * PER + PER)
                    for t in range(2):
                        for i in range(DC):
                            last = matmul_parts(nc, ps[t][:, 0:TILE], [q_parts[:, s, i, :] for s in range(2)],
                                                [col_parts[:, s, i, t * TILE:(t + 1) * TILE] for s in range(2)],
                                                i == 0, i == DC - 1)
                    last.then_inc(c.sem("scores_ready"), 1)
                for k in range(PER):
                    if prepare:
                        columns(1 - b, g + 1, k)
                    if weigh:
                        weigh_chunk(g - 1, k)
                if attend:
                    pe.wait_ge(c.sem("probs_ready"), g + 1)
                    flat = probs[:, :, :].rearrange("p a n -> p (a n)")
                    for k in range(PER):
                        last = nc.tensor.transpose(ps[5 + k // 4][:, (k % 4) * P:(k % 4 + 1) * P],
                                                   flat[:, k * P:(k + 1) * P], core.ident)
                    last.then_inc(c.sem("probs_transposed"), 1)

            if own_kT is not None:
                for i in range(DC):
                    last = nc.tensor.matmul(ps[7][:, 0:P], qT[:, i, :], own_kT[:, i, :], start=(i == 0),
                                            stop=(i == DC - 1))
                last.then_inc(c.sem("own_step"), 1)
                pe.wait_ge(c.sem("own_probs_ready"), 1)
                nc.tensor.transpose(ps[7][:, P:2 * P], own_p[:, :], core.ident).then_inc(c.sem("own_step"), 1)
                pe.wait_ge(c.sem("own_probsT_ready"), 1)
                nc.tensor.matmul(ps[4], own_pT[:, :], own_v, start=True, stop=True).then_inc(c.sem("own_step"), 1)
                pe.wait_ge(c.sem("out_added"), 1)
            pe.wait_ge(c.sem("q_lo_ready"), 1)
            over_steps(pe, step)
            for k in range(PER):
                weigh_chunk(GROUPS - 1, k)

        @block.gpsimd
        def _(pool):
            with pool.Fori(0, GROUPS // 2) as i:
                for b in range(2):
                    for k in range(GPSIMD_ROWS):
                        row_lo(pool, nc.gpsimd, "gpsimd_rows_ready", b, i * 2 + b, k)

        @block.vector
        def _(dve):
            link = Chain(dve, c.sem("dve_chain"))

            def maximum(b, g):
                dve.wait_ge(c.sem("scores_ready"), g + 1)
                if seen is None:
                    nc.vector.tensor_reduce(top[:, :], scores, mybir.AxisListType.XY, ALU.max).then_inc(
                        c.sem("topped"), 1)
                else:
                    nc.vector.tensor_tensor(seen_scores[:, :, :], scores, seen_of(g), ALU.mult).then_inc(
                        c.sem("seen_scored"), 1)
                    dve.wait_ge(c.sem("unseen_ready"), g + 1)
                    dve.wait_ge(c.sem("seen_scored"), g + 1)
                    dve.wait_ge(c.sem("probs_transposed"), g + 1)
                    dve.sem_inc(c.sem("masking_started"), 1)
                    nc.vector.tensor_tensor_reduce(out=probs[:, :, :], in0=seen_scores[:, :, :], in1=unseen[:, :, :],
                                                   scale=1.0, scalar=-3e38, op0=ALU.add, op1=ALU.max,
                                                   accum_out=top[:, :]).then_inc(c.sem("topped"), 1)
                dve.wait_ge(c.sem("topped"), g + 2)
                nc.vector.scalar_tensor_tensor(out=neg[b][:, :], in0=top[:, :], scalar=-1.0, in1=neg[1 - b][:, :],
                                               op0=ALU.mult, op1=ALU.min).then_inc(c.sem("max_ready"), 1)

            def column_lo(b, n, k):
                dve.wait_ge(c.sem("col_hi_ready"), n * PER + (k + 1))
                at = slice(k * P, (k + 1) * P)
                nc.vector.tensor_tensor(short(col_parts[:, 1, :, at]), columns_bank(b, k).rearrange(
                    "p (c t) -> p c t", c=DC), col_parts[:, 0, :, at], ALU.subtract).then_inc(
                    c.sem("col_lo_ready"), 1)

            def add(b, m):
                dve.wait_ge(c.sem("chunk_weighed"), m * PER + PER)
                nc.vector.scalar_tensor_tensor(out=total[:, :], in0=total[:, :], scalar=decay[b][:, 0:1],
                                               in1=part[b][:, :], op0=ALU.mult, op1=ALU.add)
                nc.vector.scalar_tensor_tensor(out=acc[:, :], in0=acc[:, :], scalar=decay[b][:, 0:1], in1=ps[4],
                                               op0=ALU.mult, op1=ALU.add).then_inc(c.sem("out_added"), 1)
                dve.wait_ge(c.sem("out_added"), m + 2)

            def step(b, g, attend, prepare, weigh):
                for k in range(PER):
                    if prepare:
                        column_lo(1 - b, g + 1, k)
                    if attend and k == 0:
                        maximum(b, g)
                if weigh:
                    add(1 - b, g - 1)
                if attend:
                    dve.wait_ge(c.sem("probT_hi_ready"), g + 1)
                    nc.vector.tensor_tensor(short(probT_parts[:, 1, :]), probsT, probT_parts[:, 0, :],
                                            ALU.subtract).then_inc(c.sem("probT_lo_ready"), 1)
                    for k in range(GPSIMD_ROWS, PER):
                        row_lo(dve, nc.vector, "vector_rows_ready", b, g, k)

            dve.sem_inc(c.sem("probs_transposed"), 1)
            dve.sem_inc(c.sem("topped"), 1)
            dve.wait_ge(c.sem("q_hi_ready"), 1)
            nc.vector.tensor_tensor(short(q_parts[:, 1, :, :]), qT[:, :, :], q_parts[:, 0, :, :],
                                    ALU.subtract).then_inc(c.sem("q_lo_ready"), 1)
            if own_kT is None:
                link(nc.vector.memset(neg[1][:, :], 3e38))
                link(nc.vector.memset(total[:, :], 0.0))
                link(nc.vector.memset(acc[:, :], 0.0))
                dve.sem_inc(c.sem("out_added"), 1)
            else:
                dve.wait_ge(c.sem("own_step"), 1)
                nc.vector.tensor_reduce(neg[1][:, :], ps[7][:, 0:P], X, ALU.max, negate=True).then_inc(
                    c.sem("own_max_ready"), 1)
                dve.wait_ge(c.sem("own_step"), 3)
                nc.vector.tensor_copy(acc[:, :], ps[4]).then_inc(c.sem("out_added"), 1)
                dve.wait_ge(c.sem("out_added"), 1)
            over_steps(dve, step)
            add(1, GROUPS - 1)
            link(nc.vector.reciprocal(top[:, :], total[:, :]))
            nc.vector.tensor_scalar(out, acc[:, :], top[:, 0:1], None, ALU.mult)

        @block.scalar
        def _(act):
            def column_hi(b, n, k):
                act.wait_ge(c.sem("columns_ready"), n * PER + (k + 1))
                nc.scalar.copy(short(col_parts[:, 0, :, k * P:(k + 1) * P]), columns_bank(b, k).rearrange(
                    "p (c t) -> p c t", c=DC)).then_inc(c.sem("col_hi_ready"), 1)

            def row_hi(b, g, k, weigh):
                if weigh:
                    act.wait_ge(c.sem("chunk_weighed"), (g - 1) * PER + (k + 1))
                nc.scalar.copy(short(row_parts[:, 0, k, :]), rows[b][:, k, :]).then_inc(c.sem("row_hi_ready"), 1)

            def exps(b, g):
                act.wait_ge(c.sem("max_ready"), g + 1)
                nc.scalar.activation(decay[b][:, :], neg[1 - b][:, :], ACT.Exp, scale=-1.0, bias=neg[b][:, 0:1])
                act.wait_ge(c.sem("probs_transposed"), g + 1)
                nc.scalar.activation(probs[:, :, :], scores if seen is None else probs[:, :, :], ACT.Exp,
                                     bias=neg[b][:, 0:1], accum_out=part[b][:, :]).then_inc(c.sem("probs_ready"), 1)

            def step(b, g, attend, prepare, weigh):
                if attend and seen is not None:
                    act.wait_ge(c.sem("topped"), g + 1)
                    nc.scalar.activation(unseen[:, :, :], seen_of(g), ACT.Copy, scale=1e30, bias=-1e30).then_inc(
                        c.sem("unseen_ready"), 1)
                for k in range(PER):
                    if prepare:
                        column_hi(1 - b, g + 1, k)
                    if attend and k == 4:
                        exps(b, g)
                    if attend and k % 2 == 1:
                        row_hi(b, g, k // 2, weigh)
                if attend:
                    act.wait_ge(c.sem("probs_transposed"), g + 2)
                    nc.scalar.copy(short(probT_parts[:, 0, :]), probsT).then_inc(c.sem("probT_hi_ready"), 1)
                    for k in range(PER // 2, PER):
                        row_hi(b, g, k, weigh)

            nc.scalar.copy(short(q_parts[:, 0, :, :]), qT[:, :, :]).then_inc(c.sem("q_hi_ready"), 1)
            if own_kT is not None:
                act.wait_ge(c.sem("own_max_ready"), 1)
                nc.scalar.activation(own_p[:, :], ps[7][:, 0:P], ACT.Exp, bias=neg[1][:, 0:1],
                                     accum_out=total[:, :]).then_inc(c.sem("own_probs_ready"), 1)
                act.wait_ge(c.sem("own_step"), 2)
                nc.scalar.copy(own_pT[:, :], ps[7][:, P:2 * P]).then_inc(c.sem("own_probsT_ready"), 1)
            over_steps(act, step)




def add_to_x(core):
    def evacuate(bank, link):
        link(core.nc.vector.tensor_tensor(core.x, core.x, bank, ALU.add))
    return evacuate


def l0_xattn(core):
    ring, nc = core.ring, core.nc
    with core.scratch(xn=[P, D], xnT=[P, DC, P], qT=[P, DC, P], kT=[P, DC, P], v=[P, D],
                      o=[P, D]) as (xn, xnT, qT, kT, v, o):
        norm_stage(core, core.x, xn[:, :], xnT[:, :, :], 1e-5)
        cols_stage(core, xnT, ring.take("L0_xattn_wq"), qT, scale=D ** -0.5)
        cols_stage(core, xnT, ring.take("L0_xattn_wk"), kT)
        rows_stage(core, xnT, ring.take("L0_xattn_wv"), lambda j, bank, link: nc.vector.tensor_copy(v[:, :], bank))
        wide_stage(core, qT, o[:, :], own_kT=kT, own_v=v[:, :])
        transpose_stage(core, o, qT, DC)
        down_stage(core, qT, ring.take("L0_xattn_wo"), add_to_x(core))


def small_products_stage(core, aT, products, evacuate):
    nc, c = core.nc, core
    with core.stage() as block:

        @block.tensor
        def _(pe):
            for out, kind, w in products:
                for i in range(DC):
                    lhsT, rhs = (aT[:, i, :], w[:, i, :]) if kind == "rows" else (w[:, i, :], aT[:, i, :])
                    last = nc.tensor.matmul(out, lhsT, rhs, start=(i == 0), stop=(i == DC - 1))
            last.then_inc(c.sem("products_ready"), 1)

        @block.vector
        def _(dve):
            dve.wait_ge(c.sem("products_ready"), 1)
            evacuate(Chain(dve, c.sem("dve_chain")))


def chain_stage(core, steps):
    c = core
    with core.stage() as block:

        def run(engine, name):
            for n, (who, step) in enumerate(steps):
                if who == name:
                    if n:
                        engine.wait_ge(c.sem("step_done"), n)
                    step().then_inc(c.sem("step_done"), 1)

        block.vector(lambda dve: run(dve, "vector"))
        block.scalar(lambda act: run(act, "scalar"))
        block.gpsimd(lambda pool: run(pool, "gpsimd"))
        block.tensor(lambda pe: run(pe, "tensor"))


def l0_attn(core):
    ring, nc, ps, c = core.ring, core.nc, core.psum, core
    small = core.operands[:, 0:DC * 400].rearrange("p (c n) -> p c n", c=DC)
    wk_idx, wk, wv, w_iw = small[:, :, 0:P], small[:, :, P:2 * P], small[:, :, 2 * P:3 * P], small[:, :, 3 * P:]
    hadamard = core.table["hadamard"]
    K = 64
    with core.scratch(xn=[P, D], xnT=[P, DC, P], qT=[P, HEADS, P], oT=[P, HEADS, P], keysT=[P, P], kT=[P, P],
                      v=[P, P], head_weight=[P, HEADS], index=[P, P], work=[P, P], top8=[P, 8], mask=[P, P]) as (
        xn, xnT, qT, oT, keysT, kT, v, head_weight, index, work, top8, mask,
    ):
        norm_stage(core, core.x, xn[:, :], xnT[:, :, :], 1e-5,
                   loads=[(core.operands[:, 0:DC * 400], core.dram["L0_attn_small"])])
        cols_stage(core, xnT, ring.take("L0_attn_wq_idx"), oT)

        def evacuate(link):
            nc.vector.tensor_copy(keysT[:, :], ps[0][:, 0:P])
            nc.vector.tensor_copy(kT[:, :], ps[1][:, 0:P])
            nc.vector.tensor_copy(v[:, :], ps[2][:, 0:P])
            link(nc.vector.tensor_copy(head_weight[:, :], ps[3][:, 0:HEADS]))

        small_products_stage(core, xnT, [(ps[0][:, 0:P], "cols", wk_idx), (ps[1][:, 0:P], "cols", wk),
                                         (ps[2][:, 0:P], "rows", wv), (ps[3][:, 0:HEADS], "rows", w_iw)], evacuate)

        with core.stage() as block:

            @block.tensor
            def _(pe):
                for g in range(4):
                    nc.tensor.matmul(ps[g][:, :], hadamard, oT[:, 4 * g:4 * g + 4, :].rearrange("p h t -> p (h t)"),
                                     start=True, stop=True).then_inc(c.sem("transform_ready"), 1)
                nc.tensor.matmul(ps[4][:, 0:P], hadamard, keysT[:, :], start=True, stop=True).then_inc(
                    c.sem("transform_ready"), 1)

            @block.scalar
            def _(act):
                for g in range(4):
                    act.wait_ge(c.sem("transform_ready"), g + 1)
                    nc.scalar.activation(qT[:, 4 * g:4 * g + 4, :].rearrange("p h t -> p (h t)"), ps[g][:, :],
                                         ACT.Copy, scale=P ** -0.5)

            @block.vector
            def _(dve):
                dve.wait_ge(c.sem("transform_ready"), 5)
                nc.vector.tensor_scalar(keysT[:, :], ps[4][:, 0:P], P ** -0.5, None, ALU.mult)

        with core.stage() as block:

            @block.tensor
            def _(pe):
                for h in range(HEADS):
                    last = nc.tensor.matmul(ps[h // 4][:, (h % 4) * P:(h % 4 + 1) * P], qT[:, h, :], keysT[:, :],
                                            start=True, stop=True)
                    if h % 4 == 3:
                        last.then_inc(c.sem("logits_ready"), 1)

            @block.scalar
            def _(act):
                for g in range(4):
                    act.wait_ge(c.sem("logits_ready"), g + 1)
                    nc.scalar.activation(oT[:, 4 * g:4 * g + 4, :].rearrange("p h t -> p (h t)"), ps[g][:, :],
                                         ACT.Relu).then_inc(c.sem("relu_ready"), 1)

            @block.vector
            def _(dve):
                link = Chain(dve, c.sem("dve_chain"))
                link(nc.vector.memset(index[:, :], 0.0))
                for h in range(HEADS):
                    dve.wait_ge(c.sem("relu_ready"), h // 4 + 1)
                    link(nc.vector.scalar_tensor_tensor(out=index[:, :], in0=oT[:, h, :],
                                                        scalar=head_weight[:, h:h + 1], in1=index[:, :],
                                                        op0=ALU.mult, op1=ALU.add))
                link(nc.vector.tensor_tensor(index[:, :], index[:, :], core.table["causal"], ALU.add))
                link(nc.vector.tensor_copy(work[:, :], index[:, :]))
                for _ in range(K // 8):
                    link(nc.vector.max(top8[:, :], work[:, :]))
                    link(nc.vector.match_replace(work[:, :], top8[:, :], work[:, :], TAKEN))
                link(nc.vector.tensor_scalar(index[:, :], index[:, :], NEG / 2, None, ALU.is_gt))
                link(nc.vector.scalar_tensor_tensor(out=mask[:, :], in0=work[:, :], scalar=TAKEN / 2,
                                                    in1=index[:, :], op0=ALU.is_le, op1=ALU.mult))
                link(nc.vector.tensor_scalar(mask[:, :], mask[:, :], 1.0, -NEG, ALU.subtract, ALU.mult))

        cols_stage(core, xnT, ring.take("L0_attn_wq"), qT)
        heads_stage(core, lambda h: qT[:, h, :], lambda h: kT[:, :], lambda h: v[:, :], mask[:, :], P ** -0.5,
                    lambda g, bank: nc.scalar.copy(oT[:, 4 * g:4 * g + 4, :].rearrange("p h t -> p (h t)"), bank[:, :]))
        down_stage(core, oT, ring.take("L0_attn_wo"), add_to_x(core))


def l0_ffn(core):
    ring, nc, ps = core.ring, core.nc, core.psum
    router = core.operands[:, 0:DC * 16].rearrange("p (c n) -> p c n", c=DC)
    bias = core.operands[:, DC * 16:DC * 16 + 16]
    E, PAD = 16, 8
    with core.scratch(xn=[P, D], xnT=[P, DC, P], h=[P, HEADS, P], hT=[P, HEADS, P], prob=[P, E + PAD],
                      left=[P, E + PAD], top8=[P, 8], neg_max=[P, 1], chosen=[P, E]) as (
        xn, xnT, h, hT, prob, left, top8, neg_max, chosen,
    ):
        norm_stage(core, core.x, xn[:, :], xnT[:, :, :], 1e-5,
                   loads=[(core.operands[:, 0:DC * 16], core.dram["L0_ffn_small"]),
                          (bias, core.dram["L0_ffn_rows"].partition_broadcast(P))])

        def evacuate(link):
            link(nc.vector.tensor_tensor(prob[:, 0:E], ps[0][:, 0:E], bias, ALU.add))

        small_products_stage(core, xnT, [(ps[0][:, 0:E], "rows", router)], evacuate)
        chain_stage(core, [
            ("vector", lambda: nc.vector.tensor_reduce(neg_max[:, :], prob[:, 0:E], X, ALU.max, negate=True)),
            ("scalar", lambda: nc.scalar.activation(prob[:, 0:E], prob[:, 0:E], ACT.Exp, bias=neg_max[:, 0:1])),
            ("vector", lambda: nc.vector.memset(prob[:, E:E + PAD], -1.0)),
            ("vector", lambda: nc.vector.max(top8[:, :], prob[:, :])),
            ("vector", lambda: nc.vector.memset(top8[:, 4:8], -1.0)),
            ("vector", lambda: nc.vector.match_replace(left[:, :], top8[:, :], prob[:, :], TAKEN)),
            ("vector", lambda: nc.vector.tensor_scalar(chosen[:, :], left[:, 0:E], TAKEN / 2, None, ALU.is_le)),
        ])
        rows_stage(core, xnT, ring.take("L0_ffn_W1"),
                   lambda j, bank, link: nc.scalar.activation(h[:, 4 * j:4 * j + 4, :].rearrange("p e t -> p (e t)"),
                                                              bank, ACT.Gelu),
                   on_scalar=True,
                   after=lambda link: link(nc.vector.tensor_tensor(
                       h[:, :, :], h[:, :, :], chosen[:, :].unsqueeze(2).to_broadcast([P, E, P]), ALU.mult)))
        transpose_stage(core, h[:, :, :].rearrange("p e t -> p (e t)"), hT, HEADS)
        down_stage(core, hT, ring.take("L0_ffn_W2"), add_to_x(core))


def l1_xattn(core):
    nc = core.nc
    V = nc.vector
    with core.scratch(xn=[P, D], xnT=[P, DC, P], o=[P, D], any_seen=[P, 1]) as (
        xn, xnT, o, any_seen,
    ), nc.sbuf_tensor("seen", [P, KV], U8) as seen, nc.sbuf_tensor("seen_once", [P, KV // P], U8) as seen_once:
        mask = core.dram["memory_mask"]
        norm_stage(core, core.x, xn[:, :], xnT[:, :, :], 1e-5, scale=D ** -0.5,
                   loads=[(seen[:, :], mask.partition_broadcast(P)),
                          (seen_once[:, :], mask.rearrange("(p n) -> p n", p=P))])
        wide_stage(core, xnT, o[:, :], seen=seen)
        chain_stage(core, [
            ("vector", lambda: V.tensor_reduce(any_seen[:, :], seen_once[:, :], X, ALU.max)),
            ("tensor", lambda: nc.tensor.matmul(core.psum[0][:, 0:1], core.ones, any_seen[:, :], start=True,
                                                stop=True)),
            ("vector", lambda: V.tensor_scalar(any_seen[:, :], core.psum[0][:, 0:1], 1.0, None, ALU.min)),
            ("vector", lambda: V.scalar_tensor_tensor(out=core.x, in0=o[:, :], scalar=any_seen[:, 0:1],
                                                      in1=core.x, op0=ALU.mult, op1=ALU.add)),
        ])


def rotation_steps(core, first, second, cos, sin, t):
    nc = core.nc
    V = nc.vector.tensor_tensor
    return [
        ("vector", lambda: V(t[0], first, cos, ALU.mult)),
        ("vector", lambda: V(t[1], second, sin, ALU.mult)),
        ("vector", lambda: V(t[2], second, cos, ALU.mult)),
        ("vector", lambda: V(t[3], first, sin, ALU.mult)),
        ("vector", lambda: V(first, t[0], t[1], ALU.subtract)),
        ("vector", lambda: V(second, t[2], t[3], ALU.add)),
    ]


def head_norm_steps(core, rows, heads, width, eps, square, sums, mean=True):
    nc = core.nc
    r3 = rows.rearrange("p (h d) -> p h d", h=heads)
    s3 = square.rearrange("p (h d) -> p h d", h=heads)
    return [
        ("vector", lambda: nc.vector.tensor_tensor(square, rows, rows, ALU.mult)),
        ("vector", lambda: nc.vector.tensor_reduce(sums, s3, X, ALU.add)),
        ("vector", lambda: nc.vector.tensor_scalar(sums, sums, 1.0 / width if mean else 1.0, eps, ALU.mult, ALU.add)),
        ("gpsimd", lambda: nc.gpsimd.tensor_tensor(sums, sums, core.minus_half[:, 0:heads], ALU.pow)),
        ("vector", lambda: nc.vector.tensor_tensor(r3, r3, sums.unsqueeze(2).to_broadcast([P, heads, width]),
                                                   ALU.mult)),
    ]


def l1_attn(core):
    ring, nc, ps, c = core.ring, core.nc, core.psum, core
    ops = core.operands
    b_in, b_out, gamma, beta = ops[:, 0:3 * D], ops[:, 3 * D:4 * D], ops[:, 4 * D:5 * D], ops[:, 5 * D:6 * D]
    R = D // 2
    cos, sin = core.table["cos1"], core.table["sin1"]
    with core.scratch(xn=[P, D], xnT=[P, DC, P], xg=[P, D], xgT=[P, DC, P], qkv=[P, 3 * D], square=[P, D],
                      turn=[P, 4, R // 2], sums=[P, 1], y=[P, D]) as (xn, xnT, xg, xgT, qkv, square, turn, sums, y):
        norm_stage(core, core.x, xn[:, :], xnT[:, :, :], 1e-5,
                   loads=[(ops[:, 0:6 * D], core.dram["L1_attn_rows"].partition_broadcast(P))])
        norm_stage(core, xn[:, :], xg[:, :], xgT[:, :, :], 1e-5, gain=gamma, shift=beta)
        rows_stage(core, xgT, ring.take("L1_attn_W_in"),
                   lambda j, bank, link: nc.vector.tensor_tensor(qkv[:, j * D:(j + 1) * D], bank,
                                                                 b_in[:, j * D:(j + 1) * D], ALU.add))
        steps = []
        for part in (1, 2):
            rows = qkv[:, part * D:(part + 1) * D]
            pairs = rows[:, 0:R].rearrange("p (i two) -> p i two", two=2)
            steps += rotation_steps(core, pairs[:, :, 0], pairs[:, :, 1], cos, sin, [turn[:, i, :] for i in range(4)])
            steps += head_norm_steps(core, rows, 1, D, 0.0, square[:, :], sums[:, :], mean=False)
        steps.append(("vector", lambda: nc.vector.tensor_tensor(y[:, :], qkv[:, D:2 * D], qkv[:, 2 * D:3 * D],
                                                                ALU.mult)))
        chain_stage(core, steps)
        with core.stage() as block:

            @block.tensor
            def _(pe):
                nc.tensor.matmul(ps[0][:, :], core.ones, y[:, :], start=True, stop=True).then_inc(
                    c.sem("token_sum_ready"), 1)

            @block.vector
            def _(dve):
                link = Chain(dve, c.sem("dve_chain"))
                dve.wait_ge(c.sem("token_sum_ready"), 1)
                link(nc.vector.tensor_scalar(square[:, :], ps[0][:, :], 0.5, 0.5, ALU.mult, ALU.add))
                link(nc.vector.tensor_tensor(y[:, :], square[:, :], qkv[:, 0:D], ALU.mult))
                link(nc.vector.tensor_tensor(core.x, core.x, xn[:, :], ALU.add))
                link(nc.vector.tensor_tensor(core.x, core.x, b_out, ALU.add))

        transpose_stage(core, y, xgT, DC)
        down_stage(core, xgT, ring.take("L1_attn_W_out"), add_to_x(core))


def l1_ffn(core):
    ring, nc, ps, c = core.ring, core.nc, core.psum, core
    R, K = 64, 8
    ops = core.operands
    small = ops[:, 0:DC * 96].rearrange("p (c n) -> p c n", c=DC)
    upT, biases = ops[0:R, 384:384 + D], ops[:, 896:896 + R]
    with core.scratch(xn=[P, D], xnT=[P, DC, P], sig=[P, R // 2], logits=[P, R], mid=[P, R], top8=[P, 8], left=[P, R],
                      total=[P, 1], midT=[R, P]) as (xn, xnT, sig, logits, mid, top8, left, total, midT):
        norm_stage(core, core.x, xn[:, :], xnT[:, :, :], 1e-5,
                   loads=[(ops[:, 0:384], core.dram["L1_ffn_small"]), (upT, core.dram["L1_ffn_BT"]),
                          (biases, core.dram["L1_ffn_rows"].partition_broadcast(P))])

        def evacuate(link):
            nc.vector.tensor_copy(sig[:, :], ps[0][:, 0:R // 2])
            link(nc.vector.tensor_copy(mid[:, :], ps[0][:, R // 2:R // 2 + R]))

        small_products_stage(core, xnT, [(ps[0][:, 0:96], "rows", small)], evacuate)
        l3, b3 = logits[:, :].rearrange("p (r two) -> p r two", two=2), biases.rearrange("p (r two) -> p r two", two=2)
        V = nc.vector
        chain_stage(core, [
            ("scalar", lambda: nc.scalar.activation(sig[:, :], sig[:, :], ACT.Sigmoid)),
            ("vector", lambda: V.tensor_tensor(l3, sig[:, :].unsqueeze(2).to_broadcast([P, R // 2, 2]), b3, ALU.add)),
            ("vector", lambda: V.max(top8[:, :], logits[:, :])),
            ("vector", lambda: V.match_replace(left[:, :], top8[:, :], logits[:, :], TAKEN)),
            ("vector", lambda: V.tensor_reduce(total[:, :], top8[:, :], X, ALU.add)),
            ("vector", lambda: V.reciprocal(total[:, :], total[:, :])),
            ("vector", lambda: V.scalar_tensor_tensor(out=logits[:, :], in0=left[:, :], scalar=TAKEN / 2,
                                                      in1=logits[:, :], op0=ALU.is_le, op1=ALU.mult)),
            ("vector", lambda: V.tensor_scalar(logits[:, :], logits[:, :], total[:, 0:1], K * 16.0 / K, ALU.mult,
                                               ALU.mult)),
            ("vector", lambda: V.tensor_tensor(mid[:, :], mid[:, :], logits[:, :], ALU.mult)),
        ])
        (base,) = ring.take("L1_ffn_base_W")
        with core.stage() as block:

            @block.sync
            def _(sp):
                base.refill(sp)

            @block.tensor
            def _(pe):
                nc.tensor.transpose(ps[1][0:R, 0:P], mid[:, :], core.ident).then_inc(c.sem("transposed"), 1)
                base.wait_landed(pe)
                for i in range(DC):
                    last = nc.tensor.matmul(ps[0][:, :], xnT[:, i, :], base.data[:, i, :], start=(i == 0), stop=False)
                base.done(last)
                pe.wait_ge(c.sem("midT_ready"), 1)
                nc.tensor.matmul(ps[0][:, :], midT[:, :], upT, start=False, stop=True).then_inc(
                    c.sem("output_ready"), 1)

            @block.scalar
            def _(act):
                act.wait_ge(c.sem("transposed"), 1)
                nc.scalar.copy(midT[:, :], ps[1][0:R, 0:P]).then_inc(c.sem("midT_ready"), 1)

            @block.vector
            def _(dve):
                dve.wait_ge(c.sem("output_ready"), 1)
                nc.vector.tensor_tensor(core.x, core.x, ps[0][:, :], ALU.add)


KVH = 4
USES = 3 * PER


class SideBank:

    def __init__(self):
        self.before = {h: ("values" if h % 2 else "keys", h // 2) for h in range(2 * PER)}
        self.after = {2 * j + 2: ("keysT", j) for j in range(PER)}
        order = []
        for h in range(HEADS):
            order += [self.before[h]] if h in self.before else []
            order += [self.after[h]] if h in self.after else []
        self.index = {use: n for n, use in enumerate(order)}
        assert len(order) == USES


def over_groups(engine, group, count=GROUPS, peeled=2):
    group(1, -1, False, True)
    with engine.Fori(0, (count - peeled) // 2) as i:
        for b in range(2):
            group(b, i * 2 + b, True, True)
    for g in range(count - peeled, count):
        group(g % 2, g, True, g + 1 < count)


def grouped_stage(core, qT, wk, wv, bk, acc, total):
    nc, c, ps = core.nc, core, core.psum
    side = SideBank()
    with core.scratch(ctx0=[P, DC, P], ctx1=[P, DC, P], parts0=[P, 2, DC, P], parts1=[P, 2, DC, P],
                      w=[P, 2, 2, DC, D], keysT0=[P, KVH, GROUP], keysT1=[P, KVH, GROUP],
                      values0=[P, PER, D], values1=[P, PER, D], mask0=[P, 2, TILE], mask1=[P, 2, TILE],
                      probs0=[P, 2, TILE], probs1=[P, 2, TILE], probsT0=[P, PER, P], probsT1=[P, PER, P],
                      keys0=[P, D], keys1=[P, D], square=[P, D], sumsq=[P, KVH], rnorm=[P, KVH],
                      top=[P, HEADS], neg0=[P, HEADS], neg1=[P, HEADS], decay0=[P, HEADS], decay1=[P, HEADS],
                      part0=[P, HEADS], part1=[P, HEADS]) as (
        ctx0, ctx1, parts0, parts1, w, keysT0, keysT1, values0, values1, mask0, mask1, probs0, probs1, probsT0,
        probsT1, keys0, keys1, square, sumsq, rnorm, top, neg0, neg1, decay0, decay1, part0, part1,
    ), core.stage() as block:
        ctxT, keysT, values, mask = [ctx0, ctx1], [keysT0, keysT1], [values0, values1], [mask0, mask1]
        probs, probsT, keys, neg = [probs0, probs1], [probsT0, probsT1], [keys0, keys1], [neg0, neg1]
        decay, part, parts = [decay0, decay1], [part0, part1], [parts0, parts1]
        dram, units = core.dram, (wk, wv)

        @block.sync
        def _(sp):
            def load_mask(b, g, masked):
                sp.wait_ge(c.sem("scores_masked"), masked * HEADS + 2)
                sp.dma_start(mask[b][:, :, :].rearrange("p a n -> p (a n)"),
                             dram["score_mask"][bass.ds(g, 1)].rearrange("a p n -> (a p) n")).then_inc(
                    c.sem(f"mask_landed_{b}"), 16)

            def two_groups(i, chunks):
                for m in range(chunks):
                    sp.wait_ge(c.sem("ctx_lo_ready"), i * (2 * PER) + (m + 1))
                    sp.dma_start(ctxT[m % 2][:, :, :], dram["ctxT_chunks"][bass.ds(
                        i * (2 * PER) + (2 + m), 1)].rearrange("a p c n -> (a p) c n")).then_inc(
                        c.sem(f"ctxT_landed_{m % 2}"), 16)
                    if m == PER - 1:
                        load_mask(1, i * 2 + 1, i * 2)
                    if m == 2 * PER - 1:
                        load_mask(0, i * 2 + 2, i * 2 + 1)

            for b in range(2):
                sp.dma_start(ctxT[b][:, :, :], dram["ctxT_chunks"][b]).then_inc(c.sem(f"ctxT_landed_{b}"), 16)
            load_mask(0, 0, 0)
            for u in units:
                u.refill(sp)
            with sp.Fori(0, GROUPS // 2 - 1) as i:
                two_groups(i, 2 * PER)
            two_groups(GROUPS // 2 - 1, 2 * PER - 2)

        @block.tensor
        def _(pe):
            def project(b, use, g):
                what, j = use
                wait_count(pe, c.sem("side_evacuated"), g * USES + side.index[use])
                if what == "keysT":
                    pe.wait_ge(c.sem("keys_normed"), g * PER + (j + 1))
                    for kh in range(KVH):
                        last = nc.tensor.transpose(ps[7][:, kh * P:(kh + 1) * P],
                                                   keys[j % 2][:, kh * P:(kh + 1) * P], core.ident)
                else:
                    pe.wait_ge(c.sem("ctx_lo_ready"), g * PER + (j + 1))
                    which, own = ("keys", "values").index(what), parts[(b + j) % 2]
                    if j == 0 and isinstance(g, int) and g == 0:
                        pe.wait_ge(c.sem("weight_lo_ready"), which + 1)
                        units[which].done(nc.tensor.matmul(ps[7][:, 0:P], core.zeros[:, 0:P], core.zeros[:, 0:P],
                                                           start=True, stop=True))
                    for i in range(DC):
                        last = matmul_parts(nc, ps[7], [own[:, s, i, :] for s in range(2)],
                                            [w[:, which, s, i, :] for s in range(2)], i == 0, i == DC - 1)
                last.then_inc(c.sem("side_product"), 1)

            def score(b, h, g):
                pe.wait_ge(c.sem("scores_masked"), g * HEADS + (h + 1))
                for t in range(2):
                    last = nc.tensor.matmul(ps[2 * (h % 2) + t][:, 0:TILE], qT[:, h, :],
                                            keysT[b][:, h // 4, t * TILE:(t + 1) * TILE], start=True, stop=True)
                last.then_inc(c.sem("scores_ready"), 1)

            def transpose_probs(h, g):
                pe.wait_ge(c.sem("probs_ready"), g * HEADS + (h + 1))
                pe.wait_ge(c.sem("probsT_head_ready"), g * HEADS + (h + 1))
                pe.wait_ge(c.sem("probsT_tail_ready"), g * HEADS + (h + 1))
                flat = probs[h % 2][:, :, :].rearrange("p a n -> p (a n)")
                for k in range(PER):
                    last = nc.tensor.transpose(ps[4 + k // 4][:, (k % 4) * P:(k % 4 + 1) * P],
                                               flat[:, k * P:(k + 1) * P], core.ident)
                last.then_inc(c.sem("probs_transposed"), 1)

            def weigh(b, h, g):
                pe.wait_ge(c.sem("probsT_head_ready"), g * HEADS + (h + 2))
                pe.wait_ge(c.sem("probsT_tail_ready"), g * HEADS + (h + 2))
                pe.wait_ge(c.sem("out_added"), g * HEADS + (h + 1))
                kh = h // 4
                for k in range(PER):
                    last = nc.tensor.matmul(ps[6][:, 0:P], probsT[h % 2][:, k, :],
                                            values[b][:, k, kh * P:(kh + 1) * P], start=(k == 0),
                                            stop=(k == PER - 1))
                last.then_inc(c.sem("out_ready"), 1)

            def group(b, g, attend, prepare):
                if attend:
                    pe.wait_ge(c.sem("side_evacuated"), g * USES + USES)
                    score(b, 0, g)
                for h in range(HEADS):
                    if attend and h + 1 < HEADS:
                        score(b, h + 1, g)
                    if prepare and h in side.before:
                        project(1 - b, side.before[h], g + 1)
                    if attend:
                        transpose_probs(h, g)
                        if h > 0:
                            weigh(b, h - 1, g)
                    if prepare and h in side.after:
                        project(1 - b, side.after[h], g + 1)
                if attend:
                    weigh(b, HEADS - 1, g)

            over_groups(pe, group)

        def splits(g, j):
            return not (isinstance(g, int) and g * PER + j + 1 >= GROUPS * PER)

        @block.vector
        def _(dve):
            def ctx_lo(b, g, j):
                dve.wait_ge(c.sem("ctx_hi_ready"), g * PER + (j + 1))
                nc.vector.tensor_tensor(short(parts[b][:, 1, :, :]), ctxT[b][:, :, :], parts[b][:, 0, :, :],
                                        ALU.subtract).then_inc(c.sem("ctx_lo_ready"), 1)

            def evacuate_keys(g, j):
                dve.wait_ge(c.sem("side_product"), g * USES + (side.index["keys", j] + 1))
                nc.vector.tensor_tensor(keys[j % 2][:, :], ps[7], bk, ALU.add).then_inc(c.sem("side_evacuated"), 1)

            def spread_of_keys(g, j):
                dve.wait_ge(c.sem("keys_squared"), g * PER + (j + 1))
                nc.vector.tensor_reduce(sumsq[:, :], square[:, :].rearrange("p (h d) -> p h d", h=KVH), X,
                                        ALU.add).then_inc(c.sem("sumsq_ready"), 1)
                dve.wait_ge(c.sem("sumsq_ready"), g * PER + (j + 1))
                nc.vector.tensor_scalar(sumsq[:, :], sumsq[:, :], 1.0 / P, 1e-6, ALU.mult, ALU.add).then_inc(
                    c.sem("spread_ready"), 1)

            def norm_keys(g, j):
                dve.wait_ge(c.sem("rnorm_ready"), g * PER + (j + 1))
                k3 = keys[j % 2][:, :].rearrange("p (h d) -> p h d", h=KVH)
                nc.vector.tensor_tensor(k3, k3, rnorm[:, :].unsqueeze(2).to_broadcast([P, KVH, P]),
                                        ALU.mult).then_inc(c.sem("keys_normed"), 1)

            def store_keysT(b, g, j):
                dve.wait_ge(c.sem("side_product"), g * USES + (side.index["keysT", j] + 1))
                nc.vector.tensor_copy(keysT[b][:, :, j * P:(j + 1) * P], ps[7].rearrange(
                    "p (h t) -> p h t", h=KVH)).then_inc(c.sem("side_evacuated"), 1)

            def mask_scores(b, h, g):
                dve.wait_ge(c.sem("scores_ready"), g * HEADS + (h + 1))
                dve.wait_ge(c.sem("probs_transposed"), g * HEADS + (h + 1))
                dve.sem_inc(c.sem("masking_started"), 1)
                nc.vector.tensor_tensor_reduce(
                    out=probs[h % 2][:, :, :], in0=core.banks[:, 2 * (h % 2):2 * (h % 2) + 2, 0:TILE],
                    in1=mask[b][:, :, :], scale=1.0, scalar=-3e38, op0=ALU.add, op1=ALU.max,
                    accum_out=top[:, h:h + 1]).then_inc(c.sem("scores_masked"), 1)
                dve.wait_ge(c.sem("scores_masked"), g * HEADS + (h + 3))
                nc.vector.scalar_tensor_tensor(out=neg[b][:, h:h + 1], in0=top[:, h:h + 1], scalar=-1.0,
                                               in1=neg[1 - b][:, h:h + 1], op0=ALU.mult, op1=ALU.min).then_inc(
                    c.sem("max_ready"), 1)

            def add_out(b, h, g):
                dve.wait_ge(c.sem("out_ready"), g * HEADS + (h + 1))
                nc.vector.scalar_tensor_tensor(out=acc[:, h, :], in0=acc[:, h, :], scalar=decay[b][:, h:h + 1],
                                               in1=ps[6][:, 0:P], op0=ALU.mult,
                                               op1=ALU.add).then_inc(c.sem("out_added"), 1)

            def group(b, g, attend, prepare):
                n = g + 1
                if attend:
                    dve.wait_ge(c.sem(f"mask_landed_{b}"), (g - b) * 8 + 16)
                    mask_scores(b, 0, g)
                for h in range(HEADS):
                    if prepare and h % 2 == 1 and h - 1 in side.after:
                        store_keysT(1 - b, n, side.after[h - 1][1])
                    if attend and h > 1:
                        add_out(b, h - 2, g)
                    if attend and h + 1 < HEADS:
                        mask_scores(b, h + 1, g)
                    if prepare and h in side.before and h % 2 == 0:
                        evacuate_keys(n, h // 2)
                        if splits(n, h // 2):
                            ctx_lo((b + h // 2) % 2, n, h // 2 + 1)
                    if prepare and h % 2 == 0 and h > 0:
                        norm_keys(n, h // 2 - 1)
                    if attend:
                        dve.wait_ge(c.sem("probs_transposed"), g * HEADS + (h + 3))
                        nc.vector.tensor_copy(probsT[h % 2][:, 0:4, :].rearrange("p k t -> p (k t)"),
                                              ps[4]).then_inc(c.sem("probsT_head_ready"), 1)
                    if prepare and h in side.before and h % 2 == 1:
                        spread_of_keys(n, h // 2)
                if attend:
                    add_out(b, HEADS - 2, g)
                    add_out(b, HEADS - 1, g)
                    dve.wait_ge(c.sem("probs_ready"), g * HEADS + HEADS)
                    nc.vector.tensor_tensor(total, total, decay[b][:, :], ALU.mult).then_inc(c.sem("totalled"), 1)
                    dve.wait_ge(c.sem("totalled"), g * 2 + 1)
                    nc.vector.tensor_tensor(total, total, part[b][:, :], ALU.add).then_inc(c.sem("totalled"), 1)
                    dve.wait_ge(c.sem("totalled"), g * 2 + 2)

            dve.sem_inc(c.sem("scores_masked"), 2)
            dve.sem_inc(c.sem("probs_transposed"), 2)
            dve.sem_inc(c.sem("out_added"), 1)
            dve.sem_inc(c.sem("probsT_head_ready"), 1)
            dve.sem_inc(c.sem("probsT_tail_ready"), 1)
            ctx_lo(0, 0, 0)
            for k, u in enumerate(units):
                dve.wait_ge(c.sem("weight_hi_ready"), k + 1)
                nc.vector.tensor_tensor(short(w[:, k, 1, :, :]), u.data, w[:, k, 0, :, :], ALU.subtract).then_inc(
                    c.sem("weight_lo_ready"), 1)
            nc.vector.memset(neg[1][:, :], 3e38)
            nc.vector.memset(total, 0.0)
            nc.vector.memset(acc.rearrange("p h d -> p (h d)"), 0.0).then_inc(c.sem("cleared"), 1)
            dve.wait_ge(c.sem("cleared"), 1)
            over_groups(dve, group)

        @block.gpsimd
        def _(pool):
            with pool.Fori(0, GROUPS * PER) as n:
                pool.wait_ge(c.sem("spread_ready"), n + 1)
                nc.gpsimd.tensor_tensor(rnorm[:, :], sumsq[:, :], core.minus_half[:, 0:KVH], ALU.pow).then_inc(
                    c.sem("rnorm_ready"), 1)

        @block.scalar
        def _(act):
            def ctx_hi(b, g, j):
                act.wait_ge(c.sem(f"ctxT_landed_{b}"), g * (8 * PER) + ((j - b) * 8 + 16))
                nc.scalar.copy(short(parts[b][:, 0, :, :]), ctxT[b][:, :, :]).then_inc(c.sem("ctx_hi_ready"), 1)

            def square_keys(g, j):
                act.wait_ge(c.sem("side_evacuated"), g * USES + (side.index["keys", j] + 1))
                wait_count(act, c.sem("sumsq_ready"), g * PER + j)
                nc.scalar.activation(square[:, :], keys[j % 2][:, :], ACT.Square).then_inc(c.sem("keys_squared"), 1)

            def store_values(b, g, j):
                act.wait_ge(c.sem("side_product"), g * USES + (side.index["values", j] + 1))
                nc.scalar.copy(values[b][:, j, :], ps[7]).then_inc(c.sem("side_evacuated"), 1)

            def exp_scores(b, h, g):
                act.wait_ge(c.sem("max_ready"), g * HEADS + (h + 1))
                nc.scalar.activation(decay[b][:, h:h + 1], neg[1 - b][:, h:h + 1], ACT.Exp, scale=-1.0,
                                     bias=neg[b][:, h:h + 1])
                flat = probs[h % 2][:, :, :].rearrange("p a n -> p (a n)")
                nc.scalar.activation(flat, flat, ACT.Exp, bias=neg[b][:, h:h + 1],
                                     accum_out=part[b][:, h:h + 1]).then_inc(c.sem("probs_ready"), 1)

            def group(b, g, attend, prepare):
                n = g + 1
                if attend:
                    exp_scores(b, 0, g)
                for h in range(HEADS):
                    if attend and h + 1 < HEADS:
                        exp_scores(b, h + 1, g)
                    if prepare and h in side.before and h % 2 == 0 and splits(n, h // 2):
                        act.wait_ge(c.sem("side_product"), n * USES + (side.index["keys", h // 2] + 1))
                        ctx_hi((b + h // 2) % 2, n, h // 2 + 1)
                    if prepare and h in side.before and h % 2 == 1:
                        store_values(1 - b, n, h // 2)
                    if attend:
                        act.wait_ge(c.sem("probs_transposed"), g * HEADS + (h + 3))
                        nc.scalar.copy(probsT[h % 2][:, 4:PER, :].rearrange("p k t -> p (k t)"),
                                       ps[5][:, 0:(PER - 4) * P]).then_inc(c.sem("probsT_tail_ready"), 1)
                    if prepare and h in side.before and h % 2 == 0:
                        square_keys(n, h // 2)

            ctx_hi(0, 0, 0)
            for k, u in enumerate(units):
                u.wait_landed(act)
                nc.scalar.copy(short(w[:, k, 0, :, :]), u.data).then_inc(c.sem("weight_hi_ready"), 1)
            over_groups(act, group)


def l2_xattn(core):
    ring, nc = core.ring, core.nc
    ops = core.operands
    bk, bv = ops[:, 0:D], ops[:, D:2 * D]
    qn, kn = ops[:, 2 * D:2 * D + P], ops[:, 2 * D + P:2 * D + 2 * P]
    rows = core.dram["L2_xattn_rows"]
    V = nc.vector
    with core.scratch(qT=[P, HEADS, P], acc=[P, HEADS, P], total=[P, HEADS]) as (qT, acc, total):
        with core.scratch(xn=[P, D], xnT=[P, DC, P], q=[P, HEADS * P], square=[P, HEADS * P], sums=[P, HEADS],
                          bias=[P, HEADS * P]) as (xn, xnT, q, square, sums, bias):
            norm_stage(core, core.x, xn[:, :], xnT[:, :, :], 1e-5,
                       loads=[(ops, rows[0:2 * D + 2 * P].partition_broadcast(P)),
                              (bias[:, :], rows[2 * D + 2 * P:2 * D + 2 * P + HEADS * P].partition_broadcast(P))])
            rows_stage(core, xnT, ring.take("L2_xattn_Wq"),
                       lambda j, bank, link: V.tensor_tensor(q[:, j * D:(j + 1) * D], bank,
                                                             bias[:, j * D:(j + 1) * D], ALU.add))
            q3 = q[:, :].rearrange("p (h d) -> p h d", h=HEADS)
            steps = head_norm_steps(core, q[:, :], HEADS, P, 1e-6, square[:, :], sums[:, :])
            for w in (qn, kn):
                steps.append(("vector", lambda w=w: V.tensor_tensor(q3, q3, w.unsqueeze(1).to_broadcast(
                    [P, HEADS, P]), ALU.mult)))
            chain_stage(core, steps)
            transpose_stage(core, q, qT, HEADS, scale=P ** -0.5)
        (wk,), (wv,) = ring.take("L2_xattn_Wk"), ring.take("L2_xattn_Wv")
        grouped_stage(core, qT, wk, wv, bk, acc[:, :, :], total[:, :])
        acc4 = acc[:, :, :].rearrange("p (k g) d -> p k g d", k=KVH)
        bv4 = bv.rearrange("p (k d) -> p k d", k=KVH).unsqueeze(2).to_broadcast([P, KVH, HEADS // KVH, P])
        chain_stage(core, [
            ("vector", lambda: V.reciprocal(total[:, :], total[:, :])),
            ("vector", lambda: V.tensor_tensor(acc[:, :, :], acc[:, :, :],
                                               total[:, :].unsqueeze(2).to_broadcast([P, HEADS, P]), ALU.mult)),
            ("vector", lambda: V.tensor_tensor(acc4, acc4, bv4, ALU.add)),
        ])
        transpose_stage(core, acc[:, :, :].rearrange("p h d -> p (h d)"), qT, HEADS)
        down_stage(core, qT, ring.take("L2_xattn_Wo"), add_to_x(core))


def l2_attn(core):
    ring, nc = core.ring, core.nc
    W = D // HEADS
    ops = core.operands
    V = nc.vector
    with core.scratch(xn=[P, D], xnT=[P, DC, P], q=[P, D], k=[P, D], v=[P, D], qT=[P, DC, P], kT=[P, DC, P],
                      own_qT=[P, HEADS, P], oT=[P, DC, P]) as (xn, xnT, q, k, v, qT, kT, own_qT, oT):
        norm_stage(core, core.x, xn[:, :], xnT[:, :, :], 1e-5,
                   loads=[(ops, core.dram["L2_attn_rows"].partition_broadcast(P))])
        rows_stage(core, xnT, ring.take("L2_attn_wq") + ring.take("L2_attn_wk") + ring.take("L2_attn_wv"),
                   lambda j, bank, link: V.tensor_tensor((q, k, v)[j][:, :], bank, ops[:, j * D:(j + 1) * D], ALU.add))
        transpose_stage(core, q, qT, DC)
        transpose_stage(core, k, kT, DC)
        own4 = own_qT[:, :, :].rearrange("p (c b) t -> p c b t", b=4)
        steps = [("vector", lambda: V.memset(own_qT[:, :, :].rearrange("p h t -> p (h t)"), 0.0))]
        for b in range(4):
            at = slice(W * b, W * (b + 1))
            steps.append(("vector", lambda at=at, b=b: V.tensor_copy(own4[at, :, b, :], qT[at, :, :])))
        steps.append(("vector", lambda: V.tensor_tensor(core.x, core.x, ops[:, 3 * D:4 * D], ALU.add)))
        chain_stage(core, steps)
        heads_stage(core, lambda h: own_qT[:, h, :], lambda h: kT[:, h // 4, :], lambda h: v[:, h * W:(h + 1) * W],
                    core.table["causal"], W ** -0.5, lambda g, bank: nc.scalar.copy(oT[:, g, :], bank[:, 0:P]),
                    value_rows=W)
        down_stage(core, oT, ring.take("L2_attn_wo"), add_to_x(core))


def l2_ffn(core):
    ring, nc, ps, c = core.ring, core.nc, core.psum, core
    F = 2048
    V = nc.vector
    with core.scratch(xn=[P, D], xnT=[P, DC, P], h=[P, F], other=[P, F], hT=[P, HEADS, P], outT=[P, HEADS, P]) as (
        xn, xnT, h, other, hT, outT,
    ):
        norm_stage(core, core.x, xn[:, :], xnT[:, :, :], 1e-5)
        rows_stage(core, xnT, ring.take("L2_ffn_W1"),
                   lambda j, bank, link: nc.scalar.activation(h[:, j * D:(j + 1) * D], bank, ACT.Silu), on_scalar=True)
        rows_stage(core, xnT, ring.take("L2_ffn_W3"),
                   lambda j, bank, link: V.tensor_tensor(h[:, j * D:(j + 1) * D], h[:, j * D:(j + 1) * D], bank,
                                                         ALU.mult))
        steps, a, b = [], h, other
        for width in (P, 2 * P, 4 * P, 8 * P):
            va, vb = (t[:, :].rearrange("p (n two w) -> p n two w", two=2, w=width) for t in (a, b))
            for half, op in enumerate((ALU.add, ALU.subtract)):
                steps.append(("vector", lambda va=va, vb=vb, half=half, op=op: V.tensor_tensor(
                    vb[:, :, half, :], va[:, :, 0, :], va[:, :, 1, :], op)))
            a, b = b, a
        chain_stage(core, steps)
        transpose_stage(core, a, hT, HEADS)
        with core.stage() as block:

            @block.tensor
            def _(pe):
                for g in range(4):
                    nc.tensor.matmul(ps[g], core.table["hadamard"], hT[:, 4 * g:4 * g + 4, :].rearrange(
                        "p h t -> p (h t)"), start=True, stop=True).then_inc(c.sem("transform_ready"), 1)

            @block.scalar
            def _(act):
                for g in range(4):
                    act.wait_ge(c.sem("transform_ready"), g + 1)
                    nc.scalar.activation(outT[:, 4 * g:4 * g + 4, :].rearrange("p h t -> p (h t)"), ps[g],
                                         ACT.Copy, scale=F ** -0.5)

        down_stage(core, outT, ring.take("L2_ffn_W2"), add_to_x(core))


NARROW = 32
W16 = D // NARROW


def narrow_stage(core, own_qT, wkeys, wvalues):
    nc, c, ps = core.nc, core, core.psum
    chunks = KV // P
    with core.scratch(ctx0=[P, DC, P], ctx1=[P, DC, P], parts0=[P, 2, DC, P], parts1=[P, 2, DC, P],
                      keysT0=[P, HEADS, P], keysT1=[P, HEADS, P], values0=[P, NARROW, 32], values1=[P, NARROW, 32],
                      probs0=[P, 4, D], probs1=[P, 4, D], keys=[P, D], key_parts=[P, HEADS, 2, 32], square=[P, D],
                      sumsq=[P, NARROW], rnorm=[P, NARROW], w=[P, 2, 2, DC, D]) as (
        ctx0, ctx1, parts0, parts1, keysT0, keysT1, values0, values1, probs0, probs1, keys, key_parts, square,
        sumsq, rnorm, w,
    ), core.stage() as block:
        ctxT, parts, keysT, values = [ctx0, ctx1], [parts0, parts1], [keysT0, keysT1], [values0, values1]
        probs, turned = [probs0, probs1], [ps[0], ps[7]]
        units = (wkeys, wvalues)

        def pairs_from(b, bank, odd, to):
            return (short(keysT[b][64 * to:64 * to + 64, bank * 8:bank * 8 + 8, :].rearrange(
                "p (c two) t -> p c two t", two=2)[:, :, odd, :]),
                turned[bank][64 * odd:64 * odd + 64, :].rearrange("p (c t) -> p c t", c=DC))

        def there_is(chunk):
            return not isinstance(chunk, int) or chunk < chunks

        @block.sync
        def _(sp):
            chunk_of = core.dram["ctxT_chunks"]
            for b in range(2):
                sp.dma_start(ctxT[b][:, :, :], chunk_of[b]).then_inc(c.sem(f"ctxT_landed_{b}"), 16)
            for u in units:
                u.refill(sp)
            with sp.Fori(0, chunks // 2 - 1) as i:
                for b in range(2):
                    sp.wait_ge(c.sem("ctx_lo_ready"), i * 2 + (b + 1))
                    sp.dma_start(ctxT[b][:, :, :], chunk_of[bass.ds(i * 2 + (2 + b), 1)].rearrange(
                        "a p c n -> (a p) c n")).then_inc(c.sem(f"ctxT_landed_{b}"), 16)

        @block.tensor
        def _(pe):
            def project(b, n, which, bank, signal):
                for i in range(DC):
                    last = matmul_parts(nc, ps[bank], [parts[b][:, s, i, :] for s in range(2)],
                                        [w[:, which, s, i, :] for s in range(2)], i == 0, i == DC - 1)
                last.then_inc(c.sem(signal), 1)

            def project_keys(b, m):
                pe.wait_ge(c.sem("ctx_lo_ready"), m + 1)
                wait_count(pe, c.sem("keys_copied"), m)
                project(b, m, 0, 6, "keys_product")

            def project_values(b, n):
                wait_count(pe, c.sem("even_pairs_stored"), n * 2)
                wait_count(pe, c.sem("odd_pairs_stored"), n * 2)
                project(b, n, 1, 7, "values_product")

            def transpose_keys(n):
                pe.wait_ge(c.sem("key_lo_ready"), n + 1)
                pe.wait_ge(c.sem("probs_ready"), n * 2 + 1)
                pe.wait_ge(c.sem("values_stored"), n + 1)
                flat = key_parts[:, :, :, :].rearrange("p g s f -> p (g s f)")
                for i in range(8):
                    last = nc.tensor.transpose(turned[i // DC][:, (i % DC) * P:(i % DC + 1) * P],
                                               flat[:, i * P:(i + 1) * P], core.ident)
                last.then_inc(c.sem("keysT_product"), 1)

            def score(b, g, t):
                pe.wait_ge(c.sem("probs_ready"), g * 2 + (t + 1))
                for half in range(2):
                    for r in range(4):
                        pair = 4 * (2 * t + half) + r
                        last = nc.tensor.matmul(ps[r][:, half * 2 * P:(half + 1) * 2 * P],
                                                short(keysT[b][:, pair, :]),
                                                short(own_qT[:, pair, :, :].rearrange("p e t -> p (e t)")),
                                                start=True, stop=True)
                last.then_inc(c.sem("scores_ready"), 1)

            def weigh(b, g, t):
                pe.wait_ge(c.sem("probs_ready"), g * 2 + (t + 2))
                for n in range(4 * t, 4 * t + 4):
                    half, e = n // 2 % 2, n % 2
                    for j in range(4):
                        last = nc.tensor.matmul(ps[4 + t][32 * j:32 * j + 32, (n % 4) * P:(n % 4 + 1) * P],
                                                values[b][:, 4 * n - 3 * e + 2 * j, :],
                                                probs[t][:, j, (2 * half + e) * P:(2 * half + e + 1) * P],
                                                start=False, stop=False, skip_group_check=True)
                last.then_inc(c.sem("round_done"), 1)

            def chunk(b, g, attend, prepare):
                if attend:
                    pe.wait_ge(c.sem("even_pairs_stored"), g * 2 + 1)
                    pe.wait_ge(c.sem("odd_pairs_stored"), g * 2 + 1)
                    score(b, g, 0)
                if prepare:
                    project_values(1 - b, g + 1)
                if attend:
                    pe.wait_ge(c.sem("even_pairs_stored"), g * 2 + 2)
                    pe.wait_ge(c.sem("odd_pairs_stored"), g * 2 + 2)
                    score(b, g, 1)
                if there_is(g + 2):
                    project_keys(b, g + 2)
                if prepare:
                    transpose_keys(g + 1)
                if attend:
                    weigh(b, g, 0)
                    weigh(b, g, 1)

            for bank in (4, 5):
                nc.tensor.matmul(ps[bank], core.zeros[:, 0:P], core.zeros[:, :], start=True, stop=False,
                                 skip_group_check=True)
            for k, u in enumerate(units):
                pe.wait_ge(c.sem("weight_lo_ready"), k + 1)
                u.done(nc.tensor.matmul(ps[0][:, 0:P], core.zeros[:, 0:P], core.zeros[:, 0:P], start=True,
                                        stop=True))
                if k == 0:
                    project_keys(0, 0)
            over_groups(pe, chunk, chunks, 4)

        @block.vector
        def _(dve):
            def ctx_lo(b, m):
                dve.wait_ge(c.sem("ctx_hi_ready"), m + 1)
                nc.vector.tensor_tensor(short(parts[b][:, 1, :, :]), ctxT[b][:, :, :], parts[b][:, 0, :, :],
                                        ALU.subtract).then_inc(c.sem("ctx_lo_ready"), 1)

            def spread_of_keys(n):
                dve.wait_ge(c.sem("keys_squared"), n + 1)
                nc.vector.tensor_reduce(sumsq[:, :], square[:, :].rearrange("p (h d) -> p h d", h=NARROW), X,
                                        ALU.add).then_inc(c.sem("sumsq_ready"), 1)
                dve.wait_ge(c.sem("sumsq_ready"), n + 1)
                nc.vector.tensor_scalar(sumsq[:, :], sumsq[:, :], 1.0 / W16, 1e-6, ALU.mult, ALU.add).then_inc(
                    c.sem("spread_ready"), 1)

            def chunk(b, g, attend, prepare):
                if not prepare:
                    return
                n = g + 1
                dve.wait_ge(c.sem("values_product"), n + 1)
                nc.vector.tensor_copy(values[1 - b][:, :, 0:W16], ps[7].rearrange(
                    "p (h d) -> p h d", h=NARROW)).then_inc(c.sem("values_stored"), 1)
                if there_is(g + 3):
                    ctx_lo(1 - b, g + 3)
                dve.wait_ge(c.sem("rnorm_ready"), n + 1)
                dve.wait_ge(c.sem("keys_copied"), n + 1)
                nc.vector.tensor_tensor(keys[:, :].rearrange("p (h d) -> p h d", h=NARROW),
                                        keys[:, :].rearrange("p (h d) -> p h d", h=NARROW),
                                        rnorm[:, :].unsqueeze(2).to_broadcast([P, NARROW, W16]),
                                        ALU.mult).then_inc(c.sem("keys_normed"), 1)
                dve.wait_ge(c.sem("keys_normed"), n + 1)
                nc.vector.tensor_copy(short(key_parts[:, :, 0, :]), keys[:, :].rearrange(
                    "p (g f) -> p g f", f=32)).then_inc(c.sem("key_hi_ready"), 1)
                dve.wait_ge(c.sem("key_hi_ready"), n + 1)
                nc.vector.tensor_tensor(short(key_parts[:, :, 1, :]), keys[:, :].rearrange("p (g f) -> p g f", f=32),
                                        key_parts[:, :, 0, :], ALU.subtract).then_inc(c.sem("key_lo_ready"), 1)
                if there_is(g + 2):
                    spread_of_keys(g + 2)
                dve.wait_ge(c.sem("keysT_product"), n + 1)
                for bank in range(2):
                    for to in range(2):
                        last = nc.vector.tensor_copy(*pairs_from(1 - b, bank, 0, to))
                    last.then_inc(c.sem("even_pairs_stored"), 1)

            for m in range(2):
                ctx_lo(m, m)
            for k, u in enumerate(units):
                dve.wait_ge(c.sem("weight_hi_ready"), k + 1)
                nc.vector.tensor_tensor(short(w[:, k, 1, :, :]), u.data, w[:, k, 0, :, :], ALU.subtract).then_inc(
                    c.sem("weight_lo_ready"), 1)
            for b in range(2):
                nc.vector.memset(values[b][:, :, :].rearrange("p h d -> p (h d)"), 0.0).then_inc(c.sem("cleared"), 1)
            dve.wait_ge(c.sem("cleared"), 2)
            for b in range(2):
                nc.vector.memset(values[b][:, :, W16:W16 + 1], 1.0).then_inc(c.sem("cleared"), 1)
            dve.wait_ge(c.sem("cleared"), 4)
            spread_of_keys(0)
            over_groups(dve, chunk, chunks, 4)

        @block.gpsimd
        def _(pool):
            with pool.Fori(0, chunks) as n:
                pool.wait_ge(c.sem("spread_ready"), n + 1)
                nc.gpsimd.tensor_tensor(rnorm[:, :], sumsq[:, :], core.minus_half[:, 0:NARROW], ALU.pow).then_inc(
                    c.sem("rnorm_ready"), 1)

        @block.scalar
        def _(act):
            def ctx_hi(b, m, landed):
                act.wait_ge(c.sem(f"ctxT_landed_{b}"), landed)
                wait_count(act, c.sem("values_product"), max(m - 1, 0) if isinstance(m, int) else m - 1)
                nc.scalar.copy(short(parts[b][:, 0, :, :]), ctxT[b][:, :, :]).then_inc(c.sem("ctx_hi_ready"), 1)

            def square_keys(m):
                act.wait_ge(c.sem("keys_product"), m + 1)
                wait_count(act, c.sem("sumsq_ready"), m)
                nc.scalar.activation(square[:, :], ps[6], ACT.Square).then_inc(c.sem("keys_squared"), 1)
                wait_count(act, c.sem("key_lo_ready"), m)
                nc.scalar.copy(keys[:, :], ps[6]).then_inc(c.sem("keys_copied"), 1)

            def exps(b, g, t):
                act.wait_ge(c.sem("scores_ready"), g * 2 + (t + 1))
                act.wait_ge(c.sem("round_done"), g * 2 + (t + 1))
                nc.scalar.activation(probs[t][:, :, :], core.banks[:, 0:4, :], ACT.Exp).then_inc(
                    c.sem("probs_ready"), 1)

            def chunk(b, g, attend, prepare):
                if attend:
                    exps(b, g, 0)
                if there_is(g + 3):
                    ctx_hi(1 - b, g + 3, (g + b) * 8 + 32)
                if attend:
                    exps(b, g, 1)
                if there_is(g + 2):
                    square_keys(g + 2)
                if prepare:
                    act.wait_ge(c.sem("keysT_product"), g + 2)
                    for bank in range(2):
                        for to in range(2):
                            last = nc.scalar.copy(*pairs_from(1 - b, bank, 1, to))
                        last.then_inc(c.sem("odd_pairs_stored"), 1)

            act.sem_inc(c.sem("probs_ready"), 1)
            act.sem_inc(c.sem("round_done"), 2)
            for m in range(2):
                ctx_hi(m, m, 16)
            for k, u in enumerate(units):
                u.wait_landed(act)
                nc.scalar.copy(short(w[:, k, 0, :, :]), u.data).then_inc(c.sem("weight_hi_ready"), 1)
            square_keys(0)
            over_groups(act, chunk, chunks, 4)


def l3_xattn(core):
    ring, nc, ps, c = core.ring, core.nc, core.psum, core
    V = nc.vector
    with core.scratch(own_qT=[P, HEADS, 2, P], outT=[P, 8, P], out=[P, D], inverse=[P, 8, 4]) as (
        own_qT, outT, out, inverse,
    ):
        with core.scratch(xn=[P, D], xnT=[P, DC, P], q=[P, D], square=[P, D], sums=[P, NARROW], repeated=[P, 4 * D],
                          qT=[P, HEADS, P], own=[P, HEADS, P], low=[P, HEADS, P]) as (
            xn, xnT, q, square, sums, repeated, qT, own, low,
        ):
            norm_stage(core, core.x, xn[:, :], xnT[:, :, :], 1e-5)
            rows_stage(core, xnT, ring.take("L3_xattn_Wq"), lambda j, bank, link: V.tensor_copy(q[:, :], bank))
            chain_stage(core, head_norm_steps(core, q[:, :], NARROW, W16, 1e-6, square[:, :], sums[:, :]))
            pairs = repeated[:, :].rearrange("p (g s f) -> p g s f", s=4, f=32)
            chain_stage(core, [("vector", lambda: V.tensor_copy(pairs, q[:, :].rearrange(
                "p (g f) -> p g f", f=32).unsqueeze(2).to_broadcast([P, HEADS, 4, 32])))])
            transpose_stage(core, repeated, qT, HEADS, scale=W16 ** -0.5)
            parity = core.table["head_parity"]
            steps = []
            for e in range(2):
                steps += [
                    ("vector", lambda e=e: V.tensor_scalar(own[:, :, :], qT[:, :, :], parity[:, e:e + 1], None,
                                                           ALU.mult)),
                    ("vector", lambda e=e: V.tensor_copy(short(own_qT[:, :, e, :]), own[:, :, :])),
                    ("vector", lambda e=e: V.tensor_tensor(short(low[:, :, :]), own[:, :, :], own_qT[:, :, e, :],
                                                           ALU.subtract)),
                    ("vector", lambda e=e: V.tensor_copy(short(own_qT[64:P, :, e, :]), low[64:P, :, :])),
                ]
            chain_stage(core, steps)
        (wkeys,), (wvalues,) = ring.take("L3_xattn_Wkeys"), ring.take("L3_xattn_Wvalues")
        narrow_stage(core, own_qT, wkeys, wvalues)

        with core.stage() as block:

            @block.scalar
            def _(act):
                for i in range(2):
                    nc.scalar.copy(outT[:, 4 * i:4 * i + 4, :].rearrange("p n t -> p (n t)"), ps[4 + i]).then_inc(
                        c.sem("sums_copied"), 1)

            @block.tensor
            def _(pe):
                for n in range(8):
                    pe.wait_ge(c.sem("sums_copied"), n // 4 + 1)
                    nc.tensor.transpose(ps[n // 4][:, (n % 4) * P:(n % 4 + 1) * P], outT[:, n, :],
                                        core.ident).then_inc(c.sem("transposed"), 1)

            @block.vector
            def _(dve):
                link = Chain(dve, c.sem("dve_chain"))
                dve.wait_ge(c.sem("transposed"), 8)
                for t in range(4):
                    rows = ps[t // 2][:, (t % 2) * 2 * P:(t % 2 + 1) * 2 * P].rearrange(
                        "p (e j d) -> p e j d", e=2, j=4)
                    own = inverse[:, 2 * t:2 * t + 2, :]
                    link(V.reciprocal(own, rows[:, :, :, W16]))
                    link(V.tensor_tensor(
                        out[:, t * P:(t + 1) * P].rearrange("p (j e d) -> p e j d", j=4, e=2),
                        rows[:, :, :, 0:W16], own.unsqueeze(3).to_broadcast([P, 2, 4, W16]), ALU.mult))
                link(V.tensor_tensor(core.x, core.x, out[:, :], ALU.add))


def l3_attn(core):
    ring, nc, ps, c = core.ring, core.nc, core.psum, core
    V = nc.vector
    F = HEADS * P
    rest = core.operands[:, 0:HEADS]
    with core.scratch(xn=[P, D], xnT=[P, DC, P], qT=[P, HEADS, P], kT=[P, HEADS, P], v=[P, F],
                      oT=[P, HEADS, P]) as (xn, xnT, qT, kT, v, oT):
        norm_stage(core, core.x, xn[:, :], xnT[:, :, :], 1e-5, loads=[(rest, core.dram["L3_attn_betas"])])
        cols_stage(core, xnT, ring.take("L3_attn_Wq"), qT)
        cols_stage(core, xnT, ring.take("L3_attn_Wk"), kT)
        rows_stage(core, xnT, ring.take("L3_attn_Wv"), lambda j, bank, link: V.tensor_copy(
            v[:, j * D:(j + 1) * D], bank))
        chain_stage(core, [
            ("scalar", lambda: nc.scalar.activation(rest, rest, ACT.Sigmoid)),
            ("vector", lambda: V.tensor_scalar(rest, rest, -1.0, 1.0, ALU.mult, ALU.add)),
        ])

        def store(g, bank):
            for j in range(4):
                h = 4 * g + j
                last = nc.scalar.activation(oT[:, :, 8 * h:8 * h + 8], bank[:, j * P:(j + 1) * P].rearrange(
                    "p (m k) -> p k m", k=HEADS), ACT.Copy, scale=rest[:, h:h + 1])
            return last

        heads_stage(core, lambda h: qT[:, h, :], lambda h: kT[:, h, :], lambda h: v[:, h * P:(h + 1) * P],
                    core.table["causal"], P ** -0.5, store)
        down_stage(core, oT, ring.take("L3_attn_Wo"), add_to_x(core))


def l3_ffn(core):
    ring, nc, ps, c = core.ring, core.nc, core.psum, core
    V = nc.vector
    F, KV_HEADS, CHOSEN = HEADS * P, 8, P // 8
    ops = core.operands
    bq, bk, bv = ops[:, 0:F], ops[:, F:F + 1024], ops[:, F + 1024:F + 2048]
    ln1, ln2, router = (ops[:, F + 2048 + i * D:F + 2048 + (i + 1) * D] for i in range(3))
    cos, sin = core.table["cos3"], core.table["sin3"]
    with core.scratch(xn=[P, D], xnT=[P, DC, P], score=[P, 1], score_all=[P, P], row=[P, P], left=[P, P], top8=[P, 8],
                      chosen=[P, 1], gate=[P, 1], mask=[P, P], x1=[P, D], h2=[P, D], h2T=[P, DC, P]) as (
        xn, xnT, score, score_all, row, left, top8, chosen, gate, mask, x1, h2, h2T,
    ):
        norm_stage(core, core.x, xn[:, :], xnT[:, :, :], 1e-5,
                   loads=[(ops, core.dram["L3_ffn_rows"].partition_broadcast(P))])
        chain_stage(core, [
            ("vector", lambda: V.tensor_tensor(x1[:, :], xn[:, :], router, ALU.mult)),
            ("vector", lambda: V.tensor_reduce(score[:, :], x1[:, :], X, ALU.add)),
            ("scalar", lambda: nc.scalar.activation(gate[:, :], score[:, :], ACT.Sigmoid)),
            ("vector", lambda: V.tensor_copy(score_all[:, :], score[:, 0:1].to_broadcast([P, P]))),
        ])
        with core.stage() as block:

            @block.tensor
            def _(pe):
                nc.tensor.transpose(ps[0][:, 0:P], score_all[:, :], core.ident).then_inc(c.sem("row_ready"), 1)

            @block.vector
            def _(dve):
                link = Chain(dve, c.sem("dve_chain"))
                dve.wait_ge(c.sem("row_ready"), 1)
                link(V.tensor_copy(left[:, :], ps[0][:, 0:P]))
                for _ in range(CHOSEN // 8):
                    link(V.max(top8[:, :], left[:, :]))
                    link(V.match_replace(left[:, :], top8[:, :], left[:, :], TAKEN))
                link(V.tensor_scalar(row[:, :], left[:, :], TAKEN / 2, None, ALU.is_le))
                link(V.tensor_scalar(mask[:, :], row[:, :], 1.0, -NEG, ALU.subtract, ALU.mult))
                link(V.tensor_tensor(mask[:, :], mask[:, :], core.table["causal"], ALU.min))
                link(V.tensor_tensor(row[:, :], row[:, :], core.ident, ALU.mult))
                link(V.tensor_reduce(chosen[:, :], row[:, :], X, ALU.add))
                link(V.tensor_tensor(gate[:, :], gate[:, :], chosen[:, :], ALU.mult))

        with core.scratch(h=[P, D], hT=[P, DC, P], q=[P, F], k=[P, KV_HEADS * P], v=[P, KV_HEADS * P],
                          qT=[P, HEADS, P], kT=[P, KV_HEADS, P], turn=[P, 2 * F], oT=[P, HEADS, P]) as (
            h, hT, q, k, v, qT, kT, turn, oT,
        ):
            norm_stage(core, xn[:, :], h[:, :], hT[:, :, :], 1e-6, rms=True, gain=ln1)
            to = [t[:, i * D:(i + 1) * D] for t, n in ((q, 4), (k, 2), (v, 2)) for i in range(n)]
            bias = [t[:, i * D:(i + 1) * D] for t, n in ((bq, 4), (bk, 2), (bv, 2)) for i in range(n)]
            rows_stage(core, hT, ring.take("L3_ffn_wq") + ring.take("L3_ffn_wk") + ring.take("L3_ffn_wv"),
                       lambda j, bank, link: V.tensor_tensor(to[j], bank, bias[j], ALU.add))
            steps = []
            for rows, heads in ((q, HEADS), (k, KV_HEADS)):
                half = rows[:, :].rearrange("p (h two i) -> p h two i", h=heads, two=2)
                n = heads * P // 2
                t = [turn[:, i * n:(i + 1) * n].rearrange("p (h i) -> p h i", h=heads) for i in range(4)]
                wide = [a.unsqueeze(1).to_broadcast([P, heads, P // 2]) for a in (cos, sin)]
                steps += rotation_steps(core, half[:, :, 0, :], half[:, :, 1, :], *wide, t)
            chain_stage(core, steps)
            transpose_stage(core, q, qT, HEADS)
            transpose_stage(core, k, kT, KV_HEADS)
            heads_stage(core, lambda i: qT[:, i, :], lambda i: kT[:, i // 2, :],
                        lambda i: v[:, (i // 2) * P:(i // 2 + 1) * P], mask[:, :], P ** -0.5,
                        lambda g, bank: nc.scalar.copy(oT[:, 4 * g:4 * g + 4, :].rearrange("p h t -> p (h t)"), bank))
            down_stage(core, oT, ring.take("L3_ffn_wo"),
                       lambda bank, link: link(V.tensor_tensor(x1[:, :], xn[:, :], bank, ALU.add)))
        norm_stage(core, x1[:, :], h2[:, :], h2T[:, :, :], 1e-6, rms=True, gain=ln2)
        with core.scratch(up=[P, F], upT=[P, HEADS, P]) as (up, upT):
            rows_stage(core, h2T, ring.take("L3_ffn_w_gate"), lambda j, bank, link: nc.scalar.activation(
                up[:, j * D:(j + 1) * D], bank, ACT.Silu), on_scalar=True)
            rows_stage(core, h2T, ring.take("L3_ffn_w_up"), lambda j, bank, link: V.tensor_tensor(
                up[:, j * D:(j + 1) * D], up[:, j * D:(j + 1) * D], bank, ALU.mult))
            transpose_stage(core, up, upT, HEADS)

            def finish(bank, link):
                link(V.tensor_tensor(x1[:, :], x1[:, :], bank, ALU.add))
                link(V.tensor_tensor(x1[:, :], x1[:, :], xn[:, :], ALU.subtract))
                link(V.scalar_tensor_tensor(out=x1[:, :], in0=x1[:, :], scalar=gate[:, 0:1], in1=xn[:, :],
                                            op0=ALU.mult, op1=ALU.add))
                link(V.tensor_tensor(core.x, core.x, x1[:, :], ALU.add))

            down_stage(core, upT, ring.take("L3_ffn_w_down"), finish)


BLOCKS = [(l0_xattn, 16), (l0_attn, DC * 400), (l0_ffn, DC * 16 + 16), (l1_xattn, 16), (l1_attn, 6 * D),
          (l1_ffn, 960), (l2_xattn, 2 * D + 2 * P), (l2_attn, 4 * D), (l2_ffn, 16), (l3_xattn, 16), (l3_attn, HEADS),
          (l3_ffn, 4096 + 3 * D)]


def build(nc, dram):
    with ExitStack() as ctx:
        core = Core(nc, ctx, dram)
        core.banks = ctx.enter_context(nc.psum_tensor("banks", [P, 8, D], F32))
        core.psum = [core.banks[:, i, :] for i in range(8)]
        core.ring = WeightRing(core, dram["weights"])
        x = core.sbuf("x", [P, D])
        zeros = core.sbuf("zeros", [P, D])
        ones = core.sbuf("ones", [P, P])
        half = core.sbuf("minus_half", [P, 32])
        tables = core.sbuf("tables", [P, TABLES])
        core.x, core.zeros, core.ones, core.minus_half = x[:, :], zeros, ones[:, :], half
        core.table = {name: tables[:, a:b] for name, (a, b) in TABLE_AT.items()}
        core.ident = core.table["identity"]

        with core.stage() as block:

            @block.sync
            def _(sp):
                sp.dma_start(x[:, :], dram["x"]).then_inc(core.sem("x_landed"), 16)
                sp.dma_start(tables[:, :], dram["tables"]).then_inc(core.sem("x_landed"), 16)
                for n in range(RING):
                    core.ring.load(sp, n)
                sp.wait_ge(core.sem("x_landed"), 32)

            @block.vector
            def _(dve):
                nc.vector.memset(zeros[:, :], 0.0)
                nc.vector.memset(ones[:, :], 1.0)
                nc.vector.memset(half[:, :], -0.5)

        for block_of_layer, words in BLOCKS:
            with core.scratch(operands=[P, words]) as (operands,):
                core.operands = operands[:, :]
                block_of_layer(core)

        with core.stage() as block:

            @block.sync
            def _(sp):
                sp.dma_start(dram["out"], x[:, :]).then_inc(core.sem("out_stored"), 16)
                sp.wait_ge(core.sem("out_stored"), 16)




def rotation_tables(width):
    inverse = (1.0 / 10000.0 ** (np.arange(0, width, 2, dtype=np.float32) / np.float32(width))).astype(np.float32)
    angle = (np.arange(P, dtype=np.float32)[:, None] * inverse[None, :]).astype(np.float32)
    return np.cos(angle), np.sin(angle)


def constant_tables():
    hadamard = np.array([[1.0]])
    while len(hadamard) < P:
        hadamard = np.block([[hadamard, hadamard], [hadamard, -hadamard]])
    p = np.arange(P)
    cos1, sin1 = rotation_tables(256)
    cos3, sin3 = rotation_tables(P)
    return {
        "identity": np.eye(P),
        "hadamard": hadamard,
        "causal": np.where(p[:, None] >= p[None, :], 0.0, NEG),
        "head_parity": np.stack([(p // 16) % 2 == 0, (p // 16) % 2 == 1], 1),
        "cos1": cos1, "sin1": sin1, "cos3": cos3, "sin3": sin3,
    }


TABLE_AT, TABLES = {}, 0
for _name, _t in constant_tables().items():
    TABLE_AT[_name] = (TABLES, TABLES + _t.shape[1])
    TABLES += _t.shape[1]


def unit_rows(w):
    n = w.shape[1] // D
    return w.reshape(DC, P, n, D).transpose(2, 1, 0, 3).reshape(n, P, DC * D)


def unit_down(w):
    n = w.shape[0] // D
    return w.reshape(n, DC, P, D).transpose(0, 2, 1, 3).reshape(n, P, DC * D)


def small_columns(*ws):
    w = np.concatenate(ws, 1)
    return w.reshape(DC, P, -1).transpose(1, 0, 2).reshape(P, -1)


def small_operands(a):
    return {
        "L0_attn_small": small_columns(a["L0_attn_wk_idx"], a["L0_attn_wk"], a["L0_attn_wv"], a["L0_attn_w_iw"]),
        "L0_ffn_small": small_columns(a["L0_ffn_Wr"].T),
        "L0_ffn_rows": a["L0_ffn_br"],
        "L1_attn_rows": np.concatenate([a["L1_attn_" + n] for n in ("b_in", "b_out", "gamma", "beta")]),
        "L1_ffn_small": small_columns(a["L1_ffn_router_W"].T, a["L1_ffn_A"].T),
        "L2_xattn_rows": np.concatenate([a["L2_xattn_" + n] for n in ("bk", "bv", "qn_w", "kn_w", "bq")]),
        "L2_attn_rows": np.concatenate([a["L2_attn_" + n] for n in ("bq", "bk", "bv", "bo")]),
        "L3_attn_betas": np.ascontiguousarray(a["L3_attn_betas"].reshape(HEADS, P).T),
        "L3_ffn_rows": np.concatenate([a["L3_ffn_" + n] for n in ("bq", "bk", "bv", "ln1_w", "ln2_w", "w_router")]),
        "L1_ffn_BT": np.ascontiguousarray(a["L1_ffn_B"].T),
        "L1_ffn_rows": a["L1_ffn_biases"],
    }


def layout(a):
    kv = np.concatenate([a["L3_xattn_Wk"], a["L3_xattn_Wv"]], 0)
    w = {n: a[n].T for n in ("L0_xattn_wq", "L0_xattn_wk", "L0_xattn_wv", "L0_xattn_wo", "L0_ffn_W1", "L0_ffn_W2",
                             "L1_ffn_base_W", "L2_attn_wq", "L2_attn_wk", "L2_attn_wv", "L2_attn_wo", "L2_ffn_W1",
                             "L2_ffn_W3", "L2_ffn_W2", "L3_xattn_Wq")}
    w["L3_xattn_Wkeys"], w["L3_xattn_Wvalues"] = kv[0::2].T, kv[1::2].T
    parts = []
    for name, n in UNITS:
        m = w[name] if name in w else a[name]
        parts.append(unit_rows(m) if m.shape[0] == D else unit_down(m))
        assert len(parts[-1]) == n
    ctx = a["ctx_2048"][0]
    return {
        "weights": np.ascontiguousarray(np.concatenate(parts, 0)),
        "x": a["x"][0],
        "ctxT_chunks": np.ascontiguousarray(ctx.reshape(KV // P, P, DC, P).transpose(0, 3, 2, 1)),
        "ctx_rows": np.ascontiguousarray(ctx.reshape(GROUPS, PER, P, D).transpose(0, 2, 1, 3)),
        "tables": np.concatenate(list(constant_tables().values()), 1).astype(np.float32),
        **small_operands(a),
        "score_mask": np.ascontiguousarray(a["mask_1xSxS2_ff0"][0].reshape(P, GROUPS, GROUP).transpose(1, 0, 2)),
        "memory_mask": a["mask_BxS2_bk0"].reshape(KV),
    }


def kernel(**inputs):
    import concourse.bacc as bacc
    from concourse.bass_utils import run_bass_kernel_spmd

    a = {k: np.ascontiguousarray(v) for k, v in inputs.items()}
    arrays = layout(a)
    nc = bacc.Bacc("TRN2", target_bir_lowering=False, num_devices=1)
    dram = {n: nc.dram_tensor(f"in_{n}", v.shape, mybir.dt.from_np(v.dtype), kind="ExternalInput").ap()
            for n, v in arrays.items()}
    dram["out"] = nc.dram_tensor("out_x", (P, D), F32, kind="ExternalOutput").ap()
    build(nc, dram)
    got = run_bass_kernel_spmd(nc, [{f"in_{n}": v for n, v in arrays.items()}], core_ids=[0])
    return np.asarray(got.results[0]["out_x"]).reshape(1, P, D)
```
